# Optimizing a Trainium2 kernel written in Bass

```python
import numpy as np
import jax
import jax.numpy as jnp

def _softmax(x, axis=-1):
    return jax.nn.softmax(x, axis=axis)

def _gelu(x):
    return jax.nn.gelu(x, approximate=True)

def _silu(x):
    return jax.nn.silu(x)

def _sigmoid(x):
    return jax.nn.sigmoid(x)

def _layernorm(x, axis=-1, eps=1e-05):
    m = jnp.mean(x, axis=axis, keepdims=True)
    v = jnp.var(x, axis=axis, keepdims=True)
    return (x - m) / jnp.sqrt(v + eps)

def _scatter_add(tgt, idx, src, axis=0):
    return tgt.at[idx].add(src)

def _segment_sum(src, seg, n):
    return jax.ops.segment_sum(src, seg, n)
kernel_name = 'mk_decoder_preln_d1_seqx_r4_af5c03'

def setup_inputs(seed: int=0):
    np.random.seed(seed)
    _w = jnp.asarray

    def _rec_inputs():
        import jax
        import jax.numpy as jnp
        _rk = jax.random.key(seed)
        x = 0.0003765 + 1 * jax.random.normal(jax.random.fold_in(_rk, 1), (8, 256, 512), jnp.float32)
        _lenS = 256 - jax.random.randint(jax.random.fold_in(_rk, 7), (8,), 0, max(1, 256 // 4) + 1, jnp.int32)
        _lenS2 = 256 - jax.random.randint(jax.random.fold_in(_rk, 8), (8,), 0, max(1, 256 // 4) + 1, jnp.int32)
        _ctx_2048P = jax.random.normal(jax.random.fold_in(_rk, 11), (8, 16, 512), jnp.float32)
        _ctx_2048c = jax.random.dirichlet(jax.random.fold_in(_rk, 511), 0.3 * jnp.ones((16,), jnp.float32), (8, 256))
        _ctx_2048t = jnp.einsum('bsk,bkd->bsd', _ctx_2048c, _ctx_2048P)
        _ctx_2048t = _ctx_2048t * jax.lax.rsqrt(jnp.mean(jnp.square(_ctx_2048t)) + 1e-12) * 0.953939
        ctx_2048 = -0.000292821 + 1.00034 * (_ctx_2048t + 0.3 * jax.random.normal(jax.random.fold_in(_rk, 611), (8, 256, 512), jnp.float32))
        return (x, ctx_2048)
    x, ctx_2048 = _rec_inputs()

    def _L0_attn_setup():
        import jax, jax.numpy as jnp
        import numpy as np
        B, S, DIM = (2, 512, 512)
        H, KVH = (16, 8)
        HD = DIM // H
        WIN = 128
        GLOB = 64
        NEG = -1000000000.0

        def _alibi_slopes(n):
            cp2 = 2.0 ** jnp.floor(jnp.log2(jnp.float32(n)))
            base = 2.0 ** (-2.0 ** (-(jnp.log2(cp2) - 3.0)))
            powers = jnp.arange(1, 1 + n, dtype=jnp.float32)
            return jnp.power(base, powers)

        def _rope_tables(head_dim, seq_len, dtype=jnp.float32, base=10000.0):
            half = head_dim // 2
            freqs = 1.0 / base ** (jnp.arange(0, half, dtype=dtype) / half)
            t = jnp.arange(seq_len, dtype=dtype)
            f = jnp.outer(t, freqs)
            return (jnp.sin(f)[None, None], jnp.cos(f)[None, None])

        def _rotary(x, sin, cos):
            x1, x2 = jnp.split(x, 2, axis=-1)
            return jnp.concatenate([x1 * cos - x2 * sin, x1 * sin + x2 * cos], axis=-1)

        def _window_mask(seq_len):
            i = jnp.arange(seq_len)[:, None]
            j = jnp.arange(seq_len)[None, :]
            m = jnp.where(jnp.abs(i - j) <= WIN // 2, 0.0, NEG)
            m = jnp.where((i < GLOB) | (j < GLOB), 0.0, m)
            return m
        key = jax.random.key(seed)
        k1, k2, k3, k4 = jax.random.split(key, 4)
        x = jax.random.normal(k1, (B, S, DIM), dtype=jnp.float32)
        Wq = jax.random.normal(k2, (DIM, DIM), dtype=jnp.float32) * 0.02
        Wkv = jax.random.normal(k3, (DIM, 2 * KVH * HD), dtype=jnp.float32) * 0.02
        Wo = jax.random.normal(k4, (DIM, DIM), dtype=jnp.float32) * 0.02
        bo = jnp.zeros((DIM,), dtype=jnp.float32)
        return {'x': x, 'Wq': Wq, 'Wkv': Wkv, 'Wo': Wo, 'bo': bo}
    _L0_attn_all = _L0_attn_setup()
    _L0_attn_in = {k: v for k, v in _L0_attn_all.items() if k in ('Wq', 'Wkv', 'Wo', 'bo')}
    del _L0_attn_all

    def _L0_xattn_setup():
        import jax, jax.numpy as jnp
        import numpy as np
        key = jax.random.key(seed)
        k1, k2, k3, k4, k5 = jax.random.split(key, 5)
        B, D_MODEL, L = (2, 256, 512)
        HEAD_DIM = 8
        H = D_MODEL // HEAD_DIM
        return {'k': jax.random.normal(k1, (B, D_MODEL, L), dtype=jnp.float32), 'v': jax.random.normal(k2, (B, D_MODEL, L), dtype=jnp.float32), 'q': jax.random.normal(k3, (B, D_MODEL, L), dtype=jnp.float32), 'ssm_kernel': jax.random.normal(k4, (H, L), dtype=jnp.float32), 'D': jax.random.normal(k5, (H,), dtype=jnp.float32), 'head_dim': HEAD_DIM}
    _L0_xattn_all = _L0_xattn_setup()
    _L0_xattn_in = {k: v for k, v in _L0_xattn_all.items() if k in ('ssm_kernel', 'D')}
    del _L0_xattn_all

    def _L0_ffn_setup():
        import jax, jax.numpy as jnp
        import numpy as np
        E = 64
        K = 6
        NG = 8
        TKG = 4
        SCALE = 2.5
        CAP = 128

        def _router(x, gate_w, e_bias):
            logits = x.astype(jnp.float32) @ gate_w.T
            scores = jax.nn.sigmoid(logits)
            sc = scores + e_bias[None, :]
            T = x.shape[0]
            gs = sc.reshape(T, NG, E // NG)
            grp_score = jax.lax.top_k(gs, 2)[0].sum(-1)
            _, gidx = jax.lax.top_k(grp_score, TKG)
            gmask = jax.nn.one_hot(gidx, NG, dtype=sc.dtype).sum(1)
            emask = jnp.repeat(gmask, E // NG, axis=1)
            masked = jnp.where(emask > 0, sc, -jnp.inf)
            _, idx = jax.lax.top_k(masked, K)
            w = jnp.take_along_axis(scores, idx, axis=1)
            w = w / (w.sum(-1, keepdims=True) + 1e-20) * SCALE
            return (idx, w)

        def _relu2(h):
            return jnp.square(jax.nn.relu(h))

        def _moe(x, idx, w, w1, w2):
            T, D = x.shape
            e_flat = idx.reshape(-1)
            tok = jnp.repeat(jnp.arange(T), K)
            oh = jax.nn.one_hot(e_flat, E, dtype=jnp.float32)
            pos = jnp.cumsum(oh, axis=0) - oh
            pos = (pos * oh).sum(-1).astype(jnp.int32)
            keep = pos < CAP
            slot = jnp.where(keep, pos, CAP)
            xd = jnp.zeros((E, CAP + 1, D), x.dtype).at[e_flat, slot].set(x[tok])
            h = _relu2(jnp.einsum('ecd,eid->eci', xd, w1))
            yd = jnp.einsum('eci,edi->ecd', h, w2)
            gate = w.reshape(-1)[:, None] * keep[:, None].astype(x.dtype)
            y_assign = yd[e_flat, slot] * gate
            return jnp.zeros((T, D), x.dtype).at[tok].add(y_assign)
        key = jax.random.key(seed)
        ks = jax.random.split(key, 6)
        D, I, SH, T = (512, 256, 1024, 512)
        x = jax.random.normal(ks[0], (1, T, D), jnp.float32)
        gate_w = jax.random.normal(ks[1], (E, D), jnp.float32) * D ** (-0.5)
        e_bias = jnp.zeros((E,), jnp.float32)
        w1 = jax.random.normal(ks[2], (E, I, D), jnp.float32) * D ** (-0.5)
        w2 = jax.random.normal(ks[3], (E, D, I), jnp.float32) * I ** (-0.5)
        su = jax.random.normal(ks[4], (SH, D), jnp.float32) * D ** (-0.5)
        sd = jax.random.normal(ks[5], (D, SH), jnp.float32) * SH ** (-0.5)
        return {'hidden_states': x, 'gate_w': gate_w, 'e_bias': e_bias, 'w1': w1, 'w2': w2, 'shared_up_w': su, 'shared_down_w': sd}
    _L0_ffn_all = _L0_ffn_setup()
    _L0_ffn_in = {k: v for k, v in _L0_ffn_all.items() if k in ('gate_w', 'e_bias', 'w1', 'w2', 'shared_up_w', 'shared_down_w')}
    del _L0_ffn_all
    return {'x': x, 'ctx_2048': ctx_2048, 'L0_attn_Wq': _L0_attn_in['Wq'], 'L0_attn_Wkv': _L0_attn_in['Wkv'], 'L0_attn_Wo': _L0_attn_in['Wo'], 'L0_attn_bo': _L0_attn_in['bo'], 'L0_xattn_ssm_kernel': _L0_xattn_in['ssm_kernel'], 'L0_xattn_D': _L0_xattn_in['D'], 'L0_ffn_gate_w': _L0_ffn_in['gate_w'], 'L0_ffn_e_bias': _L0_ffn_in['e_bias'], 'L0_ffn_w1': _L0_ffn_in['w1'], 'L0_ffn_w2': _L0_ffn_in['w2'], 'L0_ffn_shared_up_w': _L0_ffn_in['shared_up_w'], 'L0_ffn_shared_down_w': _L0_ffn_in['shared_down_w']}

def reference(x, ctx_2048, L0_attn_Wq, L0_attn_Wkv, L0_attn_Wo, L0_attn_bo, L0_xattn_ssm_kernel, L0_xattn_D, L0_ffn_gate_w, L0_ffn_e_bias, L0_ffn_w1, L0_ffn_w2, L0_ffn_shared_up_w, L0_ffn_shared_down_w):
    import jax
    import jax.numpy as jnp

    def _L0_attn_ref(x, Wq, Wkv, Wo, bo):
        import jax, jax.numpy as jnp
        import numpy as np
        B, S, DIM = (2, 512, 512)
        H, KVH = (16, 8)
        HD = DIM // H
        WIN = 128
        GLOB = 64
        NEG = -1000000000.0

        def _alibi_slopes(n):
            cp2 = 2.0 ** jnp.floor(jnp.log2(jnp.float32(n)))
            base = 2.0 ** (-2.0 ** (-(jnp.log2(cp2) - 3.0)))
            powers = jnp.arange(1, 1 + n, dtype=jnp.float32)
            return jnp.power(base, powers)

        def _rope_tables(head_dim, seq_len, dtype=jnp.float32, base=10000.0):
            half = head_dim // 2
            freqs = 1.0 / base ** (jnp.arange(0, half, dtype=dtype) / half)
            t = jnp.arange(seq_len, dtype=dtype)
            f = jnp.outer(t, freqs)
            return (jnp.sin(f)[None, None], jnp.cos(f)[None, None])

        def _rotary(x, sin, cos):
            x1, x2 = jnp.split(x, 2, axis=-1)
            return jnp.concatenate([x1 * cos - x2 * sin, x1 * sin + x2 * cos], axis=-1)

        def _window_mask(seq_len):
            i = jnp.arange(seq_len)[:, None]
            j = jnp.arange(seq_len)[None, :]
            m = jnp.where(jnp.abs(i - j) <= WIN // 2, 0.0, NEG)
            m = jnp.where((i < GLOB) | (j < GLOB), 0.0, m)
            return m
        b, s, dim = x.shape
        complexity = jax.nn.sigmoid(jnp.sum(jnp.abs(x), axis=-1, keepdims=True))
        q = jnp.dot(x * complexity, Wq)
        kv = jnp.dot(x, Wkv)
        k, v = jnp.split(kv, 2, axis=-1)
        q = q.reshape(b, s, H, HD).transpose(0, 2, 1, 3)
        k = k.reshape(b, s, KVH, HD).transpose(0, 2, 1, 3)
        v = v.reshape(b, s, KVH, HD).transpose(0, 2, 1, 3)
        sin, cos = _rope_tables(HD, s, dtype=x.dtype)
        q = _rotary(q, sin, cos)
        k = _rotary(k, sin, cos)
        r = H // KVH
        k = jnp.repeat(k, r, axis=1)
        v = jnp.repeat(v, r, axis=1)
        scale = 1.0 / jnp.sqrt(jnp.float32(HD)).astype(x.dtype)
        qk = jnp.einsum('bhid,bhjd->bhij', q, k) * scale
        slopes = _alibi_slopes(H)
        pos = jnp.arange(s)
        dist = -jnp.abs(pos[:, None] - pos[None, :]).astype(jnp.float32)
        qk = qk + slopes[:, None, None] * dist
        m = _window_mask(s)
        qk = jnp.where(m != 0.0, qk, NEG)
        attn = jax.nn.softmax(qk, axis=-1)
        out = jnp.einsum('bhij,bhjd->bhid', attn, v)
        out = out.transpose(0, 2, 1, 3).reshape(b, s, dim)
        out = jnp.dot(out, Wo) + bo
        return out

    def _L0_xattn_ref(k, v, q, ssm_kernel, D, head_dim):
        import jax, jax.numpy as jnp
        import numpy as np
        B, HD, L = k.shape
        H = HD // head_dim
        fft_size = 2 * L
        k_ = k.reshape(B, H, head_dim, L)
        v_ = v.reshape(B, H, head_dim, L)
        q_ = q.reshape(B, H, head_dim, L)
        kv = jnp.einsum('bhil,bhjl->bijhl', k_, v_)
        kv_f = jnp.fft.rfft(kv, n=fft_size)
        kernel_f = jnp.fft.rfft(ssm_kernel, n=fft_size)
        y = jnp.fft.irfft(kv_f * kernel_f, n=fft_size)[..., :L]
        out = y + kv * D[None, None, None, :, None]
        out = jnp.einsum('bijhl,bhil->bjhl', out, q_)
        out = jnp.transpose(out, (0, 2, 1, 3)).reshape(B, H * head_dim, L)
        return out.astype(k.dtype)

    def _L0_ffn_ref(hidden_states, gate_w, e_bias, w1, w2, shared_up_w, shared_down_w):
        import jax, jax.numpy as jnp
        import numpy as np
        E = 64
        K = 6
        NG = 8
        TKG = 4
        SCALE = 2.5
        CAP = 128

        def _router(x, gate_w, e_bias):
            logits = x.astype(jnp.float32) @ gate_w.T
            scores = jax.nn.sigmoid(logits)
            sc = scores + e_bias[None, :]
            T = x.shape[0]
            gs = sc.reshape(T, NG, E // NG)
            grp_score = jax.lax.top_k(gs, 2)[0].sum(-1)
            _, gidx = jax.lax.top_k(grp_score, TKG)
            gmask = jax.nn.one_hot(gidx, NG, dtype=sc.dtype).sum(1)
            emask = jnp.repeat(gmask, E // NG, axis=1)
            masked = jnp.where(emask > 0, sc, -jnp.inf)
            _, idx = jax.lax.top_k(masked, K)
            w = jnp.take_along_axis(scores, idx, axis=1)
            w = w / (w.sum(-1, keepdims=True) + 1e-20) * SCALE
            return (idx, w)

        def _relu2(h):
            return jnp.square(jax.nn.relu(h))

        def _moe(x, idx, w, w1, w2):
            T, D = x.shape
            e_flat = idx.reshape(-1)
            tok = jnp.repeat(jnp.arange(T), K)
            oh = jax.nn.one_hot(e_flat, E, dtype=jnp.float32)
            pos = jnp.cumsum(oh, axis=0) - oh
            pos = (pos * oh).sum(-1).astype(jnp.int32)
            keep = pos < CAP
            slot = jnp.where(keep, pos, CAP)
            xd = jnp.zeros((E, CAP + 1, D), x.dtype).at[e_flat, slot].set(x[tok])
            h = _relu2(jnp.einsum('ecd,eid->eci', xd, w1))
            yd = jnp.einsum('eci,edi->ecd', h, w2)
            gate = w.reshape(-1)[:, None] * keep[:, None].astype(x.dtype)
            y_assign = yd[e_flat, slot] * gate
            return jnp.zeros((T, D), x.dtype).at[tok].add(y_assign)
        orig = hidden_states.shape
        x = hidden_states.reshape(-1, orig[-1])
        idx, wts = _router(x, gate_w, e_bias)
        shared = _relu2(x @ shared_up_w.T) @ shared_down_w.T
        routed = _moe(x, idx, wts.astype(x.dtype), w1, w2)
        return (shared + routed).reshape(orig)
    x = x + _L0_attn_ref(_layernorm(x, axis=-1), L0_attn_Wq, L0_attn_Wkv, L0_attn_Wo, L0_attn_bo)
    x = x + _L0_xattn_ref(ctx_2048, ctx_2048, _layernorm(x, axis=-1), L0_xattn_ssm_kernel, L0_xattn_D, 8)
    x = x + _L0_ffn_ref(_layernorm(x, axis=-1), L0_ffn_gate_w, L0_ffn_e_bias, L0_ffn_w1, L0_ffn_w2, L0_ffn_shared_up_w, L0_ffn_shared_down_w)
    return x

_drawn_inputs = setup_inputs


def setup_inputs(seed=0):
    import zlib

    import numpy as np

    out = dict(_drawn_inputs(seed))
    spreads = {'L0_attn_bo': (0.0, 0.1), 'L0_ffn_e_bias': (0.0, 0.495)}
    factors = {'L0_attn_Wq': 7.068,
     'L0_ffn_gate_w': 3.627,
     'L0_ffn_w1': 3.752,
     'L0_ffn_w2': 3.428,
     'L0_ffn_shared_up_w': 2.808}
    for name, (base, spread) in spreads.items():
        noise = np.random.default_rng([zlib.crc32(name.encode()), seed]).standard_normal(out[name].shape)
        drawn = base * np.exp(spread * noise) if base else spread * noise
        out[name] = jnp.asarray(drawn.astype(out[name].dtype))
    for name, factor in factors.items():
        out[name] = (out[name] * factor).astype(out[name].dtype)
    return out
```

```python
import numpy as np
from contextlib import ExitStack

import concourse.bass as bass
from concourse import mybir

P = 128
B, S, D = 8, 256, 512
T = B * S
NT = T // P
DC = D // P
H, KVH, HD = 16, 8, 32
NEG = -1e9
WIN, GLOB = 128, 64
QB = 3
SH, SD = 32, 8
NPAIR = 36
E, K, NG, TKG, CAP, I = 64, 6, 8, 4, 128, 256
SHD = 1024
ROWS = T + P
XW = D + E
EPS = 1e-5
NBANK = 8


class Fills:

    def __init__(self, before, names, times=1):
        self.before, self.at, per = list(before), {}, [0] * NBANK
        for name, bank in names:
            assert name not in self.at, name
            self.at[name] = (bank, per[bank])
            per[bank] += 1
        self.per = per
        self.after = [a + times * b for a, b in zip(before, per)]

    def bank(self, name):
        return self.at[name][0]

    def free(self, name, i=0):
        bank, n = self.at[name]
        return (self.before[bank] + n + 1) + i * self.per[bank]

    def drained(self, name, i=0):
        return self.free(name, i) + 1

    def all_drained(self, bank):
        return self.after[bank] + 1

    def filled(self, name, i=0):
        bank, n = self.at[name]
        return (self.before[bank] + n + 1) + i * self.per[bank]


def program(nc, a, out):
    f32, u32 = mybir.dt.float32, mybir.dt.uint32
    ALU, ACT, AX = mybir.AluOpType, mybir.ActivationFunctionType, mybir.AxisListType
    V, G, A, TE = nc.vector, nc.gpsimd, nc.scalar, nc.tensor
    ds = bass.ds

    toep = nc.dram_tensor("toeplitz_rows", (SH, P + D), f32, kind="Internal").ap()
    xrows = nc.dram_tensor("token_rows", (ROWS, XW), f32, kind="Internal").ap()
    acc = nc.dram_tensor("routed_sum", (ROWS, D), f32, kind="Internal").ap()

    ctx = ExitStack()
    with ctx:
        def sb(name, shape, dt=f32):
            return ctx.enter_context(nc.sbuf_tensor(name, shape, dt))

        def sem(name):
            return ctx.enter_context(nc.semaphore(name))

        X = sb("residual", [P, NT, D])
        QT2 = sb("features_T", [P, DC, T])
        x3T = QT2
        ident = sb("ident", [P, P])
        stats1 = sb("stats1", [P, 4, 6])
        meanvar1 = sb("meanvar1", [P, 4, 2])
        rstd1 = sb("rstd1", [P, 4])
        stats = sb("stats", [P, NT, 6])
        meanvar = sb("meanvar", [P, NT, 2])
        rstd = sb("rstd", [P, NT])
        minus_half = sb("minus_half", [P, NT])
        eps = sb("eps", [P, NT])
        zeros = sb("zeros", [P, D])
        kpad = sb("padded_kernels", [SH, P + D])
        dcol = sb("skip_gain", [SH, 1])
        idxU = sb("slot_rows_u32", [P, E], u32)
        idxg = sb("gather_rows", [P, 4], u32)
        idxs = sb("scatter_rows", [P, 2], u32)
        AREA = 34400
        arena = sb("arena", [P, AREA])
        place = [0]

        def carve(shape, at=None, rows=P):
            n = int(np.prod(shape))
            if at is not None:
                place[0] = at
            v = arena[0:rows, place[0]:place[0] + n]
            place[0] += n
            assert place[0] <= AREA, place[0]
            if len(shape) > 1:
                names = "abcde"[:len(shape)]
                v = v.rearrange(f"p ({' '.join(names)}) -> p {' '.join(names)}",
                                **{c: s for c, s in zip(names, shape)})
            return v

        wq = carve([DC, D], at=0)
        wkv = carve([DC, D])
        wo = carve([DC, D])
        bo = carve([D])
        rope = carve([2, 2, HD])
        bias = carve([KVH, QB, P])
        xln = carve([4, D])
        xl2 = xln
        xlnT = carve([DC, 4, P])
        qs = carve([3, D])
        qr = carve([3, D])
        ks = carve([3, D // 2])
        kr = carve([3, D // 2])
        qT = carve([3, 2, 4, 64])
        kT = carve([2, 2, 192])
        vlo = carve([2, D // 2])
        vkey = carve([2, QB, D // 2])
        prob = carve([2, KVH, QB, P])
        pT_at = place[0]
        pT = carve([KVH, QB, P])
        negmax = carve([2, KVH, QB])
        rowsum = carve([2, KVH, QB])
        rinv = carve([2, KVH, QB])
        osb = carve([QB, D // 2])
        oT = carve([4, S])
        inv_s = carve([64])
        asum = carve([4])
        edec = carve([4])
        cgate = carve([3])
        tq = carve([3, D], at=pT_at)
        tk = carve([3, D // 2])
        NTR = 4
        O2 = carve([DC, B, S], at=0)
        tring = carve([NTR, D])
        cring = carve([NTR, DC * B, 12])
        kvb = carve([2, DC * B, NPAIR])
        qx = carve([2, DC * B, 12])
        prodb = carve([DC * B, 8, 8])
        assert place[0] <= 18944
        NW = 4
        wring = carve([NW, 2048], at=16896)
        suT = carve([DC, SHD])
        sdT = carve([SHD // P, D])
        gwT = carve([DC, E])
        ebias = carve([E])
        tri = carve([64])
        x3 = carve([2, D], at=8192)
        W = carve([NT, E])
        t1 = carve([NT, E])
        t2 = carve([NT, E])
        t3 = carve([NT, E])
        t4 = carve([NT, E])
        t5 = carve([NT, E])
        g1 = carve([NT, 8])
        g2 = carve([NT, 8])
        m8 = carve([NT, 8])
        cnt = carve([NT])
        assert place[0] <= 16896, place[0]
        rev = carve([T], at=12288, rows=E)
        key = carve([T], rows=E)
        kvals = carve([P], rows=E)
        empty = carve([P], rows=E)
        idxf = carve([P], rows=E)
        slotno = carve([P], rows=E)
        hid = carve([2, SHD // P, D], at=0)
        xg = carve([4, XW], at=8192)
        xgT = carve([2, DC, P])
        hrel = carve([2, 2, P])
        hsq = carve([2, 2, P])
        ysb = carve([2, D])
        fin = carve([2, 4, D], at=0)
        ps = ctx.enter_context(nc.psum_tensor("ps", [P, NBANK, 512], f32))

        full = [sem(f"bank{k}_filled") for k in range(NBANK)]
        empt = [sem(f"bank{k}_drained") for k in range(NBANK)]
        w_loaded = sem("attention_weights_loaded")
        x_loaded = sem("x_loaded")
        consts_ready = sem("consts_ready")
        small_loaded = sem("small_loaded")
        pad_ready = sem("padded_kernels_ready")
        toep_written = sem("toeplitz_written")
        zero_written = sem("zero_rows_written")
        stats_ready = sem("ln1_stats_ready")
        rstd_ready = sem("ln1_rstd_ready")
        xln_ready = sem("xln_ready")
        bo_added = sem("bo_added")
        asum_ready = sem("asum_ready")
        edec_ready = sem("edec_ready")
        cgate_ready = sem("cgate_ready")
        tq_ready = sem("rope_cos_part_ready")
        rope_ready = sem("rope_ready")
        max_ready = sem("row_max_ready")
        prob_ready = sem("prob_ready")
        stats2_ready = sem("ln2_stats_ready")
        rstd2_ready = sem("ln2_rstd_ready")
        xl2_ready = sem("xl2_ready")
        head_loaded = [sem(f"head_slot{k}_loaded") for k in range(NTR)]
        kv_ready = sem("kv_products_ready")
        qx_ready = sem("q_cyclic_ready")
        ffnw_loaded = sem("ffn_weights_loaded")
        conv_filled = [sem(f"head_slot{k}_multiplied") for k in range(NTR)]
        conv_used = [sem(f"head_slot{k}_products_taken") for k in range(NTR)]
        conv_done = sem("heads_convolved")
        stats3_ready = sem("ln3_stats_ready")
        rstd3_ready = sem("ln3_rstd_ready")
        x3_ready = [sem(f"x3_slot{k}_ready") for k in range(2)]
        x3_written = [sem(f"x3_slot{k}_written") for k in range(2)]
        score_ready = sem("exp_logits_ready")
        sel_ready = sem("selection_ready")
        rev_ready = sem("token_keys_ready")
        gates_ready = sem("gates_ready")
        gates_written = sem("gates_written")
        idxf_ready = sem("slot_tokens_ready")
        idx_ready = sem("slot_rows_ready")
        hid_ready = sem("shared_hidden_ready")
        wexp_loaded = [sem(f"expert_weights_slot{k}_loaded") for k in range(NW)]
        xg_loaded = [sem(f"gathered_slot{k}_loaded") for k in range(4)]
        hsq_ready = sem("expert_hidden_ready")
        y_filled = [sem(f"expert_out_slot{k}_filled") for k in range(4)]
        y_ready = [sem(f"expert_rows{k}_ready") for k in range(2)]
        y_added = sem("expert_out_added")
        scatter_begun = sem("scatter_begun")
        fin_loaded = [sem(f"routed_slot{k}_loaded") for k in range(2)]
        fin_ready = sem("result_ready")
        out_written = sem("out_written")

        names = []
        turn = [0]

        def rot(*fills):
            for f in fills:
                names.append((f, 4 + turn[0] % 4))
                turn[0] += 1

        def scores(b, c):
            names.extend(((("s", b, c, g), g) for g in range(4)))

        rot(*[("xT", u) for u in range(4)])
        rot(*[("q", m) for m in range(3)], ("kv", 0), ("kv", 1), ("kmix",), ("vlo",))
        rot(*[("qT", m) for m in range(3)], ("kT", 0), ("kT", 1))
        scores(0, 0)
        scores(0, 1)
        rot(*[("pT", 0, 0, q) for q in range(QB)])
        scores(1, 0)
        rot(*[("pT", 0, 1, q) for q in range(QB)])
        scores(1, 1)
        rot(*[("pv", 0, q) for q in range(QB)])
        rot(*[("pT", 1, 0, q) for q in range(QB)])
        rot(("mean", 0), *[("oT", 0, c) for c in range(2)])
        rot(*[("pT", 1, 1, q) for q in range(QB)])
        rot(*[("wo", 0, h) for h in range(2)])
        rot(*[("pv", 1, q) for q in range(QB)])
        rot(("mean", 1), *[("oT", 1, c) for c in range(2)])
        rot(*[("wo", 1, h) for h in range(2)])
        ORDER_A = [x for x, _ in names]
        FA = Fills([0] * NBANK, names, 4)
        FQ = Fills(FA.after, [(("x2T", t), 4 + t % 4) for t in range(NT)])
        names = [(("o", t), t % 4) for t in range(NT)] + [(("x3T", t), t % 2) for t in range(NT)]
        names += [(("logit", 0), 2), (("logit", 1), 3)]
        names += [(("selT", q), 4 + q) for q in range(4)] + [(("idxT",), 7)]
        FC = Fills(FQ.after, names)
        names = []
        for c in range(4):
            names += [(("up", c, j), j % 4) for j in range(SHD // P)]
            names += [(("dn", c, j), 4 + j % 2) for j in range(4)]
        FS = Fills(FC.after, names)
        FE = Fills(FS.after, [(("xgT", s), s % 2) for s in range(4)] + [(("h", s), 2 + s % 2) for s in range(4)],
                   E // 4)

        block = ctx.enter_context(nc.Block())

        @block.sync
        def _(sp):
            for s in (*empt, *conv_used, *conv_filled, *y_filled, *y_ready, scatter_begun, hsq_ready):
                sp.sem_inc(s, 1)
            sp.sem_inc(x_loaded, 16)
            with sp.Fori(0, 4) as i:
                sp.wait_ge(x_loaded, i * 16 + 16)
                sp.dma_start(X[:, ds(i * 4, 4), :],
                             a["x"][ds(i * (4 * P), 4 * P), :].rearrange("(t p) d -> p t d", p=P)).then_inc(x_loaded, 16)
            sp.wait_ge(xl2_ready, NT)
            for k in range(4, 8):
                sp.wait_ge(empt[k], FQ.all_drained(k))
            sp.wait_ge(toep_written, 16)
            toep_v = bass.AP(toep.tensor, 1, [[P + D, SH], [1, P], [1, D]])
            with sp.Fori(0, SH // NTR) as i:
                for s in range(NTR):
                    sp.wait_ge(conv_filled[s], i + 1)
                    sp.wait_ge(toep_written, 16)
                    sp.dma_start(tring[:, s:s + 1, :], toep_v[ds(i * NTR + s, 1), :, :].rearrange("h p d -> p h d"))\
                      .then_inc(head_loaded[s], 16)
                    sp.dma_start(cring[:, s, :, :].rearrange("p m i -> p (m i)"),
                                 a["ctxE"][ds((i * NTR + s) * P, P), :]).then_inc(head_loaded[s], 16)
            for t in range(NT):
                sp.wait_ge(x3_ready[t % 2], t // 2 + 1)
                sp.dma_start(xrows[t * P:(t + 1) * P, 0:D], x3[:, t % 2, :]).then_inc(x3_written[t % 2], 16)
            sp.wait_ge(gates_ready, 1)
            sp.dma_start(xrows[0:T, D:XW].rearrange("(t p) c -> p t c", p=P), W).then_inc(gates_written, 16)
            with sp.Fori(0, E // NW) as i:
                for s in range(NW):
                    sp.wait_ge(y_filled[s], i + 1)
                    sp.wait_ge(gates_ready, 1)
                    sp.dma_start(wring[:, s, :], a["wexp"][ds((i * NW + s) * P, P), :]).then_inc(wexp_loaded[s], 16)
            sp.wait_ge(y_added, 16 * E)
            acc_v = acc[0:T, :].rearrange("(t p) d -> p t d", p=P)
            out_v = out.rearrange("(t p) d -> p t d", p=P)
            for g in range(5):
                if g < 4:
                    if g >= 2:
                        sp.wait_ge(fin_ready, g - 1)
                    sp.dma_start(fin[:, g % 2], acc_v[:, 4 * g:4 * g + 4, :]).then_inc(fin_loaded[g % 2], 16)
                if g >= 1:
                    sp.wait_ge(fin_ready, g)
                    sp.dma_start(out_v[:, 4 * g - 4:4 * g, :], X[:, 4 * g - 4:4 * g, :]).then_inc(out_written, 16)
            sp.wait_ge(out_written, 64)

        @block.gpsimd
        def _(pool):
            G.memset(ident[:], 0.0)
            G.memset(minus_half[:], -0.5)
            G.memset(eps[:], EPS)
            G.memset(zeros[:], 0.0)
            G.memset(kpad[:, 0:P], 0.0)
            G.memset(inv_s, 1.0 / S)
            G.drain()
            G.affine_select(out=ident[:], in_=ident[:], compare_op=ALU.not_equal, fill=1.0, base=0,
                            pattern=[[-1, P]], channel_multiplier=1).then_inc(consts_ready, 1)
            pool.wait_ge(small_loaded, 32)
            G.tensor_tensor(kpad[:, P:P + 1], kpad[:, P:P + 1], dcol[:], ALU.add).then_inc(pad_ready, 1)
            for t in range(ROWS // P):
                pool.dma_start(acc[t * P:(t + 1) * P, :], zeros[:]).then_inc(zero_written, 16)
            pool.dma_start(xrows[T:ROWS, 0:D], zeros[:]).then_inc(zero_written, 16)
            pool.dma_start(xrows[T:ROWS, D:XW], zeros[:, 0:E]).then_inc(zero_written, 16)
            pool.wait_ge(w_loaded, 16 * 6)
            with pool.Fori(0, 4) as i:
                pool.wait_ge(stats_ready, i + 1)
                G.tensor_tensor(rstd1[:], meanvar1[:, :, 1], eps[:, 0:4], ALU.add)
                G.drain()
                G.tensor_tensor(rstd1[:], rstd1[:], minus_half[:, 0:4], ALU.pow).then_inc(rstd_ready, 1)
                pool.wait_ge(xln_ready, i * 4 + 4)
                G.tensor_tensor(X[:, ds(i * 4, 4), :], X[:, ds(i * 4, 4), :],
                                bo.unsqueeze(1).broadcast_to((P, 4, D)), ALU.add).then_inc(bo_added, 1)
                for m in range(3):
                    cos = rope[:, min(m, 1), 0, :]
                    kfill = ("kmix",) if m == 0 else ("kv", m - 1)
                    pool.wait_ge(empt[FA.bank(kfill)], FA.drained(kfill, i))
                    pool.wait_ge(empt[FA.bank(("q", m))], FA.drained(("q", m), i))
                    G.tensor_tensor(tk[:, m, :].rearrange("p (h d) -> p h d", d=HD),
                                    ks[:, m, :].rearrange("p (h d) -> p h d", d=HD),
                                    cos.unsqueeze(1).broadcast_to((P, KVH, HD)), ALU.mult)
                    G.tensor_tensor(tq[:, m, :].rearrange("p (h d) -> p h d", d=HD),
                                    qs[:, m, :].rearrange("p (h d) -> p h d", d=HD),
                                    cos.unsqueeze(1).broadcast_to((P, H, HD)), ALU.mult).then_inc(tq_ready, 1)
            pool.wait_ge(stats2_ready, 1)
            G.tensor_tensor(rstd[:], meanvar[:, :, 1], eps[:], ALU.add)
            G.drain()
            G.tensor_tensor(rstd[:], rstd[:], minus_half[:], ALU.pow).then_inc(rstd2_ready, 1)
            qv = QT2[:].rearrange("p l (b s) -> p (l b) s", b=B)
            for k in range(4, 8):
                pool.wait_ge(empt[k], FQ.all_drained(k))
            with pool.Fori(0, SH // NTR) as i:
                for s in range(NTR):
                    h = i * NTR + s
                    pool.wait_ge(conv_used[(s + 2) % NTR], i + (s // 2 + 1))
                    G.tensor_copy(qx[:, s % 2, :, 0:SD], qv[:, :, ds(h * SD, SD)])
                    G.tensor_copy(qx[:, s % 2, :, SD:12], qv[:, :, ds(h * SD, 4)]).then_inc(qx_ready, 1)
                    pool.wait_ge(head_loaded[s], i * 32 + 32)
                    c = cring[:, s, :, :]
                    G.tensor_tensor(kvb[:, s % 2, :, 0:32].rearrange("p m (d i) -> p m d i", d=4),
                                    c[:, :, 0:SD].unsqueeze(2).broadcast_to((P, DC * B, 4, SD)),
                                    bass.AP(c.tensor, c.offset, [list(c.ap[0]), [12, DC * B], [1, 4], [1, SD]]),
                                    ALU.mult)
                    G.tensor_tensor(kvb[:, s % 2, :, 32:36], c[:, :, 0:4], c[:, :, 4:8], ALU.mult)\
                     .then_inc(kv_ready, 1)
            pool.wait_ge(stats3_ready, 1)
            G.tensor_tensor(rstd[:], meanvar[:, :, 1], eps[:], ALU.add)
            G.drain()
            G.tensor_tensor(rstd[:], rstd[:], minus_half[:], ALU.pow).then_inc(rstd3_ready, 1)
            pool.wait_ge(sel_ready, 1)
            G.iota(rev, [[-1, T]], base=T, channel_multiplier=0, allow_small_or_imprecise_dtypes=True)
            G.iota(slotno, [[1, P]], base=0, channel_multiplier=0, allow_small_or_imprecise_dtypes=True)\
             .then_inc(rev_ready, 1)
            for c in range(4):
                for j in range(SHD // P):
                    pool.wait_ge(empt[FS.bank(("up", c, j))], FS.drained(("up", c, j)))
                    G.tensor_tensor(hid[:, c % 2, j, :], hid[:, c % 2, j, :], hid[:, c % 2, j, :], ALU.mult)\
                     .then_inc(hid_ready, 1)
            pool.wait_ge(empt[FC.bank(("idxT",))], FC.drained(("idxT",)))
            for k in range(2):
                pool.wait_ge(x3_written[k], 16 * (NT // 2))
            pool.wait_ge(gates_written, 16)
            pool.wait_ge(zero_written, 16 * (ROWS // P + 2))

            def gather(e, s):
                G.tensor_copy(idxg[:, s:s + 1], idxU[:, ds(e, 1)])
                G.drain()
                pool.indirect_dma_start(xg[:, s, :], None, xrows, bass.IndirectOffsetOnAxis(ap=idxg[:, s:s + 1], axis=0))\
                    .then_inc(xg_loaded[s], 16)

            def scatter(e, s, i):
                pool.wait_ge(y_ready[s % 2], i * 2 + (s // 2 + 2))
                G.tensor_copy(idxs[:, s % 2:s % 2 + 1], idxU[:, ds(e, 1)]).then_inc(scatter_begun, 1)
                G.drain()
                pool.indirect_dma_start(acc, bass.IndirectOffsetOnAxis(ap=idxs[:, s % 2:s % 2 + 1], axis=0),
                                        ysb[:, s % 2, :], None, compute_op=ALU.add).then_inc(y_added, 16)

            for s in range(4):
                gather(s, s)
            with pool.Fori(0, E // 4 - 1) as i:
                for s in range(4):
                    scatter(i * 4 + s, s, i)
                    gather(i * 4 + (s + 4), s)
                    pool.wait_ge(y_added, (i * 4 + s) * 16 + 16)
            for s in range(4):
                scatter(E - 4 + s, s, E // 4 - 1)
                pool.wait_ge(y_added, (E - 4 + s) * 16 + 16)

        @block.scalar
        def _(act):
            def load(dst, name, s):
                act.dma_start(dst, a[name]).then_inc(s, 16)
            load(wq, "wq", w_loaded)
            load(kpad[:, P:], "kern", small_loaded)
            load(dcol[:], "skip", small_loaded)
            load(wkv, "wkv", w_loaded)
            load(rope, "rope", w_loaded)
            load(bias, "bias", w_loaded)
            load(bo, "bo", w_loaded)
            load(wo, "wo", w_loaded)
            act.wait_ge(pad_ready, 1)
            act.dma_start(toep[:], kpad[:]).then_inc(toep_written, 16)

            def evacuate(fills, name, i, dst, src, scale=None):
                bank = fills.bank(name)
                act.wait_ge(full[bank], fills.filled(name, i))
                kw = {} if scale is None else {"scale": scale}
                A.activation(dst, src, ACT.Copy, **kw).then_inc(empt[bank], 1)

            def quad(bank, rows=P):
                return ps[0:rows, bank, :].rearrange("p (c t) -> p c t", c=4)

            def exps(b, c, i):
                act.wait_ge(max_ready, i * 4 + 2 * b + c + 1)
                for g in range(4):
                    for q in range(QB):
                        k = 4 * c + g
                        ins = A.activation(prob[:, b, k, q, :], prob[:, b, k, q, :], ACT.Exp,
                                           bias=negmax[:, b, k, q:q + 1], scale=1.0,
                                           accum_out=rowsum[:, b, k, q:q + 1])
                ins.then_inc(prob_ready, 1)

            def probs_T(b, c, q, i):
                name = ("pT", b, c, q)
                evacuate(FA, name, i, pT[:, 4 * c:4 * c + 4, q, :], quad(FA.bank(name)))

            def attended_T(b, i):
                for c in range(2):
                    name = ("oT", b, c)
                    evacuate(FA, name, i,
                             oT[:, 2 * c:2 * c + 2, 64:S].rearrange("p r (q t) -> p q r t", q=QB),
                             ps[:, FA.bank(name), 0:3 * P].rearrange("p (q r t) -> p q r t", q=QB, r=2))

            with act.Fori(0, 4) as i:
                for u in range(4):
                    name = ("xT", u)
                    src = quad(FA.bank(name))
                    if u == 2:
                        act.wait_ge(full[FA.bank(name)], FA.filled(name, i))
                        A.activation(xlnT[:, :, 1, 64:P], src[:, :, 0:64], ACT.Copy)
                        A.activation(xlnT[:, :, 1, 0:64], src[:, :, 64:P], ACT.Copy).then_inc(empt[FA.bank(name)], 1)
                    else:
                        evacuate(FA, name, i, xlnT[:, :, {0: 0, 1: 2, 3: 3}[u], :], src)
                act.wait_ge(asum_ready, i + 1)
                A.activation(edec, asum, ACT.Exp, scale=-1.0).then_inc(edec_ready, 1)
                act.wait_ge(cgate_ready, i + 1)
                for m in range(3):
                    evacuate(FA, ("q", m), i, qs[:, m, :], ps[:, FA.bank(("q", m)), :], scale=cgate[:, m:m + 1])
                evacuate(FA, ("kmix",), i, ks[:, 0, :], ps[:, FA.bank(("kmix",)), 0:D // 2])
                for m in range(3):
                    evacuate(FA, ("qT", m), i, qT[:, m, :, :, :].rearrange("p n k t -> p k n t"),
                             quad(FA.bank(("qT", m))).rearrange("p k (n t) -> p k n t", n=2))
                bank = FA.bank(("kT", 0))
                act.wait_ge(full[bank], FA.filled(("kT", 0), i))
                for b in range(2):
                    A.activation(kT[:, b, :, 0:64],
                                 ps[:, bank, 0:2 * P].rearrange("p (c t) -> p c t", c=2)[:, :, b * 64:b * 64 + 64],
                                 ACT.Copy)
                A.activation(kT[:, 0, :, 64:192], ps[:, bank, 2 * P:4 * P].rearrange("p (c t) -> p c t", c=2),
                             ACT.Copy).then_inc(empt[bank], 1)
                evacuate(FA, ("kT", 1), i, kT[:, 1, :, 64:192],
                         ps[:, FA.bank(("kT", 1)), 0:2 * P].rearrange("p (c t) -> p c t", c=2))
                exps(0, 0, i)
                exps(0, 1, i)
                probs_T(0, 0, 0, i)
                probs_T(0, 0, 2, i)
                exps(1, 0, i)
                probs_T(0, 1, 0, i)
                probs_T(0, 1, 2, i)
                exps(1, 1, i)
                probs_T(1, 0, 0, i)
                probs_T(1, 0, 2, i)
                attended_T(0, i)
                probs_T(1, 1, 0, i)
                probs_T(1, 1, 2, i)
                attended_T(1, i)
            for t in range(NT):
                name = ("x2T", t)
                evacuate(FQ, name, 0, QT2[:, :, t * P:(t + 1) * P], quad(FQ.bank(name)))
            load(suT, "suT", ffnw_loaded)
            load(sdT, "sdT", ffnw_loaded)
            load(gwT, "gwT", ffnw_loaded)
            load(ebias, "ebias", ffnw_loaded)
            load(tri, "tri", ffnw_loaded)
            for t in range(NT):
                name = ("x3T", t)
                evacuate(FC, name, 0, x3T[:, :, t * P:(t + 1) * P], quad(FC.bank(name)))
            for k in range(2):
                act.wait_ge(full[2 + k], FC.filled(("logit", k)))
                A.activation(t1[:, 8 * k:8 * k + 8, :], ps[:, 2 + k, :].rearrange("p (t e) -> p t e", e=E),
                             ACT.Exp, scale=-1.0).then_inc(empt[2 + k], 1)
            for c in range(4):
                for j in range(SHD // P):
                    bank = FS.bank(("up", c, j))
                    if c >= 2 and j == 0:
                        act.wait_ge(full[FS.bank(("dn", c - 2, 3))], FS.filled(("dn", c - 2, 3)))
                    act.wait_ge(full[bank], FS.filled(("up", c, j)))
                    A.activation(hid[:, c % 2, j, :], ps[:, bank, :], ACT.Relu).then_inc(empt[bank], 1)
            with act.Fori(0, E // 4) as i:
                for s in range(4):
                    evacuate(FE, ("xgT", s), i, xgT[:, s % 2, :, :], quad(FE.bank(("xgT", s))))
                    bank = FE.bank(("h", s))
                    act.wait_ge(full[bank], FE.filled(("h", s), i))
                    act.wait_ge(hsq_ready, i * 4 + max(s, 1))
                    A.activation(hrel[:, s % 2, :, :].rearrange("p c t -> p (c t)"), ps[:, bank, 0:2 * P], ACT.Relu)\
                     .then_inc(empt[bank], 1)

        @block.vector
        def _(dve):
            def heads(v):
                return v.rearrange("p (h d) -> p h d", d=HD)

            def scores_out(b, c, i):
                for g in range(4):
                    bank = FA.bank(("s", b, c, g))
                    dve.wait_ge(full[bank], FA.filled(("s", b, c, g), i))
                    V.scalar_tensor_tensor(prob[:, b, 4 * c + g, :, :].rearrange("p q k -> p (q k)"),
                                           ps[:, bank, 0:QB * P], 1.0 / np.sqrt(HD).astype(np.float32).item(),
                                           bias[:, 4 * c + g, :, :].rearrange("p q k -> p (q k)"),
                                           op0=ALU.mult, op1=ALU.add).then_inc(empt[bank], 1)
                V.drain()
                V.tensor_reduce(negmax[:, b, 4 * c:4 * c + 4, :], prob[:, b, 4 * c:4 * c + 4, :, :],
                                axis=AX.X, op=ALU.max, negate=True).then_inc(max_ready, 1)

            def probs_T(b, c, i):
                name = ("pT", b, c, 1)
                bank = FA.bank(name)
                dve.wait_ge(full[bank], FA.filled(name, i))
                V.tensor_copy(pT[:, 4 * c:4 * c + 4, 1, :], ps[:, bank, :].rearrange("p (g t) -> p g t", g=4))\
                 .then_inc(empt[bank], 1)

            def inverse_sums(b, i):
                dve.wait_ge(prob_ready, i * 4 + 2 * b + 2)
                V.reciprocal(rinv[:, b, :, :], rowsum[:, b, :, :])
                V.drain()

            def attended(b, i):
                for q in range(QB):
                    bank = FA.bank(("pv", b, q))
                    dve.wait_ge(full[bank], FA.filled(("pv", b, q), i))
                    V.tensor_tensor(heads(osb[:, q, :]), heads(ps[:, bank, 0:D // 2]),
                                    rinv[:, b, :, q:q + 1].broadcast_to((P, KVH, HD)), ALU.mult)\
                     .then_inc(empt[bank], 1)

            def mean_rows(b, i):
                bank = FA.bank(("mean", b))
                dve.wait_ge(full[bank], FA.filled(("mean", b), i))
                V.tensor_copy(oT[:, :, 0:64].rearrange("p (c r) t -> p c r t", c=2),
                              ps[:, bank, 0:P].rearrange("p (c t) -> p c t", c=2).unsqueeze(2)
                              .broadcast_to((P, 2, 2, 64))).then_inc(empt[bank], 1)

            def project(b, i):
                for h in range(2):
                    bank = FA.bank(("wo", b, h))
                    if b == 0 and h == 0:
                        dve.wait_ge(bo_added, i + 1)
                    dve.wait_ge(full[bank], FA.filled(("wo", b, h), i))
                    xt = X[:, ds(i * 4 + (2 * b + h), 1), :].rearrange("p t d -> p (t d)")
                    V.tensor_tensor(xt, xt, ps[:, bank, :], ALU.add).then_inc(empt[bank], 1)
                V.drain()
                for h in range(2):
                    V.bn_stats(stats[:, ds(i * 4 + (2 * b + h), 1), :].rearrange("p t d -> p (t d)"),
                               X[:, ds(i * 4 + (2 * b + h), 1), :].rearrange("p t d -> p (t d)"))

            dve.wait_ge(w_loaded, 16 * 6)
            with dve.Fori(0, 4) as i:
                dve.wait_ge(x_loaded, i * 16 + 32)
                for u in range(4):
                    V.bn_stats(stats1[:, u, :], X[:, ds(i * 4 + u, 1), :].rearrange("p t d -> p (t d)"))
                V.drain()
                for u in range(4):
                    ins = V.bn_aggr(meanvar1[:, u, :], stats1[:, u, :])
                ins.then_inc(stats_ready, 1)
                dve.wait_ge(rstd_ready, i + 1)
                for u in range(4):
                    V.tensor_scalar(xln[:, u, :], X[:, ds(i * 4 + u, 1), :].rearrange("p t d -> p (t d)"),
                                    meanvar1[:, u, 0:1], rstd1[:, u:u + 1], ALU.subtract, ALU.mult)\
                     .then_inc(xln_ready, 1)
                V.drain()
                V.tensor_reduce(asum, xln, axis=AX.X, op=ALU.add, apply_absolute_value=True).then_inc(asum_ready, 1)
                dve.wait_ge(edec_ready, i + 1)
                V.tensor_scalar(edec, edec, 1.0, None, ALU.add)
                V.drain()
                V.reciprocal(cgate[0:64, 0:1], edec[64:P, 0:1])
                V.reciprocal(cgate[64:P, 0:1], edec[64:P, 2:3])
                V.reciprocal(cgate[:, 1:2], edec[:, 1:2])
                V.reciprocal(cgate[:, 2:3], edec[:, 3:4]).then_inc(cgate_ready, 1)
                for b in range(2):
                    bank = FA.bank(("kv", b))
                    dve.wait_ge(full[bank], FA.filled(("kv", b), i))
                    V.tensor_copy(ks[:, 1 + b, :], ps[:, bank, 0:D // 2])
                    V.tensor_copy(vkey[:, b, 0, :], ps[:, bank, D // 2:D])
                    V.tensor_copy(vkey[64:P, b, 1, :], ps[64:P, bank, D // 2:D])
                    V.tensor_copy(vkey[64:P, b, 2, :], ps[0:64, bank, D // 2:D]).then_inc(empt[bank], 1)
                bank = FA.bank(("vlo",))
                dve.wait_ge(full[bank], FA.filled(("vlo",), i))
                V.tensor_copy(vlo, ps[:, bank, :].rearrange("p (b d) -> p b d", b=2))
                for b in range(2):
                    rows = slice(64, P) if b == 0 else slice(0, 64)
                    for q in (1, 2):
                        ins = V.tensor_copy(vkey[0:64, b, q, :], ps[rows, bank, b * 256:(b + 1) * 256])
                ins.then_inc(empt[bank], 1)
                for m in range(3):
                    sin = rope[:, min(m, 1), 1, :]
                    kfill = ("kmix",) if m == 0 else ("kv", m - 1)
                    dve.wait_ge(empt[FA.bank(kfill)], FA.drained(kfill, i))
                    dve.wait_ge(empt[FA.bank(("q", m))], FA.drained(("q", m), i))
                    for src, dst, n in ((ks, kr, KVH), (qs, qr, H)):
                        for lo, hi in ((0, 16), (16, 0)):
                            V.tensor_tensor(heads(dst[:, m, :])[:, :, lo:lo + 16], heads(src[:, m, :])[:, :, hi:hi + 16],
                                            sin[:, lo:lo + 16].unsqueeze(1).broadcast_to((P, n, 16)), ALU.mult)
                    V.drain()
                    dve.wait_ge(tq_ready, i * 3 + m + 1)
                    V.tensor_tensor(kr[:, m, :], kr[:, m, :], tk[:, m, :], ALU.add)
                    V.tensor_tensor(qr[:, m, :], qr[:, m, :], tq[:, m, :], ALU.add).then_inc(rope_ready, 1)
                scores_out(0, 0, i)
                scores_out(0, 1, i)
                probs_T(0, 0, i)
                scores_out(1, 0, i)
                probs_T(0, 1, i)
                scores_out(1, 1, i)
                inverse_sums(0, i)
                attended(0, i)
                probs_T(1, 0, i)
                mean_rows(0, i)
                probs_T(1, 1, i)
                project(0, i)
                inverse_sums(1, i)
                attended(1, i)
                mean_rows(1, i)
                project(1, i)
            V.drain()
            for t in range(NT):
                ins = V.bn_aggr(meanvar[:, t, :], stats[:, t, :])
            ins.then_inc(stats2_ready, 1)
            dve.wait_ge(rstd2_ready, 1)
            for t in range(NT):
                if t >= 4:
                    dve.wait_ge(full[FQ.bank(("x2T", t - 4))], FQ.filled(("x2T", t - 4)))
                V.tensor_scalar(xl2[:, t % 4, :], X[:, t, :], meanvar[:, t, 0:1], rstd[:, t:t + 1],
                                ALU.subtract, ALU.mult).then_inc(xl2_ready, 1)
            pr = prodb.rearrange("p (l b) j k -> p l b j k", l=DC)
            with dve.Fori(0, SH // NTR) as i:
                for s in range(NTR):
                    k0 = 4 * (s % 2)
                    dve.wait_ge(conv_filled[s], i + 2)
                    dve.wait_ge(qx_ready, i * NTR + s + 1)
                    y = ps[:, k0:k0 + DC, 0:B * NPAIR].rearrange("p l (b n) -> p l b n", n=NPAIR)
                    q = qx[:, s % 2, :, :].rearrange("p (l b) j -> p l b j", l=DC)
                    for d in range(4):
                        V.tensor_tensor(pr[:, :, :, :, d], y[:, :, :, 8 * d:8 * d + 8], q[:, :, :, d:d + 8], ALU.mult)
                        if d:
                            V.tensor_tensor(pr[:, :, :, d:8, 3 + d], y[:, :, :, 8 * d:8 * d + 8 - d],
                                            q[:, :, :, 0:8 - d], ALU.mult)
                            V.tensor_tensor(pr[:, :, :, 0:d, 3 + d], y[:, :, :, 8 * d + 8 - d:8 * d + 8],
                                            q[:, :, :, 8 - d:8], ALU.mult)
                    V.tensor_tensor(pr[:, :, :, 0:4, 7], y[:, :, :, 32:36], q[:, :, :, 4:8], ALU.mult)
                    V.tensor_tensor(pr[:, :, :, 4:8, 7], y[:, :, :, 32:36], q[:, :, :, 0:4], ALU.mult)\
                     .then_inc(conv_used[s], 1)
                    V.drain()
                    V.tensor_reduce(O2.rearrange("p l b s -> p (l b) s")[:, :, ds((i * NTR + s) * SD, SD)],
                                    prodb, axis=AX.X, op=ALU.add).then_inc(conv_done, 1)
                    V.drain()
            for t in range(NT):
                bank = FC.bank(("o", t))
                dve.wait_ge(full[bank], FC.filled(("o", t)))
                V.tensor_tensor(X[:, t, :], X[:, t, :], ps[:, bank, :], ALU.add).then_inc(empt[bank], 1)
                V.drain()
                V.bn_stats(stats[:, t, :], X[:, t, :])
            V.drain()
            for t in range(NT):
                ins = V.bn_aggr(meanvar[:, t, :], stats[:, t, :])
            ins.then_inc(stats3_ready, 1)
            dve.wait_ge(rstd3_ready, 1)
            for t in range(NT):
                if t >= 2:
                    dve.wait_ge(full[FC.bank(("x3T", t - 2))], FC.filled(("x3T", t - 2)))
                    dve.wait_ge(x3_written[t % 2], 16 * (t // 2))
                V.tensor_scalar(x3[:, t % 2, :], X[:, t, :], meanvar[:, t, 0:1], rstd[:, t:t + 1],
                                ALU.subtract, ALU.mult).then_inc(x3_ready[t % 2], 1)
            dve.wait_ge(ffnw_loaded, 16 * 5)
            for k in range(2):
                dve.wait_ge(empt[2 + k], FC.drained(("logit", k)))
            tile64 = (P, NT, E)
            V.tensor_scalar(t1, t1, 1.0, None, ALU.add)
            V.memset(W, 1.0)
            V.drain()
            V.reciprocal(t1, t1)
            V.memset(W[:, :, 0:1], 0.0)
            V.drain()
            V.tensor_tensor(t2, t1, ebias.unsqueeze(1).broadcast_to(tile64), ALU.add)
            V.drain()
            v = t2.rearrange("p t (g e) -> p (t g) e", e=8)
            flat3 = t3.rearrange("p t e -> p (t e)")
            flat4 = t4.rearrange("p t e -> p (t e)")
            flat5 = t5.rearrange("p t e -> p (t e)")
            NP8 = NT * NG
            hi4 = flat3[:, 0:4 * NP8].rearrange("p (n e) -> p n e", e=4)
            lo4 = flat3[:, 4 * NP8:8 * NP8].rearrange("p (n e) -> p n e", e=4)
            V.tensor_tensor(hi4, v[:, :, 0:4], v[:, :, 4:8], ALU.max)
            V.tensor_tensor(lo4, v[:, :, 0:4], v[:, :, 4:8], ALU.min)
            V.drain()
            hi2, mn2, mx2, lo2 = (flat4[:, 2 * k * NP8:2 * (k + 1) * NP8].rearrange("p (n e) -> p n e", e=2)
                                  for k in range(4))
            V.tensor_tensor(hi2, hi4[:, :, 0:2], hi4[:, :, 2:4], ALU.max)
            V.tensor_tensor(mn2, hi4[:, :, 0:2], hi4[:, :, 2:4], ALU.min)
            V.tensor_tensor(mx2, lo4[:, :, 0:2], lo4[:, :, 2:4], ALU.max)
            V.drain()
            V.tensor_tensor(lo2, mn2, mx2, ALU.max)
            V.drain()
            hi1, mn1, mx1, lo1 = (flat5[:, k * NP8:(k + 1) * NP8].rearrange("p (n e) -> p n e", e=1) for k in range(4))
            V.tensor_tensor(hi1, hi2[:, :, 0:1], hi2[:, :, 1:2], ALU.max)
            V.tensor_tensor(mn1, hi2[:, :, 0:1], hi2[:, :, 1:2], ALU.min)
            V.tensor_tensor(mx1, lo2[:, :, 0:1], lo2[:, :, 1:2], ALU.max)
            V.drain()
            V.tensor_tensor(lo1, mn1, mx1, ALU.max)
            V.drain()
            V.tensor_tensor(g1.rearrange("p t g -> p (t g)").unsqueeze(2), hi1, lo1, ALU.add)
            V.drain()
            gg = (P, NT, NG, NG)
            other = g1.unsqueeze(2).broadcast_to(gg)
            own = g1.unsqueeze(3).broadcast_to(gg)
            gt3 = t3.rearrange("p t (g h) -> p t g h", h=NG)
            eq4 = t4.rearrange("p t (g h) -> p t g h", h=NG)
            V.tensor_tensor(gt3, other, own, ALU.is_gt)
            V.tensor_tensor(eq4, other, own, ALU.is_equal)
            V.drain()
            V.tensor_tensor(t4, t4, tri.unsqueeze(1).broadcast_to(tile64), ALU.mult)
            V.drain()
            V.tensor_tensor(t3, t3, t4, ALU.add)
            V.drain()
            V.tensor_reduce(g2, gt3, axis=AX.X, op=ALU.add)
            V.drain()
            V.tensor_scalar(g2, g2, TKG - 0.5, None, ALU.is_lt)
            V.drain()
            V.tensor_scalar(g1, g2, 1e30, -1e30, ALU.mult, ALU.add)
            V.tensor_tensor(t3.rearrange("p t (g e) -> p (t g) e", e=8), v,
                            g2.rearrange("p t g -> p (t g)").unsqueeze(2).broadcast_to((P, NP8, 8)), ALU.mult)
            V.drain()
            V.tensor_tensor(t3.rearrange("p t (g e) -> p (t g) e", e=8), t3.rearrange("p t (g e) -> p (t g) e", e=8),
                            g1.rearrange("p t g -> p (t g)").unsqueeze(2).broadcast_to((P, NP8, 8)), ALU.add)
            V.drain()
            for t in range(NT):
                V.max(m8[:, t, :], t3[:, t, :])
            V.drain()
            kth = m8[:, :, K - 1:K].broadcast_to(tile64)
            V.tensor_tensor(t4, t3, kth, ALU.is_gt)
            V.tensor_tensor(t5, t3, kth, ALU.is_equal)
            V.drain()
            V.tensor_reduce(cnt, t4, axis=AX.X, op=ALU.add)
            V.tensor_tensor_scan(t2.rearrange("p t e -> p (t e)"), W.rearrange("p t e -> p (t e)"), flat5, 0.0,
                                 ALU.mult, ALU.add)
            V.drain()
            V.tensor_scalar(cnt, cnt, -1.0, K + 0.5, ALU.mult, ALU.add)
            V.drain()
            V.tensor_tensor(t2, t2, cnt.unsqueeze(2).broadcast_to(tile64), ALU.is_lt)
            V.drain()
            V.tensor_tensor(t2, t2, t5, ALU.mult)
            V.drain()
            V.tensor_tensor(t2, t2, t4, ALU.add).then_inc(sel_ready, 1)
            V.drain()
            V.tensor_tensor(W, t2, t1, ALU.mult)
            V.drain()
            V.tensor_reduce(cnt, W, axis=AX.X, op=ALU.add)
            V.drain()
            V.tensor_scalar(cnt, cnt, 1e-20, None, ALU.add)
            V.drain()
            V.reciprocal(cnt, cnt)
            V.drain()
            V.tensor_tensor(W, W, cnt.unsqueeze(2).broadcast_to(tile64), ALU.mult)
            V.drain()
            V.tensor_scalar(W, W, 2.5, None, ALU.mult).then_inc(gates_ready, 1)
            V.drain()
            dve.wait_ge(rev_ready, 1)
            for q in range(4):
                bank = FC.bank(("selT", q))
                dve.wait_ge(full[bank], FC.filled(("selT", q)))
                V.tensor_tensor(key[:, q * 512:(q + 1) * 512], ps[0:E, bank, :], rev[:, q * 512:(q + 1) * 512],
                                ALU.mult).then_inc(empt[bank], 1)
            V.drain()

            def best_keys(lo, hi):
                for r in range(lo, hi):
                    V.max(kvals[:, 8 * r:8 * r + 8], key)
                    V.drain()
                    if r < CAP // 8 - 1:
                        V.match_replace(key, kvals[:, 8 * r:8 * r + 8], key, 0.0)
                        V.drain()

            def shared_out(c):
                for j in range(4):
                    bank = FS.bank(("dn", c, j))
                    dve.wait_ge(full[bank], FS.filled(("dn", c, j)))
                    V.tensor_tensor(X[:, 4 * c + j, :], X[:, 4 * c + j, :], ps[:, bank, :], ALU.add)\
                     .then_inc(empt[bank], 1)

            best_keys(0, 6)
            shared_out(0)
            best_keys(6, 12)
            shared_out(1)
            best_keys(12, CAP // 8)
            V.tensor_scalar(empty, kvals, 0.0, None, ALU.is_equal)
            V.tensor_scalar(idxf, kvals, -1.0, float(T), ALU.mult, ALU.add)
            V.drain()
            V.tensor_tensor(empty, empty, slotno, ALU.mult)
            V.drain()
            V.tensor_tensor(idxf, idxf, empty, ALU.add).then_inc(idxf_ready, 1)
            shared_out(2)
            bank = FC.bank(("idxT",))
            dve.wait_ge(full[bank], FC.filled(("idxT",)))
            V.tensor_copy(idxU[:], ps[:, bank, 0:E]).then_inc(empt[bank], 1)
            shared_out(3)
            with dve.Fori(0, E // 4) as i:
                for s in range(4):
                    bank = FE.bank(("h", s))
                    dve.wait_ge(empt[bank], FE.drained(("h", s), i))
                    V.tensor_tensor(hsq[:, s % 2, :, :], hrel[:, s % 2, :, :], hrel[:, s % 2, :, :], ALU.mult)\
                     .then_inc(hsq_ready, 1)
                    dve.wait_ge(y_filled[s], i + 2)
                    dve.wait_ge(scatter_begun, i * 4 + (s + 1))
                    dve.wait_ge(xg_loaded[s], i * 16 + 16)
                    V.tensor_scalar(ysb[:, s % 2, :], ps[:, 4 + s % 2, :], xg[:, s, ds(i * 4 + (D + s), 1)], None, ALU.mult)\
                     .then_inc(y_ready[s % 2], 1)
            for g in range(4):
                dve.wait_ge(fin_loaded[g % 2], 16 * (g // 2 + 1))
                V.tensor_tensor(X[:, 4 * g:4 * g + 4, :], X[:, 4 * g:4 * g + 4, :], fin[:, g % 2], ALU.add)\
                 .then_inc(fin_ready, 1)

        @block.tensor
        def _(pe):
            def fill(fills, name, i=0):
                bank = fills.bank(name)
                pe.wait_ge(empt[bank], fills.free(name, i))
                return bank

            def product(out_ap, pairs):
                for n, (lhsT, rhs) in enumerate(pairs):
                    ins = TE.matmul(out_ap, lhsT, rhs, start=(n == 0), stop=(n == len(pairs) - 1))
                return ins

            def probs_T(b, c, i):
                pe.wait_ge(prob_ready, i * 4 + 2 * b + c + 1)
                for q in range(QB):
                    bank = fill(FA, ("pT", b, c, q), i)
                    for g in range(4):
                        ins = TE.transpose(ps[:, bank, g * P:(g + 1) * P], prob[:, b, 4 * c + g, q, :], ident[:])
                    ins.then_inc(full[bank], 1)

            def scores(b, c, i):
                for g in range(4):
                    bank = fill(FA, ("s", b, c, g), i)
                    rows = slice(32 * g, 32 * g + 32)
                    for q in range(QB):
                        m, half = (0, b) if q == 0 else (1 + b, q - 1)
                        keys = (kT[rows, b, c, 64:192],
                                kT[rows, b, c, :].rearrange("p (n t) -> p n t", t=64)[:, 0:3:2, :],
                                kT[rows, b, c, 0:P])[q]
                        ins = TE.matmul(ps[:, bank, q * P:(q + 1) * P],
                                        qT[rows, m, half, 2 * c:2 * c + 2, :], keys, start=True, stop=True)
                    ins.then_inc(full[bank], 1)

            def attend(b, i):
                for c in range(2):
                    for q in range(QB):
                        name = ("pT", b, c, q)
                        pe.wait_ge(empt[FA.bank(name)], FA.drained(name, i))
                for q in range(QB):
                    bank = fill(FA, ("pv", b, q), i)
                    for k in range(KVH):
                        ins = TE.matmul(ps[:, bank, k * HD:(k + 1) * HD], pT[:, k, q, :],
                                        vkey[:, b, q, k * HD:(k + 1) * HD], start=True, stop=True)
                    ins.then_inc(full[bank], 1)

            def mean_rows(b, i):
                bank = fill(FA, ("mean", b), i)
                for c in range(2):
                    ins = product(ps[:, bank, c * 64:(c + 1) * 64],
                                  [(vlo[:, b, c * P:(c + 1) * P], inv_s), (vkey[:, b, 0, c * P:(c + 1) * P], inv_s)])
                ins.then_inc(full[bank], 1)

            def attended_T(b, i):
                for q in range(QB):
                    name = ("pv", b, q)
                    pe.wait_ge(empt[FA.bank(name)], FA.drained(name, i))
                for c in range(2):
                    bank = fill(FA, ("oT", b, c), i)
                    for q in range(QB):
                        ins = TE.transpose(ps[:, bank, q * P:(q + 1) * P], osb[:, q, c * P:(c + 1) * P], ident[:])
                    ins.then_inc(full[bank], 1)

            def project(b, i):
                for name in (("mean", b), ("oT", b, 0), ("oT", b, 1)):
                    pe.wait_ge(empt[FA.bank(name)], FA.drained(name, i))
                for h in range(2):
                    bank = fill(FA, ("wo", b, h), i)
                    product(ps[:, bank, :], [(oT[:, k, h * P:(h + 1) * P], wo[:, k, :]) for k in range(4)])\
                        .then_inc(full[bank], 1)

            pe.wait_ge(consts_ready, 1)
            pe.wait_ge(w_loaded, 16 * 6)
            with pe.Fori(0, 4) as i:
                for u in range(4):
                    pe.wait_ge(xln_ready, i * 4 + u + 1)
                    bank = fill(FA, ("xT", u), i)
                    for c in range(DC):
                        ins = TE.transpose(ps[:, bank, c * P:(c + 1) * P], xln[:, u, c * P:(c + 1) * P], ident[:])
                    ins.then_inc(full[bank], 1)
                for u in range(4):
                    pe.wait_ge(empt[FA.bank(("xT", u))], FA.drained(("xT", u), i))
                tokens = (lambda c: xlnT[:, c, 0:2, :].rearrange("p u t -> p (u t)")[:, 64:64 + P],
                          lambda c: xlnT[:, c, 2, :], lambda c: xlnT[:, c, 3, :])
                for m in range(3):
                    bank = fill(FA, ("q", m), i)
                    product(ps[:, bank, :], [(tokens[m](c), wq[:, c, :]) for c in range(DC)]).then_inc(full[bank], 1)
                for b in range(2):
                    bank = fill(FA, ("kv", b), i)
                    product(ps[:, bank, :], [(tokens[1 + b](c), wkv[:, c, :]) for c in range(DC)])\
                        .then_inc(full[bank], 1)
                bank = fill(FA, ("kmix",), i)
                product(ps[:, bank, 0:D // 2], [(tokens[0](c), wkv[:, c, 0:D // 2]) for c in range(DC)])\
                    .then_inc(full[bank], 1)
                bank = fill(FA, ("vlo",), i)
                for b in range(2):
                    ins = product(ps[:, bank, b * 256:(b + 1) * 256],
                                  [(xlnT[:, c, b, :], wkv[:, c, D // 2:D]) for c in range(DC)])
                ins.then_inc(full[bank], 1)
                for m in range(3):
                    pe.wait_ge(rope_ready, i * 3 + m + 1)
                    bank = fill(FA, ("qT", m), i)
                    for k in range(4):
                        ins = TE.transpose(ps[:, bank, k * P:(k + 1) * P], qr[:, m, k * P:(k + 1) * P], ident[:])
                    ins.then_inc(full[bank], 1)
                for n, ms in enumerate(((0, 1), (2,))):
                    bank = fill(FA, ("kT", n), i)
                    for k, m in enumerate(ms):
                        for c in range(2):
                            ins = TE.transpose(ps[:, bank, (2 * k + c) * P:(2 * k + c + 1) * P],
                                               kr[:, m, c * P:(c + 1) * P], ident[:])
                    ins.then_inc(full[bank], 1)
                for name in (("qT", 0), ("qT", 1), ("qT", 2), ("kT", 0), ("kT", 1)):
                    pe.wait_ge(empt[FA.bank(name)], FA.drained(name, i))
                scores(0, 0, i)
                scores(0, 1, i)
                probs_T(0, 0, i)
                scores(1, 0, i)
                probs_T(0, 1, i)
                scores(1, 1, i)
                attend(0, i)
                probs_T(1, 0, i)
                mean_rows(0, i)
                attended_T(0, i)
                probs_T(1, 1, i)
                project(0, i)
                attend(1, i)
                mean_rows(1, i)
                attended_T(1, i)
                project(1, i)
            for t in range(NT):
                pe.wait_ge(xl2_ready, t + 1)
                bank = fill(FQ, ("x2T", t))
                for c in range(DC):
                    ins = TE.transpose(ps[:, bank, c * P:(c + 1) * P], xl2[:, t % 4, c * P:(c + 1) * P], ident[:])
                ins.then_inc(full[bank], 1)
            for k in range(NBANK):
                pe.wait_ge(empt[k], FQ.all_drained(k))
            with pe.Fori(0, SH // NTR) as i:
                for s in range(NTR):
                    pe.wait_ge(head_loaded[s], i * 32 + 32)
                    pe.wait_ge(kv_ready, i * NTR + s + 1)
                    pe.wait_ge(conv_used[(s + 2) % NTR], i + (s // 2 + 1))
                    for lt in range(DC):
                        ins = product(ps[:, 4 * (s % 2) + lt, 0:B * NPAIR],
                                      [(tring[:, s, (lt - mt) * P:(lt - mt + 1) * P],
                                        kvb[:, s % 2, mt * B:(mt + 1) * B, :].rearrange("p b n -> p (b n)"))
                                       for mt in range(lt + 1)])
                    ins.then_inc(conv_filled[s], 1)
            pe.wait_ge(conv_done, SH)
            for t in range(NT):
                bank = fill(FC, ("o", t))
                at = (t % 2) * P
                for c in range(DC):
                    ins = TE.transpose(ps[:, bank, c * P:(c + 1) * P], O2[:, c, t // 2, at:at + P], ident[:])
                ins.then_inc(full[bank], 1)

            def logits(t):
                name = ("x3T", t)
                pe.wait_ge(empt[FC.bank(name)], FC.drained(name))
                bank = fill(FC, ("logit", t // 8))
                ins = product(ps[:, bank, (t % 8) * E:(t % 8 + 1) * E],
                              [(x3T[:, c, t * P:(t + 1) * P], gwT[:, c, :]) for c in range(DC)])
                if t % 8 == 7:
                    ins.then_inc(full[bank], 1)

            pe.wait_ge(ffnw_loaded, 16 * 5)
            for t in range(NT):
                pe.wait_ge(x3_ready[t % 2], t // 2 + 1)
                bank = fill(FC, ("x3T", t))
                for c in range(DC):
                    ins = TE.transpose(ps[:, bank, c * P:(c + 1) * P], x3[:, t % 2, c * P:(c + 1) * P], ident[:])
                ins.then_inc(full[bank], 1)
                if t:
                    logits(t - 1)
            logits(NT - 1)

            def shared_up(c):
                for j in range(SHD // P):
                    bank = fill(FS, ("up", c, j))
                    product(ps[:, bank, :], [(suT[:, k, j * P:(j + 1) * P], x3T[:, k, c * 512:(c + 1) * 512])
                                             for k in range(DC)]).then_inc(full[bank], 1)

            def shared_down(c):
                pe.wait_ge(hid_ready, (c + 1) * (SHD // P))
                for j in range(4):
                    bank = fill(FS, ("dn", c, j))
                    product(ps[:, bank, :], [(hid[:, c % 2, k, j * P:(j + 1) * P], sdT[:, k, :])
                                             for k in range(SHD // P)]).then_inc(full[bank], 1)

            shared_up(0)
            pe.wait_ge(sel_ready, 1)
            for q in range(4):
                bank = fill(FC, ("selT", q))
                for k in range(4):
                    ins = TE.transpose(ps[0:E, bank, k * P:(k + 1) * P], t2[:, 4 * q + k, :], ident[:])
                ins.then_inc(full[bank], 1)
            shared_up(1)
            shared_down(0)
            shared_up(2)
            shared_down(1)
            shared_up(3)
            shared_down(2)
            pe.wait_ge(idxf_ready, 1)
            bank = fill(FC, ("idxT",))
            TE.transpose(ps[:, bank, 0:E], idxf, ident[0:E, 0:E]).then_inc(full[bank], 1)
            shared_down(3)

            def tokens_T(s, i):
                pe.wait_ge(xg_loaded[s], i * 16 + 16)
                bank = fill(FE, ("xgT", s), i)
                for c in range(DC):
                    ins = TE.transpose(ps[:, bank, c * P:(c + 1) * P], xg[:, s, c * P:(c + 1) * P], ident[:])
                ins.then_inc(full[bank], 1)

            def hidden(s, i):
                pe.wait_ge(empt[FE.bank(("xgT", s))], FE.drained(("xgT", s), i))
                pe.wait_ge(wexp_loaded[s], i * 16 + 16)
                bank = fill(FE, ("h", s), i)
                for j in range(2):
                    ins = product(ps[:, bank, j * P:(j + 1) * P],
                                  [(wring[:, s, c * I + j * P:c * I + (j + 1) * P], xgT[:, s % 2, c, :])
                                   for c in range(DC)])
                ins.then_inc(full[bank], 1)

            def outputs(s, i):
                pe.wait_ge(hsq_ready, i * 4 + (s + 2))
                pe.wait_ge(y_ready[s % 2], i * 2 + (s // 2 + 1))
                product(ps[:, 4 + s % 2, :], [(hsq[:, s % 2, j, :], wring[:, s, DC * I + j * D:DC * I + (j + 1) * D])
                                              for j in range(2)]).then_inc(y_filled[s], 1)

            for k in (4, 5):
                pe.wait_ge(empt[k], FS.all_drained(k))
            tokens_T(0, 0)
            tokens_T(1, 0)
            hidden(0, 0)
            with pe.Fori(0, E // 4 - 1) as i:
                for s in range(4):
                    tokens_T((s + 2) % 4, i + (s + 2) // 4)
                    hidden((s + 1) % 4, i + (s + 1) // 4)
                    outputs(s, i)
            last = E // 4 - 1
            for s in range(4):
                if s < 2:
                    tokens_T(s + 2, last)
                if s < 3:
                    hidden(s + 1, last)
                outputs(s, last)



def constants():
    f = np.float32
    half = HD // 2
    freqs = f(1.0) / f(10000.0) ** (np.arange(half, dtype=f) / f(half))
    angle = np.outer(np.arange(S, dtype=f), freqs).astype(f)
    sin, cos = np.sin(angle), np.cos(angle)
    cos2 = np.concatenate([cos, cos], 1)
    sin2 = np.concatenate([-sin, sin], 1)
    pos = np.stack([64 + np.arange(P) % 64, 128 + np.arange(P)])
    rope = np.stack([cos2[pos], sin2[pos]], 1).transpose(2, 0, 1, 3).astype(f)
    slopes = np.power(f(2.0) ** f(-0.5), np.arange(1, H + 1, dtype=f)).astype(f)
    bias = np.zeros((P, KVH, QB, P), f)
    keys = [np.arange(128, 256), np.concatenate([np.arange(64, 128), np.arange(192, 256)]), np.arange(64, 192)]
    row = np.arange(P)
    for q in range(QB):
        dist = np.abs((64 * (q + 1) + row % 64)[:, None] - keys[q][None, :])
        for k in range(KVH):
            slope = slopes[2 * k + row // 64][:, None]
            bias[:, k, q] = np.where(dist > WIN // 2, -(slope * dist.astype(f)), f(NEG))
    tri = np.tile((np.arange(8)[None, :] < np.arange(8)[:, None]).astype(f).reshape(1, 64), (P, 1))
    return rope, bias, tri


def kernel(x, ctx_2048, L0_attn_Wq, L0_attn_Wkv, L0_attn_Wo, L0_attn_bo, L0_xattn_ssm_kernel, L0_xattn_D,
           L0_ffn_gate_w, L0_ffn_e_bias, L0_ffn_w1, L0_ffn_w2, L0_ffn_shared_up_w, L0_ffn_shared_down_w):
    import concourse.bacc as bacc
    from concourse.bass_utils import run_bass_kernel_spmd

    C = np.ascontiguousarray
    rope, bias, tri = constants()
    chunked = lambda w: C(np.asarray(w).reshape(w.shape[0] // P, P, w.shape[1]).transpose(1, 0, 2))
    wq = np.asarray(L0_attn_Wq).reshape(D, 2, 4, 2, HD).transpose(0, 1, 3, 2, 4).reshape(D, D)
    wo = np.asarray(L0_attn_Wo).reshape(2, 4, 2, HD, D).transpose(0, 2, 1, 3, 4).reshape(D, D)
    ctx = np.asarray(ctx_2048).reshape(B, SH, SD, DC, P)[..., ::-1]
    ctx = np.concatenate([ctx, ctx[:, :, :4]], 2).transpose(1, 4, 3, 0, 2)
    w1 = np.asarray(L0_ffn_w1).transpose(0, 2, 1).reshape(E, DC, P, I).transpose(0, 2, 1, 3).reshape(E, P, DC * I)
    w2 = np.asarray(L0_ffn_w2).transpose(0, 2, 1).reshape(E, 2, P, D).transpose(0, 2, 1, 3).reshape(E, P, 2 * D)
    arrays = {
        "x": C(np.asarray(x).reshape(T, D)),
        "wq": chunked(wq), "wkv": chunked(np.asarray(L0_attn_Wkv)), "wo": chunked(wo),
        "bo": C(np.broadcast_to(np.asarray(L0_attn_bo), (P, D))),
        "rope": C(rope), "bias": C(bias), "tri": C(tri),
        "kern": C(np.asarray(L0_xattn_ssm_kernel)), "skip": C(np.asarray(L0_xattn_D).reshape(SH, 1)),
        "ctxE": C(ctx.reshape(SH * P, DC * B * 12)),
        "suT": chunked(np.asarray(L0_ffn_shared_up_w).T), "sdT": chunked(np.asarray(L0_ffn_shared_down_w).T),
        "gwT": chunked(np.asarray(L0_ffn_gate_w).T),
        "ebias": C(np.broadcast_to(np.asarray(L0_ffn_e_bias), (P, E))),
        "wexp": C(np.concatenate([w1, w2], 2).reshape(E * P, 2048)),
    }
    nc = bacc.Bacc("TRN2", target_bir_lowering=False, num_devices=1)
    aps = {n: nc.dram_tensor(n, v.shape, mybir.dt.from_np(v.dtype), kind="ExternalInput").ap()
           for n, v in arrays.items()}
    out = nc.dram_tensor("out", (T, D), mybir.dt.float32, kind="ExternalOutput").ap()
    program(nc, aps, out)
    r = run_bass_kernel_spmd(nc, [arrays], core_ids=[0])
    return r.results[0]["out"].reshape(B, S, D)
```

```python
import numpy as np
from contextlib import ExitStack

import concourse.bass as bass
from concourse import mybir

P = 128
B, S, D = 8, 256, 512
T = B * S
NT = T // P
DC = D // P
H, KVH, HD = 16, 8, 32
NEG = -1e9
WIN, GLOB = 128, 64
PAIRS = B // 2
QB = 3
SH, SD = 32, 8
NPAIR = 36
E, K, NG, TKG, CAP, I = 64, 6, 8, 4, 128, 256
SHD = 1024
ROWS = T + P
XW = D + E
EPS = 1e-5
NBANK = 8


class Fills:

    def __init__(self, before, names, times=1):
        self.before, self.at, per = list(before), {}, [0] * NBANK
        for name, bank in names:
            assert name not in self.at, name
            self.at[name] = (bank, per[bank])
            per[bank] += 1
        self.per = per
        self.after = [a + times * b for a, b in zip(before, per)]

    def bank(self, name):
        return self.at[name][0]

    def free(self, name, i=0):
        bank, n = self.at[name]
        return (self.before[bank] + n + 1) + i * self.per[bank]

    def drained(self, name, i=0):
        return self.free(name, i) + 1

    def all_drained(self, bank):
        return self.after[bank] + 1

    def filled(self, name, i=0):
        bank, n = self.at[name]
        return (self.before[bank] + n + 1) + i * self.per[bank]


def program(nc, a, out):
    f32, u32 = mybir.dt.float32, mybir.dt.uint32
    ALU, ACT, AX = mybir.AluOpType, mybir.ActivationFunctionType, mybir.AxisListType
    V, G, A, TE = nc.vector, nc.gpsimd, nc.scalar, nc.tensor
    ds = bass.ds

    toep = nc.dram_tensor("toeplitz_rows", (SH, P + D), f32, kind="Internal").ap()
    xrows = nc.dram_tensor("token_rows", (ROWS, XW), f32, kind="Internal").ap()
    acc = [nc.dram_tensor(f"routed_sum{k}", (ROWS, D), f32, kind="Internal").ap() for k in range(2)]

    ctx = ExitStack()
    with ctx:
        def sb(name, shape, dt=f32):
            return ctx.enter_context(nc.sbuf_tensor(name, shape, dt))

        def sem(name):
            return ctx.enter_context(nc.semaphore(name))

        X = sb("residual", [P, NT, D])
        QT2 = sb("features_T", [P, DC, T])
        x3T = QT2
        ident = sb("ident", [P, P])
        stats1 = sb("stats1", [P, 4, 6])
        meanvar1 = sb("meanvar1", [P, 4, 2])
        rstd1 = sb("rstd1", [P, 4])
        stats = sb("stats", [P, NT, 6])
        meanvar = sb("meanvar", [P, NT, 2])
        rstd = sb("rstd", [P, NT])
        minus_half = sb("minus_half", [P, NT])
        eps = sb("eps", [P, NT])
        zeros = sb("zeros", [P, D])
        kpad = sb("padded_kernels", [SH, P + D])
        dcol = sb("skip_gain", [SH, 1])
        idxU = sb("slot_rows_u32", [P, E + 8], u32)
        idxg = sb("gather_rows", [P, 8], u32)
        idxs = sb("scatter_rows", [P, 2], u32)
        AREA = 34400
        arena = sb("arena", [P, AREA])
        place = [0]

        def carve(shape, at=None, rows=P):
            n = int(np.prod(shape))
            if at is not None:
                place[0] = at
            v = arena[0:rows, place[0]:place[0] + n]
            place[0] += n
            assert place[0] <= AREA, place[0]
            if len(shape) > 1:
                names = "abcde"[:len(shape)]
                v = v.rearrange(f"p ({' '.join(names)}) -> p {' '.join(names)}",
                                **{c: s for c, s in zip(names, shape)})
            return v

        wq = carve([DC, D], at=0)
        wkv = carve([DC, D])
        wo = carve([DC, D])
        bo = carve([D])
        rope = carve([2, 2, HD])
        bias = carve([KVH, QB, P])
        xln = carve([4, D])
        xl2 = xln
        xlnT = carve([DC, 4, P])
        qs = carve([3, D])
        qr = carve([3, D])
        ks = carve([3, D // 2])
        kr = carve([3, D // 2])
        qT = carve([3, 2, 4, 64])
        vlo = carve([2, D // 2])
        vkey = carve([2, QB, D // 2])
        prob = carve([2, KVH, QB, P])
        pT = carve([KVH, QB, P])
        negmax = carve([2, KVH, QB])
        rowsum = carve([2, KVH, QB])
        rinv = carve([2, KVH, QB])
        osb = carve([QB, D // 2])
        oT = carve([4, S])
        inv_s = carve([64])
        asum = carve([4])
        edec = carve([4])
        cgate = carve([3])
        spare = QT2[:].rearrange("p c t -> p (c t)")
        kbd = spare[:, 0:3072].rearrange("p (b c g t) -> p b c g t", b=2, c=2, g=4)
        tq = spare[:, 3072:3072 + 3 * D].rearrange("p (m d) -> p m d", m=3)
        tk = spare[:, 3072 + 3 * D:3072 + 9 * D // 2].rearrange("p (m d) -> p m d", m=3)
        NTR = 4
        O2 = carve([DC, B, S], at=0)
        tring = carve([NTR, D])
        cring = carve([NTR, DC * B, 12])
        kvb = carve([NTR, DC * B, NPAIR])
        qx = carve([NTR, DC * B, 12])
        prodb = carve([2, DC * B, 8, 8])
        halfsum = carve([2, 2 * B, 8, 4])
        assert place[0] <= 25088
        NW = 4
        wring = carve([NW, 2048], at=16896)
        suT = carve([DC, SHD])
        sdT = carve([SHD // P, D])
        gwT = carve([DC, E])
        ebias = carve([E])
        tri = carve([64])
        x3 = carve([2, D], at=8192)
        W = carve([NT, E])
        t1 = carve([NT, E])
        t2 = carve([NT, E])
        t3 = carve([NT, E])
        t4 = carve([NT, E])
        t5 = carve([NT, E])
        g1 = carve([NT, 8])
        g2 = carve([NT, 8])
        m8 = carve([NT, 8])
        cnt = carve([NT])
        assert place[0] <= 16896, place[0]
        rev = carve([T], at=12288, rows=E)
        key = carve([T], rows=E)
        kvals = carve([P], rows=E)
        empty = carve([P], rows=E)
        idxf = carve([P], rows=E)
        slotno = carve([P], rows=E)
        hid = carve([2, SHD // P, D], at=0)
        UE = 8
        xg = carve([UE, XW], at=8192)
        xgT = carve([2, DC, P])
        hrel = carve([2, 2, P])
        hsq = carve([2, 2, P])
        ysb = carve([2, D])
        FG = 2
        fin = carve([2, 2, FG, D], at=0)
        ps = ctx.enter_context(nc.psum_tensor("ps", [P, NBANK, 512], f32))

        full = [sem(f"bank{k}_filled") for k in range(NBANK)]
        empt = [sem(f"bank{k}_drained") for k in range(NBANK)]
        w_loaded = sem("attention_weights_loaded")
        x_loaded = sem("x_loaded")
        consts_ready = sem("consts_ready")
        small_loaded = sem("small_loaded")
        pad_ready = sem("padded_kernels_ready")
        toep_written = sem("toeplitz_written")
        zero_written = sem("zero_rows_written")
        stats_ready = sem("ln1_stats_ready")
        rstd_ready = sem("ln1_rstd_ready")
        xln_ready = sem("xln_ready")
        bo_added = sem("bo_added")
        asum_ready = sem("asum_ready")
        edec_ready = sem("edec_ready")
        cgate_ready = sem("cgate_ready")
        tq_ready = sem("rope_cos_part_ready")
        rope_ready = sem("rope_ready")
        max_ready = sem("row_max_ready")
        prob_ready = sem("prob_ready")
        stats2_ready = sem("ln2_stats_ready")
        rstd2_ready = sem("ln2_rstd_ready")
        xl2_ready = sem("xl2_ready")
        head_loaded = [sem(f"head_slot{k}_loaded") for k in range(NTR)]
        kv_ready = sem("kv_products_ready")
        qx_ready = sem("q_cyclic_ready")
        ffnw_loaded = sem("ffn_weights_loaded")
        conv_filled = [sem(f"head_slot{k}_multiplied") for k in range(NTR)]
        conv_used = [sem(f"head_slot{k}_products_taken") for k in range(NTR)]
        half_ready = sem("head_half_sums_ready")
        conv_done = sem("heads_convolved")
        stats3_ready = sem("ln3_stats_ready")
        rstd3_ready = sem("ln3_rstd_ready")
        x3_ready = [sem(f"x3_slot{k}_ready") for k in range(2)]
        x3_written = [sem(f"x3_slot{k}_written") for k in range(2)]
        score_ready = sem("exp_logits_ready")
        sel_ready = sem("selection_ready")
        rev_ready = sem("token_keys_ready")
        gates_ready = sem("gates_ready")
        gates_written = sem("gates_written")
        idxf_ready = sem("slot_tokens_ready")
        idx_ready = sem("slot_rows_ready")
        hid_ready = sem("shared_hidden_ready")
        wexp_loaded = [sem(f"expert_weights_slot{k}_loaded") for k in range(NW)]
        xg_loaded = [sem(f"gathered_slot{k}_loaded") for k in range(UE)]
        hsq_ready = sem("expert_hidden_ready")
        y_filled = [sem(f"expert_out_slot{k}_filled") for k in range(UE)]
        y_ready = [sem(f"expert_rows{k}_ready") for k in range(2)]
        y_added = [sem(f"expert_rows{k}_added") for k in range(2)]
        scatter_landed = sem("scatter_landed")
        scatters_begun = sem("scatters_begun")
        fin_loaded = [sem(f"routed_slot{k}_loaded") for k in range(2)]
        fin_ready = sem("result_ready")
        out_written = sem("out_written")

        names = []
        turn = [0]

        def rot(*fills):
            for f in fills:
                names.append((f, turn[0] % NBANK))
                turn[0] += 1

        def scores(b, c):
            rot(*[("s", b, c, q) for q in range(QB)])

        rot(*[("xT", u) for u in range(4)])
        rot(("q", 0), ("kmix",), ("q", 1), ("kv", 0), ("q", 2), ("kv", 1), ("vlo",))
        rot(*[(f, m) for m in range(3) for f in ("kT", "qT")])
        scores(0, 0)
        scores(0, 1)
        rot(*[("pT", 0, 0, q) for q in range(QB)])
        scores(1, 0)
        rot(*[("pT", 0, 1, q) for q in range(QB)])
        scores(1, 1)
        rot(*[("pv", 0, q) for q in range(QB)])
        rot(*[("pT", 1, 0, q) for q in range(QB)])
        rot(("mean", 0), *[("oT", 0, c) for c in range(2)])
        rot(*[("pT", 1, 1, q) for q in range(QB)])
        rot(*[("wo", 0, h) for h in range(2)])
        rot(*[("pv", 1, q) for q in range(QB)])
        rot(("mean", 1), *[("oT", 1, c) for c in range(2)])
        rot(*[("wo", 1, h) for h in range(2)])
        ORDER_A = [x for x, _ in names]
        FA = Fills([0] * NBANK, names, PAIRS)
        FQ = Fills(FA.after, [(("x2T", t), 4 + t % 4) for t in range(NT)])
        names = [(("o", t), t % 4) for t in range(NT)] + [(("x3T", t), t % 2) for t in range(NT)]
        names += [(("logit", 0), 2), (("logit", 1), 3)]
        names += [(("selT", q), 4 + q) for q in range(4)] + [(("idxT",), 7)]
        FC = Fills(FQ.after, names)
        names = []
        for c in range(4):
            names += [(("up", c, j), j % 4) for j in range(SHD // P)]
            names += [(("dn", c, j), 4 + j % 2) for j in range(4)]
        FS = Fills(FC.after, names)
        FE = Fills(FS.after, [(("xgT", s), s % 2) for s in range(UE)] + [(("h", s), 2 + s % 2) for s in range(UE)],
                   E // UE)

        block = ctx.enter_context(nc.Block())

        @block.sync
        def _(sp):
            for s in (*empt, *conv_used, *conv_filled, *y_filled, *y_ready, hsq_ready):
                sp.sem_inc(s, 1)
            sp.sem_inc(scatter_landed, 2)
            sp.sem_inc(conv_done, 2)
            sp.sem_inc(x_loaded, 16)
            with sp.Fori(0, 4) as i:
                sp.wait_ge(x_loaded, i * 16 + 16)
                sp.dma_start(X[:, ds(i * 4, 4), :],
                             a["x"][ds(i * (4 * P), 4 * P), :].rearrange("(t p) d -> p t d", p=P)).then_inc(x_loaded, 16)
            sp.wait_ge(w_loaded, 16 * 6)
            sp.wait_ge(consts_ready, 1)
            for t in range(ROWS // P):
                for k in range(2):
                    sp.dma_start(acc[k][t * P:(t + 1) * P, :], zeros[:]).then_inc(zero_written, 16)
            sp.dma_start(xrows[T:ROWS, 0:D], zeros[:]).then_inc(zero_written, 16)
            sp.dma_start(xrows[T:ROWS, D:XW], zeros[:, 0:E]).then_inc(zero_written, 16)
            sp.wait_ge(xl2_ready, NT)
            for k in range(4, 8):
                sp.wait_ge(empt[k], FQ.all_drained(k))
            sp.wait_ge(toep_written, 16)
            toep_v = bass.AP(toep.tensor, 1, [[P + D, SH], [1, P], [1, D]])
            with sp.Fori(0, SH // NTR) as i:
                for s in range(NTR):
                    sp.wait_ge(conv_filled[s], i + 1)
                    sp.wait_ge(toep_written, 16)
                    sp.dma_start(tring[:, s:s + 1, :], toep_v[ds(i * NTR + s, 1), :, :].rearrange("h p d -> p h d"))\
                      .then_inc(head_loaded[s], 16)
                    sp.dma_start(cring[:, s, :, :].rearrange("p m i -> p (m i)"),
                                 a["ctxE"][ds((i * NTR + s) * P, P), :]).then_inc(head_loaded[s], 16)
            for t in range(NT):
                sp.wait_ge(x3_ready[t % 2], t // 2 + 1)
                sp.dma_start(xrows[t * P:(t + 1) * P, 0:D], x3[:, t % 2, :]).then_inc(x3_written[t % 2], 16)
            sp.wait_ge(gates_ready, 1)
            sp.dma_start(xrows[0:T, D:XW].rearrange("(t p) c -> p t c", p=P), W).then_inc(gates_written, 16)
            with sp.Fori(0, E // UE) as i:
                for s in range(UE):
                    sp.wait_ge(y_filled[(s - NW) % UE], i + (s // NW + 1))
                    sp.wait_ge(gates_ready, 1)
                    sp.dma_start(wring[:, s % NW, :], a["wexp"][ds((i * UE + s) * P, P), :])\
                      .then_inc(wexp_loaded[s % NW], 16)
            for k in range(2):
                sp.wait_ge(y_added[k], 16 * E // 2)
            acc_v = [x[0:T, :].rearrange("(t p) d -> p t d", p=P) for x in acc]
            out_v = out.rearrange("(t p) d -> p t d", p=P)
            n = NT // FG
            for g in range(n + 1):
                if g < n:
                    if g >= 2:
                        sp.wait_ge(fin_ready, g - 1)
                    for k in range(2):
                        sp.dma_start(fin[:, g % 2, k], acc_v[k][:, FG * g:FG * g + FG, :])\
                          .then_inc(fin_loaded[g % 2], 16)
                if g >= 1:
                    sp.wait_ge(fin_ready, g)
                    sp.dma_start(out_v[:, FG * (g - 1):FG * g, :], X[:, FG * (g - 1):FG * g, :])\
                      .then_inc(out_written, 16)
            sp.wait_ge(out_written, 16 * n)

        @block.gpsimd
        def _(pool):
            G.memset(ident[:], 0.0)
            G.memset(minus_half[:], -0.5)
            G.memset(eps[:], EPS)
            G.memset(zeros[:], 0.0)
            G.memset(kpad[:, 0:P], 0.0)
            G.memset(inv_s, 1.0 / S)
            G.memset(kbd, 0.0)
            G.drain()
            G.affine_select(out=ident[:], in_=ident[:], compare_op=ALU.not_equal, fill=1.0, base=0,
                            pattern=[[-1, P]], channel_multiplier=1).then_inc(consts_ready, 1)
            pool.wait_ge(small_loaded, 32)
            G.tensor_tensor(kpad[:, P:P + 1], kpad[:, P:P + 1], dcol[:], ALU.add).then_inc(pad_ready, 1)
            pool.wait_ge(w_loaded, 16 * 6)

            def ln1_rstd(i):
                pool.wait_ge(stats_ready, i + 1)
                G.tensor_tensor(rstd1[:], meanvar1[:, :, 1], eps[:, 0:4], ALU.add)
                G.drain()
                G.tensor_tensor(rstd1[:], rstd1[:], minus_half[:, 0:4], ALU.pow).then_inc(rstd_ready, 1)

            def attention(i, more):
                pool.wait_ge(xln_ready, i * 4 + 4)
                G.tensor_tensor(X[:, ds(i * 4, 4), :], X[:, ds(i * 4, 4), :],
                                bo.unsqueeze(1).broadcast_to((P, 4, D)), ALU.add).then_inc(bo_added, 1)
                for m in range(3):
                    cos = rope[:, min(m, 1), 0, :]
                    kfill = ("kmix",) if m == 0 else ("kv", m - 1)
                    pool.wait_ge(empt[FA.bank(kfill)], FA.drained(kfill, i))
                    pool.wait_ge(empt[FA.bank(("q", m))], FA.drained(("q", m), i))
                    G.tensor_tensor(tk[:, m, :].rearrange("p (h d) -> p h d", d=HD),
                                    ks[:, m, :].rearrange("p (h d) -> p h d", d=HD),
                                    cos.unsqueeze(1).broadcast_to((P, KVH, HD)), ALU.mult)
                    G.tensor_tensor(tq[:, m, :].rearrange("p (h d) -> p h d", d=HD),
                                    qs[:, m, :].rearrange("p (h d) -> p h d", d=HD),
                                    cos.unsqueeze(1).broadcast_to((P, H, HD)), ALU.mult).then_inc(tq_ready, 1)
                if more:
                    ln1_rstd(i + 1)

            ln1_rstd(0)
            with pool.Fori(0, PAIRS - 1) as i:
                attention(i, True)
            attention(PAIRS - 1, False)
            pool.wait_ge(stats2_ready, 1)
            G.tensor_tensor(rstd[:], meanvar[:, :, 1], eps[:], ALU.add)
            G.drain()
            G.tensor_tensor(rstd[:], rstd[:], minus_half[:], ALU.pow).then_inc(rstd2_ready, 1)

            def pair_products(s, i):
                pool.wait_ge(head_loaded[s], i * 32 + 32)
                pool.wait_ge(conv_filled[s], i + 1)
                c = cring[:, s, :, :]
                G.tensor_tensor(kvb[:, s, :, 0:32].rearrange("p m (d i) -> p m d i", d=4),
                                c[:, :, 0:SD].unsqueeze(2).broadcast_to((P, DC * B, 4, SD)),
                                bass.AP(c.tensor, c.offset, [list(c.ap[0]), [12, DC * B], [1, 4], [1, SD]]),
                                ALU.mult)
                G.tensor_tensor(kvb[:, s, :, 32:36], c[:, :, 0:4], c[:, :, 4:8], ALU.mult).then_inc(kv_ready, 1)

            def half_sums(s, i):
                pool.wait_ge(conv_used[s], i + 2)
                pv = prodb[:, s % 2, 2 * B:, :, :].rearrange("p m j k -> p (m j) k")
                G.tensor_tensor(halfsum[:, s % 2].rearrange("p m j k -> p (m j) k"), pv[:, :, 0:4], pv[:, :, 4:8],
                                ALU.add).then_inc(half_ready, 1)

            pair_products(0, 0)
            pair_products(1, 0)
            last = SH // NTR - 1
            with pool.Fori(0, last) as i:
                for s in range(NTR):
                    pair_products((s + 2) % NTR, i + (s + 2) // NTR)
                    half_sums(s, i)
            for s in range(NTR):
                if s < NTR - 2:
                    pair_products(s + 2, last)
                half_sums(s, last)
            pool.wait_ge(stats3_ready, 1)
            G.tensor_tensor(rstd[:], meanvar[:, :, 1], eps[:], ALU.add)
            G.drain()
            G.tensor_tensor(rstd[:], rstd[:], minus_half[:], ALU.pow).then_inc(rstd3_ready, 1)
            pool.wait_ge(sel_ready, 1)
            G.iota(rev, [[-1, T]], base=T, channel_multiplier=0, allow_small_or_imprecise_dtypes=True)
            G.iota(slotno, [[1, P]], base=0, channel_multiplier=0, allow_small_or_imprecise_dtypes=True)\
             .then_inc(rev_ready, 1)
            for c in range(4):
                for j in range(SHD // P):
                    pool.wait_ge(empt[FS.bank(("up", c, j))], FS.drained(("up", c, j)))
                    G.tensor_tensor(hid[:, c % 2, j, :], hid[:, c % 2, j, :], hid[:, c % 2, j, :], ALU.mult)\
                     .then_inc(hid_ready, 1)
            for k in range(2):
                pool.wait_ge(x3_written[k], 16 * (NT // 2))
            pool.wait_ge(gates_written, 16)
            pool.wait_ge(zero_written, 16 * (2 * (ROWS // P) + 2))

            pool.wait_ge(idx_ready, 1)

            def gather(s):
                pool.indirect_dma_start(xg[:, s, :], None, xrows, bass.IndirectOffsetOnAxis(ap=idxg[:, s:s + 1], axis=0))\
                    .then_inc(xg_loaded[s], 16)

            def scatter(s, i):
                pool.wait_ge(y_ready[s % 2], i * (UE // 2) + (s // 2 + 2))
                pool.sem_inc(scatters_begun, 1)
                pool.indirect_dma_start(acc[s % 2], bass.IndirectOffsetOnAxis(ap=idxs[:, s % 2:s % 2 + 1], axis=0),
                                        ysb[:, s % 2, :], None, compute_op=ALU.add).then_inc(y_added[s % 2], 16)

            def landed(s, i):
                pool.wait_ge(y_added[s % 2], i * (8 * UE) + (16 * (s // 2) + 16))
                pool.sem_inc(scatter_landed, 1)

            last = E // UE - 1
            for s in range(UE):
                gather(s)
            scatter(0, 0)
            with pool.Fori(0, last) as i:
                for s in range(UE):
                    scatter((s + 1) % UE, i + (s + 1) // UE)
                    gather(s)
                    landed(s, i)
            for s in range(UE):
                if s < UE - 1:
                    scatter(s + 1, last)
                landed(s, last)

        @block.scalar
        def _(act):
            def load(dst, name, s):
                act.dma_start(dst, a[name]).then_inc(s, 16)
            load(wq, "wq", w_loaded)
            load(kpad[:, P:], "kern", small_loaded)
            load(dcol[:], "skip", small_loaded)
            load(wkv, "wkv", w_loaded)
            load(rope, "rope", w_loaded)
            load(bias, "bias", w_loaded)
            load(bo, "bo", w_loaded)
            load(wo, "wo", w_loaded)
            act.wait_ge(pad_ready, 1)
            act.dma_start(toep[:], kpad[:]).then_inc(toep_written, 16)

            def evacuate(fills, name, i, dst, src, scale=None):
                bank = fills.bank(name)
                act.wait_ge(full[bank], fills.filled(name, i))
                kw = {} if scale is None else {"scale": scale}
                A.activation(dst, src, ACT.Copy, **kw).then_inc(empt[bank], 1)

            def quad(bank, rows=P):
                return ps[0:rows, bank, :].rearrange("p (c t) -> p c t", c=4)

            def exps(b, c, i):
                for q in range(QB):
                    act.wait_ge(max_ready, i * 12 + ((2 * b + c) * QB + q + 1))
                    for k in range(4 * c, 4 * c + 4):
                        ins = A.activation(prob[:, b, k, q, :], prob[:, b, k, q, :], ACT.Exp,
                                           bias=negmax[:, b, k, q:q + 1], scale=1.0,
                                           accum_out=rowsum[:, b, k, q:q + 1])
                    ins.then_inc(prob_ready, 1)

            def probs_T(b, c, q, i):
                name = ("pT", b, c, q)
                evacuate(FA, name, i, pT[:, 4 * c:4 * c + 4, q, :], quad(FA.bank(name)))

            def attended_T(b, i):
                for c in range(2):
                    name = ("oT", b, c)
                    evacuate(FA, name, i,
                             oT[:, 2 * c:2 * c + 2, 64:S].rearrange("p r (q t) -> p q r t", q=QB),
                             ps[:, FA.bank(name), 0:3 * P].rearrange("p (q r t) -> p q r t", q=QB, r=2))

            def gate_exps(i):
                act.wait_ge(asum_ready, i + 1)
                A.activation(edec, asum, ACT.Exp, scale=-1.0).then_inc(edec_ready, 1)

            def attention(i, more):
                for u in range(4):
                    name = ("xT", u)
                    src = quad(FA.bank(name))
                    if u == 2:
                        act.wait_ge(full[FA.bank(name)], FA.filled(name, i))
                        A.activation(xlnT[:, :, 1, 64:P], src[:, :, 0:64], ACT.Copy)
                        A.activation(xlnT[:, :, 1, 0:64], src[:, :, 64:P], ACT.Copy).then_inc(empt[FA.bank(name)], 1)
                    else:
                        evacuate(FA, name, i, xlnT[:, :, {0: 0, 1: 2, 3: 3}[u], :], src)
                act.wait_ge(cgate_ready, i + 1)
                for m in range(3):
                    evacuate(FA, ("q", m), i, qs[:, m, :], ps[:, FA.bank(("q", m)), :], scale=cgate[:, m:m + 1])
                    if m == 0:
                        evacuate(FA, ("kmix",), i, ks[:, 0, :], ps[:, FA.bank(("kmix",)), 0:D // 2])
                for m in range(3):
                    if m == 0:
                        bank = FA.bank(("kT", 0))
                        act.wait_ge(full[bank], FA.filled(("kT", 0), i))
                        for g in range(4):
                            rows = slice(32 * g, 32 * g + 32)
                            ins = A.activation(kbd[rows, :, :, g, 0:64],
                                               ps[rows, bank, 0:2 * P].rearrange("p (c b t) -> p b c t", c=2, b=2),
                                               ACT.Copy)
                        ins.then_inc(empt[bank], 1)
                    evacuate(FA, ("qT", m), i, qT[:, m, :, :, :].rearrange("p n k t -> p k n t"),
                             quad(FA.bank(("qT", m))).rearrange("p k (n t) -> p k n t", n=2))
                exps(0, 0, i)
                exps(0, 1, i)
                probs_T(0, 0, 0, i)
                probs_T(0, 0, 2, i)
                exps(1, 0, i)
                probs_T(0, 1, 0, i)
                probs_T(0, 1, 2, i)
                exps(1, 1, i)
                if more:
                    gate_exps(i + 1)
                probs_T(1, 0, 0, i)
                probs_T(1, 0, 2, i)
                attended_T(0, i)
                probs_T(1, 1, 0, i)
                probs_T(1, 1, 2, i)
                attended_T(1, i)

            gate_exps(0)
            with act.Fori(0, PAIRS - 1) as i:
                attention(i, True)
            attention(PAIRS - 1, False)
            for t in range(NT):
                name = ("x2T", t)
                evacuate(FQ, name, 0, QT2[:, :, t * P:(t + 1) * P], quad(FQ.bank(name)))
            load(suT, "suT", ffnw_loaded)
            load(sdT, "sdT", ffnw_loaded)
            load(gwT, "gwT", ffnw_loaded)
            load(ebias, "ebias", ffnw_loaded)
            load(tri, "tri", ffnw_loaded)
            A.drain()
            qv = QT2[:].rearrange("p l (b s) -> p (l b) s", b=B)
            with act.Fori(0, SH // NTR) as i:
                for s in range(NTR):
                    h = i * NTR + s
                    act.wait_ge(conv_used[s], i + 1)
                    A.activation(qx[:, s, :, 0:SD], qv[:, :, ds(h * SD, SD)], ACT.Copy)
                    A.activation(qx[:, s, :, SD:12], qv[:, :, ds(h * SD, 4)], ACT.Copy).then_inc(qx_ready, 1)
            for t in range(NT):
                name = ("x3T", t)
                evacuate(FC, name, 0, x3T[:, :, t * P:(t + 1) * P], quad(FC.bank(name)))
            for k in range(2):
                act.wait_ge(full[2 + k], FC.filled(("logit", k)))
                A.activation(t1[:, 8 * k:8 * k + 8, :], ps[:, 2 + k, :].rearrange("p (t e) -> p t e", e=E),
                             ACT.Exp, scale=-1.0).then_inc(empt[2 + k], 1)
            for c in range(4):
                for j in range(SHD // P):
                    bank = FS.bank(("up", c, j))
                    if c >= 2 and j == 0:
                        act.wait_ge(full[FS.bank(("dn", c - 2, 3))], FS.filled(("dn", c - 2, 3)))
                    act.wait_ge(full[bank], FS.filled(("up", c, j)))
                    A.activation(hid[:, c % 2, j, :], ps[:, bank, :], ACT.Relu).then_inc(empt[bank], 1)
            with act.Fori(0, E // UE) as i:
                for s in range(UE):
                    evacuate(FE, ("xgT", s), i, xgT[:, s % 2, :, :], quad(FE.bank(("xgT", s))))
                    bank = FE.bank(("h", s))
                    act.wait_ge(full[bank], FE.filled(("h", s), i))
                    act.wait_ge(hsq_ready, i * UE + max(s, 1))
                    A.activation(hrel[:, s % 2, :, :].rearrange("p c t -> p (c t)"), ps[:, bank, 0:2 * P], ACT.Relu)\
                     .then_inc(empt[bank], 1)

        @block.vector
        def _(dve):
            def heads(v):
                return v.rearrange("p (h d) -> p h d", d=HD)

            def scores_out(b, c, i):
                for q in range(QB + 1):
                    if q < QB:
                        bank = FA.bank(("s", b, c, q))
                        dve.wait_ge(full[bank], FA.filled(("s", b, c, q), i))
                        V.scalar_tensor_tensor(prob[:, b, 4 * c:4 * c + 4, q, :],
                                               ps[:, bank, :].rearrange("p (g t) -> p g t", g=4),
                                               1.0 / np.sqrt(HD).astype(np.float32).item(),
                                               bias[:, 4 * c:4 * c + 4, q, :],
                                               op0=ALU.mult, op1=ALU.add).then_inc(empt[bank], 1)
                    if q:
                        dve.wait_ge(empt[FA.bank(("s", b, c, q - 1))], FA.drained(("s", b, c, q - 1), i))
                        V.tensor_reduce(negmax[:, b, 4 * c:4 * c + 4, q - 1], prob[:, b, 4 * c:4 * c + 4, q - 1, :],
                                        axis=AX.X, op=ALU.max, negate=True).then_inc(max_ready, 1)

            def probs_T(b, c, i):
                name = ("pT", b, c, 1)
                bank = FA.bank(name)
                dve.wait_ge(full[bank], FA.filled(name, i))
                V.tensor_copy(pT[:, 4 * c:4 * c + 4, 1, :], ps[:, bank, :].rearrange("p (g t) -> p g t", g=4))\
                 .then_inc(empt[bank], 1)

            def inverse_sums(b, i):
                dve.wait_ge(prob_ready, i * 12 + (2 * b + 2) * QB)
                V.reciprocal(rinv[:, b, :, :], rowsum[:, b, :, :])
                V.drain()

            def attended(b, i):
                for q in range(QB):
                    bank = FA.bank(("pv", b, q))
                    dve.wait_ge(full[bank], FA.filled(("pv", b, q), i))
                    V.tensor_tensor(heads(osb[:, q, :]), heads(ps[:, bank, 0:D // 2]),
                                    rinv[:, b, :, q:q + 1].broadcast_to((P, KVH, HD)), ALU.mult)\
                     .then_inc(empt[bank], 1)

            def mean_rows(b, i):
                bank = FA.bank(("mean", b))
                dve.wait_ge(full[bank], FA.filled(("mean", b), i))
                V.tensor_copy(oT[:, :, 0:64].rearrange("p (c r) t -> p c r t", c=2),
                              ps[:, bank, 0:P].rearrange("p (c t) -> p c t", c=2).unsqueeze(2)
                              .broadcast_to((P, 2, 2, 64))).then_inc(empt[bank], 1)

            def project(b, i):
                for h in range(2):
                    bank = FA.bank(("wo", b, h))
                    if b == 0 and h == 0:
                        dve.wait_ge(bo_added, i + 1)
                    dve.wait_ge(full[bank], FA.filled(("wo", b, h), i))
                    xt = X[:, ds(i * 4 + (2 * b + h), 1), :].rearrange("p t d -> p (t d)")
                    V.tensor_tensor(xt, xt, ps[:, bank, :], ALU.add).then_inc(empt[bank], 1)
                V.drain()
                for h in range(2):
                    V.bn_stats(stats[:, ds(i * 4 + (2 * b + h), 1), :].rearrange("p t d -> p (t d)"),
                               X[:, ds(i * 4 + (2 * b + h), 1), :].rearrange("p t d -> p (t d)"))

            dve.wait_ge(w_loaded, 16 * 6)

            def ln1_stats(i):
                dve.wait_ge(x_loaded, i * 16 + 32)
                for u in range(4):
                    V.bn_stats(stats1[:, u, :], X[:, ds(i * 4 + u, 1), :].rearrange("p t d -> p (t d)"))
                V.drain()
                for u in range(4):
                    ins = V.bn_aggr(meanvar1[:, u, :], stats1[:, u, :])
                ins.then_inc(stats_ready, 1)

            def ln1(i):
                dve.wait_ge(rstd_ready, i + 1)
                for u in range(4):
                    V.tensor_scalar(xln[:, u, :], X[:, ds(i * 4 + u, 1), :].rearrange("p t d -> p (t d)"),
                                    meanvar1[:, u, 0:1], rstd1[:, u:u + 1], ALU.subtract, ALU.mult)\
                     .then_inc(xln_ready, 1)
                V.drain()
                V.tensor_reduce(asum, xln, axis=AX.X, op=ALU.add, apply_absolute_value=True).then_inc(asum_ready, 1)

            def query_gate(i):
                dve.wait_ge(edec_ready, i + 1)
                V.tensor_scalar(edec, edec, 1.0, None, ALU.add)
                V.drain()
                V.reciprocal(cgate[0:64, 0:1], edec[64:P, 0:1])
                V.reciprocal(cgate[64:P, 0:1], edec[64:P, 2:3])
                V.reciprocal(cgate[:, 1:2], edec[:, 1:2])
                V.reciprocal(cgate[:, 2:3], edec[:, 3:4]).then_inc(cgate_ready, 1)

            def upper_kv(b, i):
                bank = FA.bank(("kv", b))
                dve.wait_ge(full[bank], FA.filled(("kv", b), i))
                V.tensor_copy(ks[:, 1 + b, :], ps[:, bank, 0:D // 2])
                V.tensor_copy(vkey[:, b, 0, :], ps[:, bank, D // 2:D])
                V.tensor_copy(vkey[64:P, b, 1, :], ps[64:P, bank, D // 2:D])
                V.tensor_copy(vkey[64:P, b, 2, :], ps[0:64, bank, D // 2:D]).then_inc(empt[bank], 1)

            def lower_v(i):
                bank = FA.bank(("vlo",))
                dve.wait_ge(full[bank], FA.filled(("vlo",), i))
                V.tensor_copy(vlo, ps[:, bank, :].rearrange("p (b d) -> p b d", b=2))
                for b in range(2):
                    rows = slice(64, P) if b == 0 else slice(0, 64)
                    for q in (1, 2):
                        ins = V.tensor_copy(vkey[0:64, b, q, :], ps[rows, bank, b * 256:(b + 1) * 256])
                ins.then_inc(empt[bank], 1)

            def rotate(m, i):
                sin = rope[:, min(m, 1), 1, :]
                kfill = ("kmix",) if m == 0 else ("kv", m - 1)
                dve.wait_ge(empt[FA.bank(kfill)], FA.drained(kfill, i))
                dve.wait_ge(empt[FA.bank(("q", m))], FA.drained(("q", m), i))
                for src, dst, n in ((ks, kr, KVH), (qs, qr, H)):
                    for lo, hi in ((0, 16), (16, 0)):
                        V.tensor_tensor(heads(dst[:, m, :])[:, :, lo:lo + 16], heads(src[:, m, :])[:, :, hi:hi + 16],
                                        sin[:, lo:lo + 16].unsqueeze(1).broadcast_to((P, n, 16)), ALU.mult)
                V.drain()
                dve.wait_ge(tq_ready, i * 3 + m + 1)
                V.tensor_tensor(kr[:, m, :], kr[:, m, :], tk[:, m, :], ALU.add)
                V.tensor_tensor(qr[:, m, :], qr[:, m, :], tq[:, m, :], ALU.add).then_inc(rope_ready, 1)

            def upper_keys(b, i):
                name = ("kT", 1 + b)
                bank = FA.bank(name)
                dve.wait_ge(full[bank], FA.filled(name, i))
                for g in range(4):
                    rows = slice(32 * g, 32 * g + 32)
                    ins = V.tensor_copy(kbd[rows, b, :, g, 64:192],
                                        ps[rows, bank, 0:2 * P].rearrange("p (c t) -> p c t", c=2))
                ins.then_inc(empt[bank], 1)

            def attention(i, more):
                rotate(0, i)
                upper_kv(0, i)
                rotate(1, i)
                upper_kv(1, i)
                rotate(2, i)
                upper_keys(0, i)
                lower_v(i)
                upper_keys(1, i)
                scores_out(0, 0, i)
                scores_out(0, 1, i)
                probs_T(0, 0, i)
                scores_out(1, 0, i)
                if more:
                    ln1_stats(i + 1)
                probs_T(0, 1, i)
                scores_out(1, 1, i)
                if more:
                    ln1(i + 1)
                inverse_sums(0, i)
                attended(0, i)
                if more:
                    query_gate(i + 1)
                probs_T(1, 0, i)
                mean_rows(0, i)
                probs_T(1, 1, i)
                project(0, i)
                inverse_sums(1, i)
                attended(1, i)
                mean_rows(1, i)
                project(1, i)

            ln1_stats(0)
            ln1(0)
            query_gate(0)
            with dve.Fori(0, PAIRS - 1) as i:
                attention(i, True)
            attention(PAIRS - 1, False)
            V.drain()
            for t in range(NT):
                ins = V.bn_aggr(meanvar[:, t, :], stats[:, t, :])
            ins.then_inc(stats2_ready, 1)
            dve.wait_ge(rstd2_ready, 1)
            for t in range(NT):
                if t >= 4:
                    dve.wait_ge(full[FQ.bank(("x2T", t - 4))], FQ.filled(("x2T", t - 4)))
                V.tensor_scalar(xl2[:, t % 4, :], X[:, t, :], meanvar[:, t, 0:1], rstd[:, t:t + 1],
                                ALU.subtract, ALU.mult).then_inc(xl2_ready, 1)
            def head_products(s, i):
                dve.wait_ge(conv_filled[s], i + 2)
                dve.wait_ge(qx_ready, i * NTR + s + 1)
                dve.wait_ge(conv_done, i * NTR + s + 1)
                y = ps[:, 4 * (s % 2):4 * (s % 2) + DC, 0:B * NPAIR].rearrange("p l (b n) -> p l b n", n=NPAIR)
                q = qx[:, s, :, :].rearrange("p (l b) j -> p l b j", l=DC)
                pr = prodb[:, s % 2].rearrange("p (l b) j k -> p l b j k", l=DC)
                for d in range(4):
                    V.tensor_tensor(pr[:, :, :, :, d], y[:, :, :, 8 * d:8 * d + 8], q[:, :, :, d:d + 8], ALU.mult)
                    if d:
                        V.tensor_tensor(pr[:, :, :, d:8, 3 + d], y[:, :, :, 8 * d:8 * d + 8 - d],
                                        q[:, :, :, 0:8 - d], ALU.mult)
                        V.tensor_tensor(pr[:, :, :, 0:d, 3 + d], y[:, :, :, 8 * d + 8 - d:8 * d + 8],
                                        q[:, :, :, 8 - d:8], ALU.mult)
                V.tensor_tensor(pr[:, :, :, 0:4, 7], y[:, :, :, 32:36], q[:, :, :, 4:8], ALU.mult)
                V.tensor_tensor(pr[:, :, :, 4:8, 7], y[:, :, :, 32:36], q[:, :, :, 0:4], ALU.mult)\
                 .then_inc(conv_used[s], 1)

            def head_sums(s, i):
                dve.wait_ge(conv_used[s], i + 2)
                o = O2.rearrange("p l b s -> p (l b) s")[:, :, ds((i * NTR + s) * SD, SD)]
                V.tensor_reduce(o[:, 0:2 * B, :], prodb[:, s % 2, 0:2 * B], axis=AX.X, op=ALU.add)
                dve.wait_ge(half_ready, i * NTR + s + 1)
                V.tensor_reduce(o[:, 2 * B:, :], halfsum[:, s % 2], axis=AX.X, op=ALU.add).then_inc(conv_done, 1)

            head_products(0, 0)
            last = SH // NTR - 1
            with dve.Fori(0, last) as i:
                for s in range(NTR):
                    head_products((s + 1) % NTR, i + (s + 1) // NTR)
                    head_sums(s, i)
            for s in range(NTR):
                if s < NTR - 1:
                    head_products(s + 1, last)
                head_sums(s, last)
            V.drain()
            for t in range(NT):
                bank = FC.bank(("o", t))
                dve.wait_ge(full[bank], FC.filled(("o", t)))
                V.tensor_tensor(X[:, t, :], X[:, t, :], ps[:, bank, :], ALU.add).then_inc(empt[bank], 1)
                V.drain()
                V.bn_stats(stats[:, t, :], X[:, t, :])
            V.drain()
            for t in range(NT):
                ins = V.bn_aggr(meanvar[:, t, :], stats[:, t, :])
            ins.then_inc(stats3_ready, 1)
            dve.wait_ge(rstd3_ready, 1)
            for t in range(NT):
                if t >= 2:
                    dve.wait_ge(full[FC.bank(("x3T", t - 2))], FC.filled(("x3T", t - 2)))
                    dve.wait_ge(x3_written[t % 2], 16 * (t // 2))
                V.tensor_scalar(x3[:, t % 2, :], X[:, t, :], meanvar[:, t, 0:1], rstd[:, t:t + 1],
                                ALU.subtract, ALU.mult).then_inc(x3_ready[t % 2], 1)
            dve.wait_ge(ffnw_loaded, 16 * 5)
            for k in range(2):
                dve.wait_ge(empt[2 + k], FC.drained(("logit", k)))
            tile64 = (P, NT, E)
            V.tensor_scalar(t1, t1, 1.0, None, ALU.add)
            V.memset(W, 1.0)
            V.drain()
            V.reciprocal(t1, t1)
            V.memset(W[:, :, 0:1], 0.0)
            V.drain()
            V.tensor_tensor(t2, t1, ebias.unsqueeze(1).broadcast_to(tile64), ALU.add)
            V.drain()
            v = t2.rearrange("p t (g e) -> p (t g) e", e=8)
            flat3 = t3.rearrange("p t e -> p (t e)")
            flat4 = t4.rearrange("p t e -> p (t e)")
            flat5 = t5.rearrange("p t e -> p (t e)")
            NP8 = NT * NG
            hi4 = flat3[:, 0:4 * NP8].rearrange("p (n e) -> p n e", e=4)
            lo4 = flat3[:, 4 * NP8:8 * NP8].rearrange("p (n e) -> p n e", e=4)
            V.tensor_tensor(hi4, v[:, :, 0:4], v[:, :, 4:8], ALU.max)
            V.tensor_tensor(lo4, v[:, :, 0:4], v[:, :, 4:8], ALU.min)
            V.drain()
            hi2, mn2, mx2, lo2 = (flat4[:, 2 * k * NP8:2 * (k + 1) * NP8].rearrange("p (n e) -> p n e", e=2)
                                  for k in range(4))
            V.tensor_tensor(hi2, hi4[:, :, 0:2], hi4[:, :, 2:4], ALU.max)
            V.tensor_tensor(mn2, hi4[:, :, 0:2], hi4[:, :, 2:4], ALU.min)
            V.tensor_tensor(mx2, lo4[:, :, 0:2], lo4[:, :, 2:4], ALU.max)
            V.drain()
            V.tensor_tensor(lo2, mn2, mx2, ALU.max)
            V.drain()
            hi1, mn1, mx1, lo1 = (flat5[:, k * NP8:(k + 1) * NP8].rearrange("p (n e) -> p n e", e=1) for k in range(4))
            V.tensor_tensor(hi1, hi2[:, :, 0:1], hi2[:, :, 1:2], ALU.max)
            V.tensor_tensor(mn1, hi2[:, :, 0:1], hi2[:, :, 1:2], ALU.min)
            V.tensor_tensor(mx1, lo2[:, :, 0:1], lo2[:, :, 1:2], ALU.max)
            V.drain()
            V.tensor_tensor(lo1, mn1, mx1, ALU.max)
            V.drain()
            V.tensor_tensor(g1.rearrange("p t g -> p (t g)").unsqueeze(2), hi1, lo1, ALU.add)
            V.drain()
            gg = (P, NT, NG, NG)
            other = g1.unsqueeze(2).broadcast_to(gg)
            own = g1.unsqueeze(3).broadcast_to(gg)
            gt3 = t3.rearrange("p t (g h) -> p t g h", h=NG)
            eq4 = t4.rearrange("p t (g h) -> p t g h", h=NG)
            V.tensor_tensor(gt3, other, own, ALU.is_gt)
            V.tensor_tensor(eq4, other, own, ALU.is_equal)
            V.drain()
            V.tensor_tensor(t4, t4, tri.unsqueeze(1).broadcast_to(tile64), ALU.mult)
            V.drain()
            V.tensor_tensor(t3, t3, t4, ALU.add)
            V.drain()
            V.tensor_reduce(g2, gt3, axis=AX.X, op=ALU.add)
            V.drain()
            V.tensor_scalar(g2, g2, TKG - 0.5, None, ALU.is_lt)
            V.drain()
            V.tensor_scalar(g1, g2, 1e30, -1e30, ALU.mult, ALU.add)
            V.tensor_tensor(t3.rearrange("p t (g e) -> p (t g) e", e=8), v,
                            g2.rearrange("p t g -> p (t g)").unsqueeze(2).broadcast_to((P, NP8, 8)), ALU.mult)
            V.drain()
            V.tensor_tensor(t3.rearrange("p t (g e) -> p (t g) e", e=8), t3.rearrange("p t (g e) -> p (t g) e", e=8),
                            g1.rearrange("p t g -> p (t g)").unsqueeze(2).broadcast_to((P, NP8, 8)), ALU.add)
            V.drain()
            for t in range(NT):
                V.max(m8[:, t, :], t3[:, t, :])
            V.drain()
            kth = m8[:, :, K - 1:K].broadcast_to(tile64)
            V.tensor_tensor(t4, t3, kth, ALU.is_gt)
            V.tensor_tensor(t5, t3, kth, ALU.is_equal)
            V.drain()
            V.tensor_reduce(cnt, t4, axis=AX.X, op=ALU.add)
            V.tensor_tensor_scan(t2.rearrange("p t e -> p (t e)"), W.rearrange("p t e -> p (t e)"), flat5, 0.0,
                                 ALU.mult, ALU.add)
            V.drain()
            V.tensor_scalar(cnt, cnt, -1.0, K + 0.5, ALU.mult, ALU.add)
            V.drain()
            V.tensor_tensor(t2, t2, cnt.unsqueeze(2).broadcast_to(tile64), ALU.is_lt)
            V.drain()
            V.tensor_tensor(t2, t2, t5, ALU.mult)
            V.drain()
            V.tensor_tensor(t2, t2, t4, ALU.add).then_inc(sel_ready, 1)
            V.drain()
            V.tensor_tensor(W, t2, t1, ALU.mult)
            V.drain()
            V.tensor_reduce(cnt, W, axis=AX.X, op=ALU.add)
            V.drain()
            V.tensor_scalar(cnt, cnt, 1e-20, None, ALU.add)
            V.drain()
            V.reciprocal(cnt, cnt)
            V.drain()
            V.tensor_tensor(W, W, cnt.unsqueeze(2).broadcast_to(tile64), ALU.mult)
            V.drain()
            V.tensor_scalar(W, W, 2.5, None, ALU.mult).then_inc(gates_ready, 1)
            V.drain()
            dve.wait_ge(rev_ready, 1)
            for q in range(4):
                bank = FC.bank(("selT", q))
                dve.wait_ge(full[bank], FC.filled(("selT", q)))
                V.tensor_tensor(key[:, q * 512:(q + 1) * 512], ps[0:E, bank, :], rev[:, q * 512:(q + 1) * 512],
                                ALU.mult).then_inc(empt[bank], 1)
            V.drain()

            def best_keys(lo, hi):
                for r in range(lo, hi):
                    V.max(kvals[:, 8 * r:8 * r + 8], key)
                    V.drain()
                    if r < CAP // 8 - 1:
                        V.match_replace(key, kvals[:, 8 * r:8 * r + 8], key, 0.0)
                        V.drain()

            def shared_out(c):
                for j in range(4):
                    bank = FS.bank(("dn", c, j))
                    dve.wait_ge(full[bank], FS.filled(("dn", c, j)))
                    V.tensor_tensor(X[:, 4 * c + j, :], X[:, 4 * c + j, :], ps[:, bank, :], ALU.add)\
                     .then_inc(empt[bank], 1)

            best_keys(0, 6)
            shared_out(0)
            best_keys(6, 12)
            shared_out(1)
            best_keys(12, CAP // 8)
            V.tensor_scalar(empty, kvals, 0.0, None, ALU.is_equal)
            V.tensor_scalar(idxf, kvals, -1.0, float(T), ALU.mult, ALU.add)
            V.drain()
            V.tensor_tensor(empty, empty, slotno, ALU.mult)
            V.drain()
            V.tensor_tensor(idxf, idxf, empty, ALU.add).then_inc(idxf_ready, 1)
            shared_out(2)
            bank = FC.bank(("idxT",))
            dve.wait_ge(full[bank], FC.filled(("idxT",)))
            V.tensor_copy(idxU[:, 0:E], ps[:, bank, 0:E]).then_inc(empt[bank], 1)
            V.memset(idxU[:, E:E + UE], 0)
            V.drain()
            V.tensor_copy(idxg[:], idxU[:, 0:UE]).then_inc(idx_ready, 1)
            shared_out(3)
            with dve.Fori(0, E // UE) as i:
                for s in range(UE):
                    bank = FE.bank(("h", s))
                    dve.wait_ge(empt[bank], FE.drained(("h", s), i))
                    V.tensor_tensor(hsq[:, s % 2, :, :], hrel[:, s % 2, :, :], hrel[:, s % 2, :, :], ALU.mult)\
                     .then_inc(hsq_ready, 1)
                    dve.wait_ge(y_filled[s], i + 2)
                    dve.wait_ge(scatter_landed, i * UE + (s + 1))
                    dve.wait_ge(xg_loaded[s], i * 16 + 16)
                    V.tensor_copy(idxs[:, s % 2:s % 2 + 1], idxU[:, ds(i * UE + s, 1)])
                    V.tensor_copy(idxg[:, s:s + 1], idxU[:, ds(i * UE + (s + UE), 1)])
                    V.tensor_scalar(ysb[:, s % 2, :], ps[:, 4 + s % 2, :], xg[:, s, ds(i * UE + (D + s), 1)], None, ALU.mult)\
                     .then_inc(y_ready[s % 2], 1)
            for g in range(NT // FG):
                dve.wait_ge(fin_loaded[g % 2], 32 * (g // 2 + 1))
                tiles = X[:, FG * g:FG * g + FG, :]
                V.tensor_tensor(tiles, tiles, fin[:, g % 2, 0], ALU.add)
                V.drain()
                V.tensor_tensor(tiles, tiles, fin[:, g % 2, 1], ALU.add).then_inc(fin_ready, 1)

        @block.tensor
        def _(pe):
            def fill(fills, name, i=0):
                bank = fills.bank(name)
                pe.wait_ge(empt[bank], fills.free(name, i))
                return bank

            def product(out_ap, pairs):
                for n, (lhsT, rhs) in enumerate(pairs):
                    ins = TE.matmul(out_ap, lhsT, rhs, start=(n == 0), stop=(n == len(pairs) - 1))
                return ins

            def probs_T(b, c, i):
                for q in range(QB):
                    pe.wait_ge(prob_ready, i * 12 + ((2 * b + c) * QB + q + 1))
                    bank = fill(FA, ("pT", b, c, q), i)
                    for g in range(4):
                        ins = TE.transpose(ps[:, bank, g * P:(g + 1) * P], prob[:, b, 4 * c + g, q, :], ident[:])
                    ins.then_inc(full[bank], 1)

            def scores(b, c, i):
                for q in range(QB):
                    bank = fill(FA, ("s", b, c, q), i)
                    m, half = (0, b) if q == 0 else (1 + b, q - 1)
                    keys = (kbd[:, b, c, :, 64:192],
                            kbd[:, b, c, :, :].rearrange("p g (n t) -> p g n t", t=64)[:, :, 0:3:2, :],
                            kbd[:, b, c, :, 0:P])[q]
                    TE.matmul(ps[:, bank, :], qT[:, m, half, 2 * c:2 * c + 2, :], keys, start=True, stop=True)\
                        .then_inc(full[bank], 1)

            def attend(b, i):
                for c in range(2):
                    for q in range(QB):
                        name = ("pT", b, c, q)
                        pe.wait_ge(empt[FA.bank(name)], FA.drained(name, i))
                for q in range(QB):
                    bank = fill(FA, ("pv", b, q), i)
                    for k in range(KVH):
                        ins = TE.matmul(ps[:, bank, k * HD:(k + 1) * HD], pT[:, k, q, :],
                                        vkey[:, b, q, k * HD:(k + 1) * HD], start=True, stop=True)
                    ins.then_inc(full[bank], 1)

            def mean_rows(b, i):
                bank = fill(FA, ("mean", b), i)
                for c in range(2):
                    ins = product(ps[:, bank, c * 64:(c + 1) * 64],
                                  [(vlo[:, b, c * P:(c + 1) * P], inv_s), (vkey[:, b, 0, c * P:(c + 1) * P], inv_s)])
                ins.then_inc(full[bank], 1)

            def attended_T(b, i):
                for q in range(QB):
                    name = ("pv", b, q)
                    pe.wait_ge(empt[FA.bank(name)], FA.drained(name, i))
                for c in range(2):
                    bank = fill(FA, ("oT", b, c), i)
                    for q in range(QB):
                        ins = TE.transpose(ps[:, bank, q * P:(q + 1) * P], osb[:, q, c * P:(c + 1) * P], ident[:])
                    ins.then_inc(full[bank], 1)

            def project(b, i):
                for name in (("mean", b), ("oT", b, 0), ("oT", b, 1)):
                    pe.wait_ge(empt[FA.bank(name)], FA.drained(name, i))
                for h in range(2):
                    bank = fill(FA, ("wo", b, h), i)
                    product(ps[:, bank, :], [(oT[:, k, h * P:(h + 1) * P], wo[:, k, :]) for k in range(4)])\
                        .then_inc(full[bank], 1)

            pe.wait_ge(consts_ready, 1)
            pe.wait_ge(w_loaded, 16 * 6)

            def attention(i):
                for u in range(4):
                    pe.wait_ge(xln_ready, i * 4 + u + 1)
                    bank = fill(FA, ("xT", u), i)
                    for c in range(DC):
                        ins = TE.transpose(ps[:, bank, c * P:(c + 1) * P], xln[:, u, c * P:(c + 1) * P], ident[:])
                    ins.then_inc(full[bank], 1)
                for u in range(4):
                    pe.wait_ge(empt[FA.bank(("xT", u))], FA.drained(("xT", u), i))
                tokens = (lambda c: xlnT[:, c, 0:2, :].rearrange("p u t -> p (u t)")[:, 64:64 + P],
                          lambda c: xlnT[:, c, 2, :], lambda c: xlnT[:, c, 3, :])
                for m in range(3):
                    bank = fill(FA, ("q", m), i)
                    product(ps[:, bank, :], [(tokens[m](c), wq[:, c, :]) for c in range(DC)]).then_inc(full[bank], 1)
                    name, width = (("kmix",), D // 2) if m == 0 else (("kv", m - 1), D)
                    bank = fill(FA, name, i)
                    product(ps[:, bank, 0:width], [(tokens[m](c), wkv[:, c, 0:width]) for c in range(DC)])\
                        .then_inc(full[bank], 1)
                bank = fill(FA, ("vlo",), i)
                for b in range(2):
                    ins = product(ps[:, bank, b * 256:(b + 1) * 256],
                                  [(xlnT[:, c, b, :], wkv[:, c, D // 2:D]) for c in range(DC)])
                ins.then_inc(full[bank], 1)
                for m in range(3):
                    pe.wait_ge(rope_ready, i * 3 + m + 1)
                    bank = fill(FA, ("kT", m), i)
                    for c in range(2):
                        ins = TE.transpose(ps[:, bank, c * P:(c + 1) * P], kr[:, m, c * P:(c + 1) * P], ident[:])
                    ins.then_inc(full[bank], 1)
                    bank = fill(FA, ("qT", m), i)
                    for k in range(4):
                        ins = TE.transpose(ps[:, bank, k * P:(k + 1) * P], qr[:, m, k * P:(k + 1) * P], ident[:])
                    ins.then_inc(full[bank], 1)
                for m in range(3):
                    for f in ("kT", "qT"):
                        pe.wait_ge(empt[FA.bank((f, m))], FA.drained((f, m), i))
                scores(0, 0, i)
                scores(0, 1, i)
                probs_T(0, 0, i)
                scores(1, 0, i)
                probs_T(0, 1, i)
                scores(1, 1, i)
                attend(0, i)
                probs_T(1, 0, i)
                mean_rows(0, i)
                attended_T(0, i)
                probs_T(1, 1, i)
                project(0, i)
                attend(1, i)
                mean_rows(1, i)
                attended_T(1, i)
                project(1, i)

            with pe.Fori(0, PAIRS) as i:
                attention(i)
            for t in range(NT):
                pe.wait_ge(xl2_ready, t + 1)
                bank = fill(FQ, ("x2T", t))
                for c in range(DC):
                    ins = TE.transpose(ps[:, bank, c * P:(c + 1) * P], xl2[:, t % 4, c * P:(c + 1) * P], ident[:])
                ins.then_inc(full[bank], 1)
            for k in range(NBANK):
                pe.wait_ge(empt[k], FQ.all_drained(k))
            with pe.Fori(0, SH // NTR) as i:
                for s in range(NTR):
                    pe.wait_ge(head_loaded[s], i * 32 + 32)
                    pe.wait_ge(kv_ready, i * NTR + s + 1)
                    pe.wait_ge(conv_used[(s + 2) % NTR], i + (s // 2 + 1))
                    for lt in range(DC):
                        ins = product(ps[:, 4 * (s % 2) + lt, 0:B * NPAIR],
                                      [(tring[:, s, (lt - mt) * P:(lt - mt + 1) * P],
                                        kvb[:, s, mt * B:(mt + 1) * B, :].rearrange("p b n -> p (b n)"))
                                       for mt in range(lt + 1)])
                    ins.then_inc(conv_filled[s], 1)
            pe.wait_ge(conv_done, SH + 2)
            for t in range(NT):
                bank = fill(FC, ("o", t))
                at = (t % 2) * P
                for c in range(DC):
                    ins = TE.transpose(ps[:, bank, c * P:(c + 1) * P], O2[:, c, t // 2, at:at + P], ident[:])
                ins.then_inc(full[bank], 1)

            def logits(t):
                name = ("x3T", t)
                pe.wait_ge(empt[FC.bank(name)], FC.drained(name))
                bank = fill(FC, ("logit", t // 8))
                ins = product(ps[:, bank, (t % 8) * E:(t % 8 + 1) * E],
                              [(x3T[:, c, t * P:(t + 1) * P], gwT[:, c, :]) for c in range(DC)])
                if t % 8 == 7:
                    ins.then_inc(full[bank], 1)

            pe.wait_ge(ffnw_loaded, 16 * 5)
            for t in range(NT):
                pe.wait_ge(x3_ready[t % 2], t // 2 + 1)
                bank = fill(FC, ("x3T", t))
                for c in range(DC):
                    ins = TE.transpose(ps[:, bank, c * P:(c + 1) * P], x3[:, t % 2, c * P:(c + 1) * P], ident[:])
                ins.then_inc(full[bank], 1)
                if t:
                    logits(t - 1)
            logits(NT - 1)

            def shared_up(c):
                for j in range(SHD // P):
                    bank = fill(FS, ("up", c, j))
                    product(ps[:, bank, :], [(suT[:, k, j * P:(j + 1) * P], x3T[:, k, c * 512:(c + 1) * 512])
                                             for k in range(DC)]).then_inc(full[bank], 1)

            def shared_down(c):
                pe.wait_ge(hid_ready, (c + 1) * (SHD // P))
                for j in range(4):
                    bank = fill(FS, ("dn", c, j))
                    product(ps[:, bank, :], [(hid[:, c % 2, k, j * P:(j + 1) * P], sdT[:, k, :])
                                             for k in range(SHD // P)]).then_inc(full[bank], 1)

            shared_up(0)
            pe.wait_ge(sel_ready, 1)
            for q in range(4):
                bank = fill(FC, ("selT", q))
                for k in range(4):
                    ins = TE.transpose(ps[0:E, bank, k * P:(k + 1) * P], t2[:, 4 * q + k, :], ident[:])
                ins.then_inc(full[bank], 1)
            shared_up(1)
            shared_down(0)
            shared_up(2)
            shared_down(1)
            shared_up(3)
            shared_down(2)
            pe.wait_ge(idxf_ready, 1)
            bank = fill(FC, ("idxT",))
            TE.transpose(ps[:, bank, 0:E], idxf, ident[0:E, 0:E]).then_inc(full[bank], 1)
            shared_down(3)

            def tokens_T(s, i):
                pe.wait_ge(xg_loaded[s], i * 16 + 16)
                bank = fill(FE, ("xgT", s), i)
                for c in range(DC):
                    ins = TE.transpose(ps[:, bank, c * P:(c + 1) * P], xg[:, s, c * P:(c + 1) * P], ident[:])
                ins.then_inc(full[bank], 1)

            def hidden(s, i):
                pe.wait_ge(empt[FE.bank(("xgT", s))], FE.drained(("xgT", s), i))
                pe.wait_ge(wexp_loaded[s % NW], i * (16 * UE // NW) + (16 * (s // NW) + 16))
                bank = fill(FE, ("h", s), i)
                for j in range(2):
                    ins = product(ps[:, bank, j * P:(j + 1) * P],
                                  [(wring[:, s % NW, c * I + j * P:c * I + (j + 1) * P], xgT[:, s % 2, c, :])
                                   for c in range(DC)])
                ins.then_inc(full[bank], 1)

            def outputs(s, i):
                pe.wait_ge(hsq_ready, i * UE + (s + 2))
                pe.wait_ge(y_ready[s % 2], i * (UE // 2) + (s // 2 + 1))
                product(ps[:, 4 + s % 2, :], [(hsq[:, s % 2, j, :], wring[:, s % NW, DC * I + j * D:DC * I + (j + 1) * D])
                                              for j in range(2)]).then_inc(y_filled[s], 1)

            for k in (4, 5):
                pe.wait_ge(empt[k], FS.all_drained(k))
            tokens_T(0, 0)
            tokens_T(1, 0)
            hidden(0, 0)
            last = E // UE - 1
            with pe.Fori(0, last) as i:
                for s in range(UE):
                    tokens_T((s + 2) % UE, i + (s + 2) // UE)
                    hidden((s + 1) % UE, i + (s + 1) // UE)
                    outputs(s, i)
            for s in range(UE):
                if s < UE - 2:
                    tokens_T(s + 2, last)
                if s < UE - 1:
                    hidden(s + 1, last)
                outputs(s, last)



def constants():
    f = np.float32
    half = HD // 2
    freqs = f(1.0) / f(10000.0) ** (np.arange(half, dtype=f) / f(half))
    angle = np.outer(np.arange(S, dtype=f), freqs).astype(f)
    sin, cos = np.sin(angle), np.cos(angle)
    cos2 = np.concatenate([cos, cos], 1)
    sin2 = np.concatenate([-sin, sin], 1)
    pos = np.stack([64 + np.arange(P) % 64, 128 + np.arange(P)])
    rope = np.stack([cos2[pos], sin2[pos]], 1).transpose(2, 0, 1, 3).astype(f)
    slopes = np.power(f(2.0) ** f(-0.5), np.arange(1, H + 1, dtype=f)).astype(f)
    bias = np.zeros((P, KVH, QB, P), f)
    keys = [np.arange(128, 256), np.concatenate([np.arange(64, 128), np.arange(192, 256)]), np.arange(64, 192)]
    row = np.arange(P)
    for q in range(QB):
        dist = np.abs((64 * (q + 1) + row % 64)[:, None] - keys[q][None, :])
        for k in range(KVH):
            slope = slopes[2 * k + row // 64][:, None]
            bias[:, k, q] = np.where(dist > WIN // 2, -(slope * dist.astype(f)), f(NEG))
    tri = np.tile((np.arange(8)[None, :] < np.arange(8)[:, None]).astype(f).reshape(1, 64), (P, 1))
    return rope, bias, tri


def kernel(x, ctx_2048, L0_attn_Wq, L0_attn_Wkv, L0_attn_Wo, L0_attn_bo, L0_xattn_ssm_kernel, L0_xattn_D,
           L0_ffn_gate_w, L0_ffn_e_bias, L0_ffn_w1, L0_ffn_w2, L0_ffn_shared_up_w, L0_ffn_shared_down_w):
    import concourse.bacc as bacc
    from concourse.bass_utils import run_bass_kernel_spmd

    C = np.ascontiguousarray
    rope, bias, tri = constants()
    chunked = lambda w: C(np.asarray(w).reshape(w.shape[0] // P, P, w.shape[1]).transpose(1, 0, 2))
    wq = np.asarray(L0_attn_Wq).reshape(D, 2, 4, 2, HD).transpose(0, 1, 3, 2, 4).reshape(D, D)
    wo = np.asarray(L0_attn_Wo).reshape(2, 4, 2, HD, D).transpose(0, 2, 1, 3, 4).reshape(D, D)
    ctx = np.asarray(ctx_2048).reshape(B, SH, SD, DC, P)[..., ::-1]
    ctx = np.concatenate([ctx, ctx[:, :, :4]], 2).transpose(1, 4, 3, 0, 2)
    w1 = np.asarray(L0_ffn_w1).transpose(0, 2, 1).reshape(E, DC, P, I).transpose(0, 2, 1, 3).reshape(E, P, DC * I)
    w2 = np.asarray(L0_ffn_w2).transpose(0, 2, 1).reshape(E, 2, P, D).transpose(0, 2, 1, 3).reshape(E, P, 2 * D)
    arrays = {
        "x": C(np.asarray(x).reshape(T, D)),
        "wq": chunked(wq), "wkv": chunked(np.asarray(L0_attn_Wkv)), "wo": chunked(wo),
        "bo": C(np.broadcast_to(np.asarray(L0_attn_bo), (P, D))),
        "rope": C(rope), "bias": C(bias), "tri": C(tri),
        "kern": C(np.asarray(L0_xattn_ssm_kernel)), "skip": C(np.asarray(L0_xattn_D).reshape(SH, 1)),
        "ctxE": C(ctx.reshape(SH * P, DC * B * 12)),
        "suT": chunked(np.asarray(L0_ffn_shared_up_w).T), "sdT": chunked(np.asarray(L0_ffn_shared_down_w).T),
        "gwT": chunked(np.asarray(L0_ffn_gate_w).T),
        "ebias": C(np.broadcast_to(np.asarray(L0_ffn_e_bias), (P, E))),
        "wexp": C(np.concatenate([w1, w2], 2).reshape(E * P, 2048)),
    }
    nc = bacc.Bacc("TRN2", target_bir_lowering=False, num_devices=1)
    aps = {n: nc.dram_tensor(n, v.shape, mybir.dt.from_np(v.dtype), kind="ExternalInput").ap()
           for n, v in arrays.items()}
    out = nc.dram_tensor("out", (T, D), mybir.dt.float32, kind="ExternalOutput").ap()
    program(nc, aps, out)
    r = run_bass_kernel_spmd(nc, [arrays], core_ids=[0])
    return r.results[0]["out"].reshape(B, S, D)
```

```python
import numpy as np
from contextlib import ExitStack

import concourse.bass as bass
from concourse import mybir

P = 128
B, S, D = 8, 256, 512
T = B * S
NT = T // P
DC = D // P
H, KVH, HD = 16, 8, 32
NEG = -1e9
WIN, GLOB = 128, 64
PAIRS = B // 2
QB = 3
SH, SD = 32, 8
NPAIR = 36
E, K, NG, TKG, CAP, I = 64, 6, 8, 4, 128, 256
SHD = 1024
ROWS = T + P
XW = D + E
EPS = 1e-5
TILES3 = list(range(1, NT, 2)) + list(range(0, NT, 2))
NBANK = 8


class Fills:

    def __init__(self, before, names, times=1):
        self.before, self.at, per = list(before), {}, [0] * NBANK
        for name, bank in names:
            assert name not in self.at, name
            self.at[name] = (bank, per[bank])
            per[bank] += 1
        self.per = per
        self.after = [a + times * b for a, b in zip(before, per)]

    def bank(self, name):
        return self.at[name][0]

    def free(self, name, i=0):
        bank, n = self.at[name]
        return (self.before[bank] + n + 1) + i * self.per[bank]

    def drained(self, name, i=0):
        return self.free(name, i) + 1

    def all_drained(self, bank):
        return self.after[bank] + 1

    def filled(self, name, i=0):
        bank, n = self.at[name]
        return (self.before[bank] + n + 1) + i * self.per[bank]


def program(nc, a, out):
    f32, u32 = mybir.dt.float32, mybir.dt.uint32
    ALU, ACT, AX = mybir.AluOpType, mybir.ActivationFunctionType, mybir.AxisListType
    V, G, A, TE = nc.vector, nc.gpsimd, nc.scalar, nc.tensor
    ds = bass.ds

    toep = nc.dram_tensor("toeplitz_rows", (SH, P + D), f32, kind="Internal").ap()
    xrows = nc.dram_tensor("token_rows", (ROWS, XW), f32, kind="Internal").ap()

    ctx = ExitStack()
    with ctx:
        def sb(name, shape, dt=f32):
            return ctx.enter_context(nc.sbuf_tensor(name, shape, dt))

        def sem(name):
            return ctx.enter_context(nc.semaphore(name))

        X = sb("residual", [P, NT, D])
        QT2 = sb("features_T", [P, DC, T])
        x3T = QT2
        ident = sb("ident", [P, P])
        stats1 = sb("stats1", [P, 4, 6])
        meanvar1 = sb("meanvar1", [P, 4, 2])
        rstd1 = sb("rstd1", [P, 4])
        stats = sb("stats", [P, NT, 6])
        meanvar = sb("meanvar", [P, NT, 2])
        rstd = sb("rstd", [P, NT])
        minus_half = sb("minus_half", [P, NT])
        zeros = sb("zeros", [P, D])
        kpad = sb("padded_kernels", [SH, P + D])
        dcol = sb("skip_gain", [SH, 1])
        idxU = sb("slot_rows_u32", [P, E + 8], u32)
        idxg = sb("gather_rows", [P, 8], u32)
        idxs = sb("scatter_rows", [P, 2], u32)
        idxt = sb("tile_scatter_rows", [P, 1], u32)
        tile_rows = sb("tile_rows", [P, NT // 2])
        AREA = 34400
        arena = sb("arena", [P, AREA])
        place = [0]

        def carve(shape, at=None, rows=P):
            n = int(np.prod(shape))
            if at is not None:
                place[0] = at
            v = arena[0:rows, place[0]:place[0] + n]
            place[0] += n
            assert place[0] <= AREA, place[0]
            if len(shape) > 1:
                names = "abcde"[:len(shape)]
                v = v.rearrange(f"p ({' '.join(names)}) -> p {' '.join(names)}",
                                **{c: s for c, s in zip(names, shape)})
            return v

        wq = carve([DC, D], at=0)
        wkv = carve([DC, D])
        wo = carve([DC, D])
        bo = carve([D])
        rope = carve([2, 2, HD])
        bias = carve([KVH, QB, P])
        xln = carve([4, D])
        xl2 = xln
        xlnT = carve([DC, 4, P])
        qs = carve([3, D])
        qr = carve([3, D])
        ks = carve([3, D // 2])
        kr = carve([3, D // 2])
        qT = carve([3, 2, 4, 64])
        vlo = carve([2, D // 2])
        vkey = carve([2, QB, D // 2])
        prob = carve([2, KVH, QB, P])
        pT = carve([KVH, QB, P])
        negmax = carve([2, KVH, QB])
        rowsum = carve([2, KVH, QB])
        rinv = carve([2, KVH, QB])
        inv_s = carve([64])
        asum = carve([4])
        edec = carve([4])
        cgate = carve([3])
        spare = QT2[:].rearrange("p c t -> p (c t)")
        kbd = spare[:, 0:3072].rearrange("p (b c g t) -> p b c g t", b=2, c=2, g=4)
        tq = spare[:, 3072:3072 + 3 * D].rearrange("p (m d) -> p m d", m=3)
        tk = spare[:, 3072 + 3 * D:3072 + 9 * D // 2].rearrange("p (m d) -> p m d", m=3)
        oT = carve([2, 4, S])
        NTR = 4
        tring = carve([NTR, D], at=0)
        cring = carve([NTR, DC * B, 12])
        O2 = carve([DC, B, S])
        kvb = carve([NTR, DC * B, NPAIR], at=11904)
        qx = carve([NTR, DC * B, 12])
        prodb = carve([2, DC * B, 8, 8])
        halfsum = carve([2, 2 * B, 8, 4])
        assert place[0] <= 25088
        oeven = carve([NT // 2, D], at=11904)
        NW = 4
        wring = carve([NW, 2048], at=16896)
        suT = carve([DC, SHD])
        sdT = carve([SHD // P, D])
        gwT = carve([DC, E])
        ebias = carve([E])
        tri = carve([64])
        NX = 4
        x3 = carve([NX, D], at=0)
        W = carve([NT, E], at=9216)
        t1 = carve([NT, E])
        t2 = carve([NT, E])
        t3 = carve([NT, E])
        t4 = carve([NT, E])
        t5 = carve([NT, E])
        g1 = carve([NT, 8])
        g2 = carve([NT, 8])
        m8 = carve([NT, 8])
        cnt = carve([NT])
        assert place[0] <= 16896, place[0]
        sel = carve([NT // 2, 2, E], at=8192)
        rev = carve([T // 2], at=12288)
        key = carve([T // 2])
        best = carve([2 * CAP])
        kvals = carve([P], rows=E)
        empty = carve([P], rows=E)
        idxf = carve([P], rows=E)
        slotno = carve([P], rows=E)
        hid = carve([2, SHD // P, D], at=0)
        UE = 8
        xg = carve([UE, XW], at=8192)
        xgT = carve([2, DC, P])
        hrel = carve([2, 2, P])
        hsq = carve([2, 2, P])
        ysb = carve([2, D])
        ytile = carve([D], at=0)
        htile = carve([SHD // P, P])
        ps = ctx.enter_context(nc.psum_tensor("ps", [P, NBANK, 512], f32))

        full = [sem(f"bank{k}_filled") for k in range(NBANK)]
        empt = [sem(f"bank{k}_drained") for k in range(NBANK)]
        w_loaded = sem("attention_weights_loaded")
        tables_loaded = sem("rope_bias_wo_loaded")
        x_loaded = sem("x_loaded")
        consts_ready = sem("consts_ready")
        small_loaded = sem("small_loaded")
        pad_ready = sem("padded_kernels_ready")
        toep_written = sem("toeplitz_written")
        zero_written = sem("zero_rows_written")
        stats_ready = sem("ln1_stats_ready")
        rstd_ready = sem("ln1_rstd_ready")
        xln_ready = sem("xln_ready")
        bo_added = sem("bo_added")
        asum_ready = sem("asum_ready")
        edec_ready = sem("edec_ready")
        cgate_ready = sem("cgate_ready")
        tq_ready = sem("rope_cos_part_ready")
        rope_ready = sem("rope_ready")
        max_ready = sem("row_max_ready")
        inverse_ready = sem("inverse_row_sums_ready")
        exp_ready = sem("exponentials_ready")
        prob_ready = sem("prob_ready")
        stats2_ready = sem("ln2_stats_ready")
        rstd2_ready = sem("ln2_rstd_ready")
        xl2_ready = sem("xl2_ready")
        head_loaded = [sem(f"head_slot{k}_loaded") for k in range(NTR)]
        kv_ready = sem("kv_products_ready")
        qx_ready = sem("q_cyclic_ready")
        ffnw_loaded = sem("ffn_weights_loaded")
        conv_filled = [sem(f"head_slot{k}_multiplied") for k in range(NTR)]
        conv_used = [sem(f"head_slot{k}_products_taken") for k in range(NTR)]
        half_ready = sem("head_half_sums_ready")
        conv_done = sem("heads_convolved")
        even_added = sem("even_tiles_added")
        stats3_ready = sem("ln3_stats_ready")
        rstd3_ready = sem("ln3_rstd_ready")
        x3_ready = [sem(f"x3_slot{k}_ready") for k in range(NX)]
        x3_written = [sem(f"x3_slot{k}_written") for k in range(NX)]
        score_ready = sem("exp_logits_ready")
        sel_ready = sem("selection_ready")
        rev_ready = sem("token_keys_ready")
        gates_ready = sem("gates_ready")
        gates_written = sem("gates_written")
        idxf_ready = sem("slot_tokens_ready")
        idx_ready = sem("slot_rows_ready")
        hid_ready = sem("shared_hidden_ready")
        wexp_loaded = [sem(f"expert_weights_slot{k}_loaded") for k in range(NW)]
        xg_loaded = [sem(f"gathered_slot{k}_loaded") for k in range(UE)]
        y_filled = [sem(f"expert_out_slot{k}_filled") for k in range(UE)]
        y_ready = [sem(f"expert_rows{k}_ready") for k in range(2)]
        hsq_ready = sem("expert_hidden_ready")
        htile_ready = sem("shared_tile_hidden_ready")
        tile_ready = sem("shared_tile_ready")
        added = sem("rows_added_to_the_result")
        scatter_landed = sem("scatter_landed")
        out_written = sem("result_rows_begun")

        names = []
        turn = [0]

        def rot(*fills):
            for f in fills:
                names.append((f, turn[0] % NBANK))
                turn[0] += 1

        def scores(b, c):
            rot(*[("s", b, c, q) for q in range(QB)])


        def prepared_fills(part):
            rot(*{"xT": [("xT", u) for u in range(4)],
                  "qk": [(f, m) for m in range(3) for f in "qk"],
                  "kqT": [(f, m) for m in range(3) for f in ("kT", "qT")]}[part])

        def pair_fills(more):
            scores(0, 0)
            scores(0, 1)
            rot(("vhi",), ("vlo",))
            rot(*[("pT", 0, 0, q) for q in range(QB)])
            scores(1, 0)
            if more:
                prepared_fills("xT")
            rot(*[("pT", 0, 1, q) for q in range(QB)])
            scores(1, 1)
            if more:
                prepared_fills("qk")
            rot(*[("pv", 0, c, q) for c in range(2) for q in range(QB)])
            rot(*[("pT", 1, 0, q) for q in range(QB)])
            rot(*[("pT", 1, 1, q) for q in range(QB)])
            rot(("mean", 0))
            if more:
                prepared_fills("kqT")
            rot(*[("pv", 1, c, q) for c in range(2) for q in range(QB)])
            rot(("mean", 1), *[("wo", b, h) for b in range(2) for h in range(2)])

        for part in ("xT", "qk", "kqT"):
            prepared_fills(part)
        FA0 = Fills([0] * NBANK, names)
        names = []
        pair_fills(True)
        FA = Fills(FA0.after, names, PAIRS - 1)
        names = []
        pair_fills(False)
        FA1 = Fills(FA.after, names)
        FQ = Fills(FA1.after, [(("x2T", t), 4 + t % 4) for t in range(NT)])
        names = [(("o", t), 4 * (t % 2) + t // 2 % 4) for t in sorted(range(NT), key=lambda t: t % 2)]
        names += [(("x3T", t), 4 + k % 4) for k, t in enumerate(TILES3)]
        names += [(("logit", 0), 2), (("logit", 1), 3)]
        names += [(("selT", q), 4 + q) for q in range(2)] + [(("idxT",), 7)]
        FC = Fills(FQ.after, names)
        names = []
        for c in range(2):
            names += [(("up", c, j), j % 4) for j in range(SHD // P)]
            names += [(("dn", c, j), 4 + (4 * c + j) % 3) for j in range(4)]
        FS = Fills(FC.after, names)
        FE = Fills(FS.after, [(("xgT", s), s % 2) for s in range(UE)] + [(("h", s), 2 + s % 2) for s in range(UE)]
                   + [(("tile_up", k), 6) for k in range(2)] + [(("tile_dn",), 7)],
                   E // UE)

        block = ctx.enter_context(nc.Block())

        @block.sync
        def _(sp):
            sp.dma_start(X[:, 0:4, :], a["x"][0:4 * P, :].rearrange("(t p) d -> p t d", p=P)).then_inc(x_loaded, 16)
            for s in (*empt, *conv_used, *conv_filled, *y_filled, *y_ready, hsq_ready, tile_ready):
                sp.sem_inc(s, 1)
            sp.sem_inc(scatter_landed, 3)
            sp.sem_inc(conv_done, 2)
            sp.sem_inc(x_loaded, 16)
            sp.wait_ge(tables_loaded, 16 * 4)
            with sp.Fori(1, PAIRS) as i:
                sp.wait_ge(x_loaded, i * 16 + 16)
                sp.dma_start(X[:, ds(i * 4, 4), :],
                             a["x"][ds(i * (4 * P), 4 * P), :].rearrange("(t p) d -> p t d", p=P)).then_inc(x_loaded, 16)
            sp.wait_ge(consts_ready, 1)
            sp.dma_start(out[T:ROWS, :], zeros[:]).then_inc(zero_written, 16)
            sp.dma_start(xrows[T:ROWS, 0:D], zeros[:]).then_inc(zero_written, 16)
            sp.dma_start(xrows[T:ROWS, D:XW], zeros[:, 0:E]).then_inc(zero_written, 16)
            sp.wait_ge(pad_ready, 1)
            sp.dma_start(toep[:], kpad[:]).then_inc(toep_written, 16)
            sp.wait_ge(full[FA1.bank(("vlo",))], FA1.filled(("vlo",)))
            sp.wait_ge(toep_written, 16)
            toep_v = bass.AP(toep.tensor, 1, [[P + D, SH], [1, P], [1, D]])
            with sp.Fori(0, SH // NTR) as i:
                for s in range(NTR):
                    sp.wait_ge(conv_filled[s], i + 1)
                    sp.wait_ge(toep_written, 16)
                    sp.dma_start(tring[:, s:s + 1, :], toep_v[ds(i * NTR + s, 1), :, :].rearrange("h p d -> p h d"))\
                      .then_inc(head_loaded[s], 16)
                    sp.dma_start(cring[:, s, :, :].rearrange("p m i -> p (m i)"),
                                 a["ctxE"][ds((i * NTR + s) * P, P), :]).then_inc(head_loaded[s], 16)
            for k, t in enumerate(TILES3):
                sp.wait_ge(x3_ready[k % NX], k // NX + 1)
                sp.dma_start(xrows[t * P:(t + 1) * P, 0:D], x3[:, k % NX, :]).then_inc(x3_written[k % NX], 16)
            sp.wait_ge(gates_ready, 1)
            sp.dma_start(xrows[0:T, D:XW].rearrange("(t p) c -> p t c", p=P), W).then_inc(gates_written, 16)
            with sp.Fori(0, E // UE) as i:
                for s in range(UE):
                    sp.wait_ge(y_filled[(s - NW) % UE], i + (s // NW + 1))
                    sp.wait_ge(gates_ready, 1)
                    sp.dma_start(wring[:, s % NW, :], a["wexp"][ds((i * UE + s) * P, P), :])\
                      .then_inc(wexp_loaded[s % NW], 16)
            sp.wait_ge(added, 16 * (E + NT // 2))

        @block.gpsimd
        def _(pool):
            G.memset(ident[:], 0.0)
            G.memset(minus_half[:], -0.5)
            G.memset(zeros[:], 0.0)
            G.memset(kpad[:, 0:P], 0.0)
            G.memset(inv_s, 1.0 / S)
            G.memset(kbd, 0.0)
            G.iota(tile_rows[:], [[P, NT // 2]], base=T // 2, channel_multiplier=1, allow_small_or_imprecise_dtypes=True)
            G.drain()
            G.affine_select(out=ident[:], in_=ident[:], compare_op=ALU.not_equal, fill=1.0, base=0,
                            pattern=[[-1, P]], channel_multiplier=1).then_inc(consts_ready, 1)

            def ln1_rstd(i):
                pool.wait_ge(stats_ready, i + 1)
                G.tensor_tensor(rstd1[:], rstd1[:], minus_half[:, 0:4], ALU.pow).then_inc(rstd_ready, 1)

            def add_bias(i):
                pool.wait_ge(xln_ready, i * 4 + 4)
                G.tensor_tensor(X[:, ds(i * 4, 4), :], X[:, ds(i * 4, 4), :],
                                bo.unsqueeze(1).broadcast_to((P, 4, D)), ALU.add).then_inc(bo_added, 1)

            def rotate(F, n):
                for m in range(3):
                    cos = rope[:, min(m, 1), 0, :]
                    for f in "kq":
                        pool.wait_ge(empt[F.bank((f, m))], F.drained((f, m), n))
                    G.tensor_tensor(tk[:, m, :].rearrange("p (h d) -> p h d", d=HD),
                                    ks[:, m, :].rearrange("p (h d) -> p h d", d=HD),
                                    cos.unsqueeze(1).broadcast_to((P, KVH, HD)), ALU.mult)
                    G.tensor_tensor(tq[:, m, :].rearrange("p (h d) -> p h d", d=HD),
                                    qs[:, m, :].rearrange("p (h d) -> p h d", d=HD),
                                    cos.unsqueeze(1).broadcast_to((P, H, HD)), ALU.mult).then_inc(tq_ready, 1)

            def softmax(b, c, i):
                pool.wait_ge(inverse_ready, i * 4 + (2 * b + c + 1))
                for q in range(QB):
                    e = prob[:, b, 4 * c:4 * c + 4, q, :]
                    G.tensor_tensor(e, e, rinv[:, b, 4 * c:4 * c + 4, q:q + 1].broadcast_to((P, 4, P)), ALU.mult)\
                     .then_inc(prob_ready, 1)

            def attention(F, n, i, more):
                softmax(0, 0, i)
                if more:
                    ln1_rstd(i + 1)
                softmax(0, 1, i)
                softmax(1, 0, i)
                softmax(1, 1, i)
                if more:
                    rotate(F, n)
                    add_bias(i + 1)

            ln1_rstd(0)
            pool.wait_ge(tables_loaded, 16 * 4)
            rotate(FA0, 0)
            add_bias(0)
            pool.wait_ge(small_loaded, 32)
            G.tensor_tensor(kpad[:, P:P + 1], kpad[:, P:P + 1], dcol[:], ALU.add).then_inc(pad_ready, 1)
            with pool.Fori(0, PAIRS - 1) as i:
                attention(FA, i, i, True)
            attention(FA1, 0, PAIRS - 1, False)

            def pair_products(s, i):
                pool.wait_ge(head_loaded[s], i * 32 + 32)
                pool.wait_ge(conv_filled[s], i + 1)
                c = cring[:, s, :, :]
                G.tensor_tensor(kvb[:, s, :, 0:32].rearrange("p m (d i) -> p m d i", d=4),
                                c[:, :, 0:SD].unsqueeze(2).broadcast_to((P, DC * B, 4, SD)),
                                bass.AP(c.tensor, c.offset, [list(c.ap[0]), [12, DC * B], [1, 4], [1, SD]]),
                                ALU.mult)
                G.tensor_tensor(kvb[:, s, :, 32:36], c[:, :, 0:4], c[:, :, 4:8], ALU.mult).then_inc(kv_ready, 1)

            def half_sums(s, i):
                pool.wait_ge(conv_used[s], i + 2)
                pv = prodb[:, s % 2, 2 * B:, :, :].rearrange("p m j k -> p (m j) k")
                G.tensor_tensor(halfsum[:, s % 2].rearrange("p m j k -> p (m j) k"), pv[:, :, 0:4], pv[:, :, 4:8],
                                ALU.add).then_inc(half_ready, 1)

            pair_products(0, 0)
            pair_products(1, 0)
            pool.wait_ge(stats2_ready, 1)
            G.tensor_tensor(rstd[:], rstd[:], minus_half[:], ALU.pow).then_inc(rstd2_ready, 1)
            last = SH // NTR - 1
            with pool.Fori(0, last) as i:
                for s in range(NTR):
                    pair_products((s + 2) % NTR, i + (s + 2) // NTR)
                    half_sums(s, i)
            for s in range(NTR):
                if s < NTR - 2:
                    pair_products(s + 2, last)
                half_sums(s, last)
            for t in range(0, NT, 2):
                pool.wait_ge(empt[FC.bank(("o", t))], FC.drained(("o", t)))
                G.tensor_tensor(X[:, t, :], X[:, t, :], oeven[:, t // 2, :], ALU.add).then_inc(even_added, 1)
            for half in range(2):
                pool.wait_ge(stats3_ready, half + 1)
                r = rstd[:].rearrange("p (k g) -> p g k", g=2)[:, 1 - half, :]
                G.tensor_tensor(r, r, minus_half[:, 0:NT // 2], ALU.pow).then_inc(rstd3_ready, 1)
            pool.wait_ge(sel_ready, 1)
            G.iota(rev, [[-1, T // 2]], base=T // 2, channel_multiplier=0, allow_small_or_imprecise_dtypes=True)
            G.iota(slotno, [[1, P]], base=0, channel_multiplier=0, allow_small_or_imprecise_dtypes=True)\
             .then_inc(rev_ready, 1)
            for c in range(2):
                for j in range(SHD // P):
                    pool.wait_ge(empt[FS.bank(("up", c, j))], FS.drained(("up", c, j)))
                    G.tensor_tensor(hid[:, c % 2, j, :], hid[:, c % 2, j, :], hid[:, c % 2, j, :], ALU.mult)\
                     .then_inc(hid_ready, 1)
            for k in range(NX):
                pool.wait_ge(x3_written[k], 16 * (NT // NX))
            pool.wait_ge(gates_written, 16)
            pool.wait_ge(zero_written, 16 * 3)
            pool.wait_ge(idx_ready, 1)

            def gather(s):
                pool.indirect_dma_start(xg[:, s, :], None, xrows, bass.IndirectOffsetOnAxis(ap=idxg[:, s:s + 1], axis=0))\
                    .then_inc(xg_loaded[s], 16)

            def scatter(s, i, before):
                pool.wait_ge(y_ready[s % 2], i * (UE // 2) + (s // 2 + 2))
                if before is not None:
                    pool.wait_ge(added, before)
                    pool.sem_inc(scatter_landed, 1)
                pool.indirect_dma_start(out, bass.IndirectOffsetOnAxis(ap=idxs[:, s % 2:s % 2 + 1], axis=0),
                                        ysb[:, s % 2, :], None, compute_op=ALU.add).then_inc(added, 16)

            def scatter_tile(i):
                pool.wait_ge(tile_ready, i + 2)
                pool.wait_ge(added, i * (16 * (UE + 1)) + 16 * UE)
                pool.sem_inc(scatter_landed, 1)
                pool.indirect_dma_start(out, bass.IndirectOffsetOnAxis(ap=idxt[:, 0:1], axis=0),
                                        ytile, None, compute_op=ALU.add).then_inc(added, 16)

            last = E // UE - 1
            for s in range(UE):
                gather(s)
            pool.wait_ge(out_written, 16 * 3)
            scatter(0, 0, None)
            with pool.Fori(0, last) as i:
                for s in range(UE):
                    if s == UE - 1:
                        scatter_tile(i)
                    scatter((s + 1) % UE, i + (s + 1) // UE, i * (16 * (UE + 1)) + 16 * (s + 1 + (s + 1) // UE))
                    gather(s)
            for s in range(UE - 1):
                scatter(s + 1, last, last * (16 * (UE + 1)) + 16 * (s + 1))
            scatter_tile(last)
        @block.scalar
        def _(act):
            def load(dst, name, s):
                act.dma_start(dst, a[name]).then_inc(s, 16)
            load(wq, "wq", w_loaded)
            load(wkv, "wkv", w_loaded)
            load(rope, "rope", tables_loaded)
            load(bo, "bo", tables_loaded)
            load(bias, "bias", tables_loaded)
            load(wo, "wo", tables_loaded)
            load(kpad[:, P:], "kern", small_loaded)
            load(dcol[:], "skip", small_loaded)

            def evacuate(fills, name, i, dst, src, scale=None):
                bank = fills.bank(name)
                act.wait_ge(full[bank], fills.filled(name, i))
                kw = {} if scale is None else {"scale": scale}
                A.activation(dst, src, ACT.Copy, **kw).then_inc(empt[bank], 1)

            def quad(bank, rows=P):
                return ps[0:rows, bank, :].rearrange("p (c t) -> p c t", c=4)

            def exps(b, c, i):
                for q in range(QB):
                    act.wait_ge(max_ready, i * 12 + ((2 * b + c) * QB + q + 1))
                    for k in range(4 * c, 4 * c + 4):
                        ins = A.activation(prob[:, b, k, q, :], prob[:, b, k, q, :], ACT.Exp,
                                           bias=negmax[:, b, k, q:q + 1], scale=1.0,
                                           accum_out=rowsum[:, b, k, q:q + 1])
                    ins.then_inc(exp_ready, 1)

            def probs_T(F, n, b, c):
                for q in (0, 2):
                    name = ("pT", b, c, q)
                    evacuate(F, name, n, pT[:, 4 * c:4 * c + 4, q, :], quad(F.bank(name)))

            def attended(F, n, b):
                for q in range(QB):
                    name = ("pv", b, 0, q)
                    bank = F.bank(name)
                    act.wait_ge(full[bank], F.filled(name, n))
                    for g in range(4):
                        rows = slice(32 * g, 32 * g + 32)
                        ins = A.activation(oT[rows, b, 0:2, 64 * (q + 1):64 * (q + 2)],
                                           ps[rows, bank, g * P:(g + 1) * P].rearrange("p (r t) -> p r t", r=2), ACT.Copy)
                    ins.then_inc(empt[bank], 1)

            def gate_exps(i):
                act.wait_ge(asum_ready, i + 1)
                A.activation(edec, asum, ACT.Exp, scale=-1.0).then_inc(edec_ready, 1)

            def tokens_T(F, n):
                for u in range(4):
                    name = ("xT", u)
                    src = quad(F.bank(name))
                    if u == 2:
                        act.wait_ge(full[F.bank(name)], F.filled(name, n))
                        A.activation(xlnT[:, :, 1, 64:P], src[:, :, 0:64], ACT.Copy)
                        A.activation(xlnT[:, :, 1, 0:64], src[:, :, 64:P], ACT.Copy).then_inc(empt[F.bank(name)], 1)
                    else:
                        evacuate(F, name, n, xlnT[:, :, {0: 0, 1: 2, 3: 3}[u], :], src)

            def lower_v(F, n):
                bank = F.bank(("vlo",))
                act.wait_ge(full[bank], F.filled(("vlo",), n))
                A.activation(vlo, ps[:, bank, :].rearrange("p (b d) -> p b d", b=2), ACT.Copy)
                for b in range(2):
                    rows = slice(64, P) if b == 0 else slice(0, 64)
                    for q in (1, 2):
                        ins = A.activation(vkey[0:64, b, q, :], ps[rows, bank, b * 256:(b + 1) * 256], ACT.Copy)
                ins.then_inc(empt[bank], 1)

            def qk(F, n, i):
                act.wait_ge(cgate_ready, i + 1)
                for m in range(3):
                    evacuate(F, ("q", m), n, qs[:, m, :], ps[:, F.bank(("q", m)), :], scale=cgate[:, m:m + 1])
                    evacuate(F, ("k", m), n, ks[:, m, :], ps[:, F.bank(("k", m)), 0:D // 2])

            def qk_T(F, n):
                bank = F.bank(("kT", 0))
                act.wait_ge(full[bank], F.filled(("kT", 0), n))
                for g in range(4):
                    rows = slice(32 * g, 32 * g + 32)
                    ins = A.activation(kbd[rows, :, :, g, 0:64],
                                       ps[rows, bank, 0:2 * P].rearrange("p (c b t) -> p b c t", c=2, b=2), ACT.Copy)
                ins.then_inc(empt[bank], 1)
                for m in range(3):
                    evacuate(F, ("qT", m), n, qT[:, m, :, :, :].rearrange("p n k t -> p k n t"),
                             quad(F.bank(("qT", m))).rearrange("p k (n t) -> p k n t", n=2))

            def attention(F, n, i, more):
                exps(0, 0, i)
                exps(0, 1, i)
                lower_v(F, n)
                probs_T(F, n, 0, 0)
                if more:
                    tokens_T(F, n)
                probs_T(F, n, 0, 1)
                exps(1, 0, i)
                if more:
                    gate_exps(i + 1)
                exps(1, 1, i)
                if more:
                    qk(F, n, i + 1)
                attended(F, n, 0)
                probs_T(F, n, 1, 0)
                probs_T(F, n, 1, 1)
                if more:
                    qk_T(F, n)
                attended(F, n, 1)

            tokens_T(FA0, 0)
            gate_exps(0)
            qk(FA0, 0, 0)
            qk_T(FA0, 0)
            with act.Fori(0, PAIRS - 1) as i:
                attention(FA, i, i, True)
            attention(FA1, 0, PAIRS - 1, False)
            for t in range(NT):
                name = ("x2T", t)
                evacuate(FQ, name, 0, QT2[:, :, t * P:(t + 1) * P], quad(FQ.bank(name)))
            load(suT, "suT", ffnw_loaded)
            load(sdT, "sdT", ffnw_loaded)
            load(gwT, "gwT", ffnw_loaded)
            load(ebias, "ebias", ffnw_loaded)
            load(tri, "tri", ffnw_loaded)
            A.drain()
            qv = QT2[:].rearrange("p l (b s) -> p (l b) s", b=B)
            with act.Fori(0, SH // NTR) as i:
                for s in range(NTR):
                    h = i * NTR + s
                    act.wait_ge(conv_used[s], i + 1)
                    A.activation(qx[:, s, :, 0:SD], qv[:, :, ds(h * SD, SD)], ACT.Copy)
                    A.activation(qx[:, s, :, SD:12], qv[:, :, ds(h * SD, 4)], ACT.Copy).then_inc(qx_ready, 1)
            for t in range(0, NT, 2):
                evacuate(FC, ("o", t), 0, oeven[:, t // 2, :], ps[:, FC.bank(("o", t)), :])
            for t in TILES3:
                name = ("x3T", t)
                evacuate(FC, name, 0, x3T[:, :, t * P:(t + 1) * P], quad(FC.bank(name)))
            for k in range(2):
                act.wait_ge(full[2 + k], FC.filled(("logit", k)))
                A.activation(t1[:, 8 * k:8 * k + 8, :], ps[:, 2 + k, :].rearrange("p (t e) -> p t e", e=E),
                             ACT.Exp, scale=-1.0).then_inc(empt[2 + k], 1)
            out_v = out[0:T, :].rearrange("(t p) d -> p t d", p=P)
            act.dma_start(out_v[:, NT // 2:, :], X[:, NT // 2:, :]).then_inc(out_written, 16)
            for k in range(NX):
                act.wait_ge(x3_written[k], 16 * (NT // NX))
            for c in range(2):
                for j in range(SHD // P):
                    bank = FS.bank(("up", c, j))
                    act.wait_ge(full[bank], FS.filled(("up", c, j)))
                    A.activation(hid[:, c % 2, j, :], ps[:, bank, :], ACT.Relu).then_inc(empt[bank], 1)
            for c in range(2):
                act.wait_ge(empt[FS.bank(("dn", c, 3))], FS.drained(("dn", c, 3)))
                act.dma_start(out_v[:, 4 * c:4 * c + 4, :], X[:, 4 * c:4 * c + 4, :]).then_inc(out_written, 16)
            with act.Fori(0, E // UE) as i:
                for s in range(UE):
                    evacuate(FE, ("xgT", s), i, xgT[:, s % 2, :, :], quad(FE.bank(("xgT", s))))
                    if s in (2, 4):
                        k = s // 2 - 1
                        if k == 0:
                            act.wait_ge(empt[7], FE.free(("tile_dn",), i))
                        act.wait_ge(full[6], FE.filled(("tile_up", k), i))
                        A.activation(htile[:, 4 * k:4 * k + 4, :].rearrange("p j t -> p (j t)"), ps[:, 6, :], ACT.Relu).then_inc(empt[6], 1)
                    bank = FE.bank(("h", s))
                    act.wait_ge(full[bank], FE.filled(("h", s), i))
                    act.wait_ge(hsq_ready, i * UE + max(s, 1))
                    A.activation(hrel[:, s % 2, :, :].rearrange("p c t -> p (c t)"), ps[:, bank, 0:2 * P], ACT.Relu)\
                     .then_inc(empt[bank], 1)

        @block.vector
        def _(dve):
            def heads(v):
                return v.rearrange("p (h d) -> p h d", d=HD)

            def scores_out(F, n, b, c):
                for q in range(QB + 1):
                    if q < QB:
                        bank = F.bank(("s", b, c, q))
                        dve.wait_ge(full[bank], F.filled(("s", b, c, q), n))
                        V.scalar_tensor_tensor(prob[:, b, 4 * c:4 * c + 4, q, :],
                                               ps[:, bank, :].rearrange("p (g t) -> p g t", g=4),
                                               1.0 / np.sqrt(HD).astype(np.float32).item(),
                                               bias[:, 4 * c:4 * c + 4, q, :],
                                               op0=ALU.mult, op1=ALU.add).then_inc(empt[bank], 1)
                    if q:
                        dve.wait_ge(empt[F.bank(("s", b, c, q - 1))], F.drained(("s", b, c, q - 1), n))
                        V.tensor_reduce(negmax[:, b, 4 * c:4 * c + 4, q - 1], prob[:, b, 4 * c:4 * c + 4, q - 1, :],
                                        axis=AX.X, op=ALU.max, negate=True).then_inc(max_ready, 1)

            def probs_T(F, n, b, c):
                name = ("pT", b, c, 1)
                bank = F.bank(name)
                dve.wait_ge(full[bank], F.filled(name, n))
                V.tensor_copy(pT[:, 4 * c:4 * c + 4, 1, :], ps[:, bank, :].rearrange("p (g t) -> p g t", g=4))\
                 .then_inc(empt[bank], 1)

            def inverse_sums(b, c, i):
                dve.wait_ge(exp_ready, i * 12 + (2 * b + c + 1) * QB)
                V.reciprocal(rinv[:, b, 4 * c:4 * c + 4, :], rowsum[:, b, 4 * c:4 * c + 4, :]).then_inc(inverse_ready, 1)

            def attended(F, n, b):
                for q in range(QB):
                    name = ("pv", b, 1, q)
                    bank = F.bank(name)
                    dve.wait_ge(full[bank], F.filled(name, n))
                    for g in range(4):
                        rows = slice(32 * g, 32 * g + 32)
                        ins = V.tensor_copy(oT[rows, b, 2:4, 64 * (q + 1):64 * (q + 2)],
                                            ps[rows, bank, g * P:(g + 1) * P].rearrange("p (r t) -> p r t", r=2))
                    ins.then_inc(empt[bank], 1)

            def mean_rows(F, n, b):
                bank = F.bank(("mean", b))
                dve.wait_ge(full[bank], F.filled(("mean", b), n))
                V.tensor_copy(oT[:, b, :, 0:64].rearrange("p (c r) t -> p c r t", c=2),
                              ps[:, bank, 0:P].rearrange("p (c t) -> p c t", c=2).unsqueeze(2)
                              .broadcast_to((P, 2, 2, 64))).then_inc(empt[bank], 1)

            def project(F, n, b, h, i):
                bank = F.bank(("wo", b, h))
                if b == 0 and h == 0:
                    dve.wait_ge(bo_added, i + 1)
                dve.wait_ge(full[bank], F.filled(("wo", b, h), n))
                xt = X[:, ds(i * 4 + (2 * b + h), 1), :].rearrange("p t d -> p (t d)")
                V.tensor_tensor(xt, xt, ps[:, bank, :], ALU.add).then_inc(empt[bank], 1)

            def ln2_stats(F, n, b, h, i):
                bank = F.bank(("wo", b, h))
                dve.wait_ge(empt[bank], F.drained(("wo", b, h), n))
                V.bn_stats(stats[:, ds(i * 4 + (2 * b + h), 1), :].rearrange("p t d -> p (t d)"),
                           X[:, ds(i * 4 + (2 * b + h), 1), :].rearrange("p t d -> p (t d)"))


            def ln1_stats(i):
                dve.wait_ge(x_loaded, i * 16 + 32)
                for u in range(4):
                    V.bn_stats(stats1[:, u, :], X[:, ds(i * 4 + u, 1), :].rearrange("p t d -> p (t d)"))
                V.drain()
                for u in range(4):
                    V.bn_aggr(meanvar1[:, u, :], stats1[:, u, :])
                V.drain()
                V.tensor_scalar(rstd1[:], meanvar1[:, :, 1], EPS, None, ALU.add).then_inc(stats_ready, 1)

            def ln1(i):
                dve.wait_ge(rstd_ready, i + 1)
                for u in range(4):
                    V.tensor_scalar(xln[:, u, :], X[:, ds(i * 4 + u, 1), :].rearrange("p t d -> p (t d)"),
                                    meanvar1[:, u, 0:1], rstd1[:, u:u + 1], ALU.subtract, ALU.mult)\
                     .then_inc(xln_ready, 1)

            def gate_sums():
                V.drain()
                V.tensor_reduce(asum, xln, axis=AX.X, op=ALU.add, apply_absolute_value=True).then_inc(asum_ready, 1)

            def query_gate(i):
                dve.wait_ge(edec_ready, i + 1)
                V.tensor_scalar(edec, edec, 1.0, None, ALU.add)
                V.drain()
                V.reciprocal(cgate[0:64, 0:1], edec[64:P, 0:1])
                V.reciprocal(cgate[64:P, 0:1], edec[64:P, 2:3])
                V.reciprocal(cgate[:, 1:2], edec[:, 1:2])
                V.reciprocal(cgate[:, 2:3], edec[:, 3:4]).then_inc(cgate_ready, 1)

            def upper_v(F, n):
                bank = F.bank(("vhi",))
                dve.wait_ge(full[bank], F.filled(("vhi",), n))
                v = ps[:, bank, :].rearrange("p (b d) -> p b d", b=2)
                V.tensor_copy(vkey[:, :, 0, :], v)
                V.tensor_copy(vkey[64:P, :, 1, :], v[64:P])
                V.tensor_copy(vkey[64:P, :, 2, :], v[0:64]).then_inc(empt[bank], 1)

            def rotate(F, n, m, i):
                sin = rope[:, min(m, 1), 1, :]
                for f in "kq":
                    dve.wait_ge(empt[F.bank((f, m))], F.drained((f, m), n))
                for src, dst, heads_of in ((ks, kr, KVH), (qs, qr, H)):
                    for lo, hi in ((0, 16), (16, 0)):
                        V.tensor_tensor(heads(dst[:, m, :])[:, :, lo:lo + 16], heads(src[:, m, :])[:, :, hi:hi + 16],
                                        sin[:, lo:lo + 16].unsqueeze(1).broadcast_to((P, heads_of, 16)), ALU.mult)
                V.drain()
                dve.wait_ge(tq_ready, i * 3 + m + 1)
                V.tensor_tensor(kr[:, m, :], kr[:, m, :], tk[:, m, :], ALU.add)
                V.tensor_tensor(qr[:, m, :], qr[:, m, :], tq[:, m, :], ALU.add).then_inc(rope_ready, 1)

            def upper_keys(F, n):
                for b in range(2):
                    name = ("kT", 1 + b)
                    bank = F.bank(name)
                    dve.wait_ge(full[bank], F.filled(name, n))
                    for g in range(4):
                        rows = slice(32 * g, 32 * g + 32)
                        ins = V.tensor_copy(kbd[rows, b, :, g, 64:192],
                                            ps[rows, bank, 0:2 * P].rearrange("p (c t) -> p c t", c=2))
                    ins.then_inc(empt[bank], 1)

            def attention(F, n, i, more):
                scores_out(F, n, 0, 0)
                scores_out(F, n, 0, 1)
                inverse_sums(0, 0, i)
                if more:
                    ln1_stats(i + 1)
                inverse_sums(0, 1, i)
                upper_v(F, n)
                if more:
                    ln1(i + 1)
                probs_T(F, n, 0, 0)
                scores_out(F, n, 1, 0)
                if more:
                    gate_sums()
                probs_T(F, n, 0, 1)
                scores_out(F, n, 1, 1)
                inverse_sums(1, 0, i)
                inverse_sums(1, 1, i)
                if more:
                    query_gate(i + 1)
                    for m in range(3):
                        rotate(F, n, m, i + 1)
                attended(F, n, 0)
                probs_T(F, n, 1, 0)
                probs_T(F, n, 1, 1)
                mean_rows(F, n, 0)
                if more:
                    upper_keys(F, n)
                attended(F, n, 1)
                mean_rows(F, n, 1)
                tiles = ((0, 0), (0, 1), (1, 0), (1, 1))
                for k in range(4):
                    project(F, n, *tiles[k], i)
                    if k:
                        ln2_stats(F, n, *tiles[k - 1], i)
                ln2_stats(F, n, 1, 1, i)

            ln1_stats(0)
            ln1(0)
            gate_sums()
            query_gate(0)
            dve.wait_ge(tables_loaded, 16 * 4)
            for m in range(3):
                rotate(FA0, 0, m, 0)
            upper_keys(FA0, 0)
            with dve.Fori(0, PAIRS - 1) as i:
                attention(FA, i, i, True)
            attention(FA1, 0, PAIRS - 1, False)
            V.drain()
            for t in range(NT):
                V.bn_aggr(meanvar[:, t, :], stats[:, t, :])
            V.drain()
            V.tensor_scalar(rstd[:], meanvar[:, :, 1], EPS, None, ALU.add).then_inc(stats2_ready, 1)
            dve.wait_ge(rstd2_ready, 1)
            for t in range(NT):
                if t >= 4:
                    dve.wait_ge(full[FQ.bank(("x2T", t - 4))], FQ.filled(("x2T", t - 4)))
                V.tensor_scalar(xl2[:, t % 4, :], X[:, t, :], meanvar[:, t, 0:1], rstd[:, t:t + 1],
                                ALU.subtract, ALU.mult).then_inc(xl2_ready, 1)
            def head_products(s, i):
                dve.wait_ge(conv_filled[s], i + 2)
                dve.wait_ge(qx_ready, i * NTR + s + 1)
                dve.wait_ge(conv_done, i * NTR + s + 1)
                y = ps[:, 4 * (s % 2):4 * (s % 2) + DC, 0:B * NPAIR].rearrange("p l (b n) -> p l b n", n=NPAIR)
                q = qx[:, s, :, :].rearrange("p (l b) j -> p l b j", l=DC)
                pr = prodb[:, s % 2].rearrange("p (l b) j k -> p l b j k", l=DC)
                for d in range(4):
                    V.tensor_tensor(pr[:, :, :, :, d], y[:, :, :, 8 * d:8 * d + 8], q[:, :, :, d:d + 8], ALU.mult)
                    if d:
                        V.tensor_tensor(pr[:, :, :, d:8, 3 + d], y[:, :, :, 8 * d:8 * d + 8 - d],
                                        q[:, :, :, 0:8 - d], ALU.mult)
                        V.tensor_tensor(pr[:, :, :, 0:d, 3 + d], y[:, :, :, 8 * d + 8 - d:8 * d + 8],
                                        q[:, :, :, 8 - d:8], ALU.mult)
                V.tensor_tensor(pr[:, :, :, 0:4, 7], y[:, :, :, 32:36], q[:, :, :, 4:8], ALU.mult)
                V.tensor_tensor(pr[:, :, :, 4:8, 7], y[:, :, :, 32:36], q[:, :, :, 0:4], ALU.mult)\
                 .then_inc(conv_used[s], 1)

            def head_sums(s, i):
                dve.wait_ge(conv_used[s], i + 2)
                o = O2.rearrange("p l b s -> p (l b) s")[:, :, ds((i * NTR + s) * SD, SD)]
                V.tensor_reduce(o[:, 0:2 * B, :], prodb[:, s % 2, 0:2 * B], axis=AX.X, op=ALU.add)
                dve.wait_ge(half_ready, i * NTR + s + 1)
                V.tensor_reduce(o[:, 2 * B:, :], halfsum[:, s % 2], axis=AX.X, op=ALU.add).then_inc(conv_done, 1)

            head_products(0, 0)
            last = SH // NTR - 1
            with dve.Fori(0, last) as i:
                for s in range(NTR):
                    head_products((s + 1) % NTR, i + (s + 1) // NTR)
                    head_sums(s, i)
            for s in range(NTR):
                if s < NTR - 1:
                    head_products(s + 1, last)
                head_sums(s, last)
            V.drain()
            def ln3_stats(t):
                if t % 2:
                    dve.wait_ge(empt[FC.bank(("o", t))], FC.drained(("o", t)))
                else:
                    dve.wait_ge(even_added, t // 2 + 1)
                V.bn_stats(stats[:, t, :], X[:, t, :])

            def ln3_variances(tiles):
                V.drain()
                for t in tiles:
                    V.bn_aggr(meanvar[:, t, :], stats[:, t, :])
                V.drain()
                g = tiles[0]
                V.tensor_scalar(rstd[:].rearrange("p (k g) -> p g k", g=2)[:, g, :],
                                meanvar[:].rearrange("p (k g) s -> p g k s", g=2)[:, g, :, 1], EPS, None,
                                ALU.add).then_inc(stats3_ready, 1)

            odd, even = TILES3[:NT // 2], TILES3[NT // 2:]
            for t in odd:
                bank = FC.bank(("o", t))
                dve.wait_ge(full[bank], FC.filled(("o", t)))
                V.tensor_tensor(X[:, t, :], X[:, t, :], ps[:, bank, :], ALU.add).then_inc(empt[bank], 1)
                if t > 1:
                    ln3_stats(t - 2)
            ln3_stats(odd[-1])
            ln3_variances(odd)
            for t in even[:3]:
                ln3_stats(t)
            for k, t in enumerate(TILES3):
                if k == NX:
                    for u in even[3:]:
                        ln3_stats(u)
                    ln3_variances(even)
                if k % (NT // 2) == 0:
                    dve.wait_ge(rstd3_ready, k // (NT // 2) + 1)
                if k >= NX:
                    before = ("x3T", TILES3[k - NX])
                    dve.wait_ge(full[FC.bank(before)], FC.filled(before))
                    dve.wait_ge(x3_written[k % NX], 16 * (k // NX))
                V.tensor_scalar(x3[:, k % NX, :], X[:, t, :], meanvar[:, t, 0:1], rstd[:, t:t + 1],
                                ALU.subtract, ALU.mult).then_inc(x3_ready[k % NX], 1)
            dve.wait_ge(ffnw_loaded, 16 * 5)
            for k in range(2):
                dve.wait_ge(empt[2 + k], FC.drained(("logit", k)))
            tile64 = (P, NT, E)
            V.tensor_scalar(t1, t1, 1.0, None, ALU.add)
            V.memset(W, 1.0)
            V.drain()
            V.reciprocal(t1, t1)
            V.memset(W[:, :, 0:1], 0.0)
            V.drain()
            V.tensor_tensor(t2, t1, ebias.unsqueeze(1).broadcast_to(tile64), ALU.add)
            V.drain()
            v = t2.rearrange("p t (g e) -> p (t g) e", e=8)
            flat3 = t3.rearrange("p t e -> p (t e)")
            flat4 = t4.rearrange("p t e -> p (t e)")
            flat5 = t5.rearrange("p t e -> p (t e)")
            NP8 = NT * NG
            hi4 = flat3[:, 0:4 * NP8].rearrange("p (n e) -> p n e", e=4)
            lo4 = flat3[:, 4 * NP8:8 * NP8].rearrange("p (n e) -> p n e", e=4)
            V.tensor_tensor(hi4, v[:, :, 0:4], v[:, :, 4:8], ALU.max)
            V.tensor_tensor(lo4, v[:, :, 0:4], v[:, :, 4:8], ALU.min)
            V.drain()
            hi2, mn2, mx2, lo2 = (flat4[:, 2 * k * NP8:2 * (k + 1) * NP8].rearrange("p (n e) -> p n e", e=2)
                                  for k in range(4))
            V.tensor_tensor(hi2, hi4[:, :, 0:2], hi4[:, :, 2:4], ALU.max)
            V.tensor_tensor(mn2, hi4[:, :, 0:2], hi4[:, :, 2:4], ALU.min)
            V.tensor_tensor(mx2, lo4[:, :, 0:2], lo4[:, :, 2:4], ALU.max)
            V.drain()
            V.tensor_tensor(lo2, mn2, mx2, ALU.max)
            V.drain()
            hi1, mn1, mx1, lo1 = (flat5[:, k * NP8:(k + 1) * NP8].rearrange("p (n e) -> p n e", e=1) for k in range(4))
            V.tensor_tensor(hi1, hi2[:, :, 0:1], hi2[:, :, 1:2], ALU.max)
            V.tensor_tensor(mn1, hi2[:, :, 0:1], hi2[:, :, 1:2], ALU.min)
            V.tensor_tensor(mx1, lo2[:, :, 0:1], lo2[:, :, 1:2], ALU.max)
            V.drain()
            V.tensor_tensor(lo1, mn1, mx1, ALU.max)
            V.drain()
            V.tensor_tensor(g1.rearrange("p t g -> p (t g)").unsqueeze(2), hi1, lo1, ALU.add)
            V.drain()
            gg = (P, NT, NG, NG)
            other = g1.unsqueeze(2).broadcast_to(gg)
            own = g1.unsqueeze(3).broadcast_to(gg)
            gt3 = t3.rearrange("p t (g h) -> p t g h", h=NG)
            eq4 = t4.rearrange("p t (g h) -> p t g h", h=NG)
            V.tensor_tensor(gt3, other, own, ALU.is_gt)
            V.tensor_tensor(eq4, other, own, ALU.is_equal)
            V.drain()
            V.tensor_tensor(t4, t4, tri.unsqueeze(1).broadcast_to(tile64), ALU.mult)
            V.drain()
            V.tensor_tensor(t3, t3, t4, ALU.add)
            V.drain()
            V.tensor_reduce(g2, gt3, axis=AX.X, op=ALU.add)
            V.drain()
            V.tensor_scalar(g2, g2, TKG - 0.5, None, ALU.is_lt)
            V.drain()
            V.tensor_scalar(g1, g2, 1e30, -1e30, ALU.mult, ALU.add)
            V.tensor_tensor(t3.rearrange("p t (g e) -> p (t g) e", e=8), v,
                            g2.rearrange("p t g -> p (t g)").unsqueeze(2).broadcast_to((P, NP8, 8)), ALU.mult)
            V.drain()
            V.tensor_tensor(t3.rearrange("p t (g e) -> p (t g) e", e=8), t3.rearrange("p t (g e) -> p (t g) e", e=8),
                            g1.rearrange("p t g -> p (t g)").unsqueeze(2).broadcast_to((P, NP8, 8)), ALU.add)
            V.drain()
            for t in range(NT):
                V.max(m8[:, t, :], t3[:, t, :])
            V.drain()
            kth = m8[:, :, K - 1:K].broadcast_to(tile64)
            V.tensor_tensor(t4, t3, kth, ALU.is_gt)
            V.tensor_tensor(t5, t3, kth, ALU.is_equal)
            V.drain()
            V.tensor_reduce(cnt, t4, axis=AX.X, op=ALU.add)
            V.tensor_tensor_scan(t2.rearrange("p t e -> p (t e)"), W.rearrange("p t e -> p (t e)"), flat5, 0.0,
                                 ALU.mult, ALU.add)
            V.drain()
            V.tensor_scalar(cnt, cnt, -1.0, K + 0.5, ALU.mult, ALU.add)
            V.drain()
            V.tensor_tensor(t2, t2, cnt.unsqueeze(2).broadcast_to(tile64), ALU.is_lt)
            V.drain()
            V.tensor_tensor(t2, t2, t5, ALU.mult)
            V.drain()
            V.tensor_tensor(t2, t2, t4, ALU.add)
            V.drain()
            V.tensor_copy(sel.rearrange("p k h e -> p h k e"), t2.rearrange("p (h k) e -> p h k e", h=2))\
             .then_inc(sel_ready, 1)
            V.drain()
            V.tensor_tensor(W, t2, t1, ALU.mult)
            V.drain()
            V.tensor_reduce(cnt, W, axis=AX.X, op=ALU.add)
            V.drain()
            V.tensor_scalar(cnt, cnt, 1e-20, None, ALU.add)
            V.drain()
            V.reciprocal(cnt, cnt)
            V.drain()
            V.tensor_tensor(W, W, cnt.unsqueeze(2).broadcast_to(tile64), ALU.mult)
            V.drain()
            V.tensor_scalar(W, W, 2.5, None, ALU.mult).then_inc(gates_ready, 1)
            V.drain()
            dve.wait_ge(rev_ready, 1)
            V.tensor_scalar(rev[0:E, :], rev[0:E, :], float(T // 2), None, ALU.add)
            V.drain()
            for q in range(2):
                bank = FC.bank(("selT", q))
                dve.wait_ge(full[bank], FC.filled(("selT", q)))
                V.tensor_tensor(key[:, q * 512:(q + 1) * 512], ps[:, bank, :], rev[:, q * 512:(q + 1) * 512],
                                ALU.mult).then_inc(empt[bank], 1)
            V.drain()

            def best_keys(dst, src, rounds=range(CAP // 8)):
                for r in rounds:
                    V.max(dst[:, 8 * r:8 * r + 8], src)
                    V.drain()
                    if r < CAP // 8 - 1:
                        V.match_replace(src, dst[:, 8 * r:8 * r + 8], src, 0.0)
                        V.drain()

            def shared_out(c, j):
                bank = FS.bank(("dn", c, j))
                dve.wait_ge(full[bank], FS.filled(("dn", c, j)))
                V.tensor_tensor(X[:, 4 * c + j, :], X[:, 4 * c + j, :], ps[:, bank, :], ALU.add)\
                 .then_inc(empt[bank], 1)

            best_keys(best[:, 0:CAP], key, range(10))
            shared_out(0, 0)
            best_keys(best[:, 0:CAP], key, range(10, 14))
            shared_out(0, 1)
            shared_out(0, 2)
            best_keys(best[:, 0:CAP], key, range(14, CAP // 8))
            V.tensor_copy(best[0:E, CAP:2 * CAP], best[E:2 * E, 0:CAP])
            V.drain()
            shared_out(0, 3)
            best_keys(kvals, best[0:E, :])
            V.tensor_scalar(empty, kvals, 0.0, None, ALU.is_equal)
            V.tensor_scalar(idxf, kvals, -1.0, float(T), ALU.mult, ALU.add)
            V.drain()
            V.tensor_tensor(empty, empty, slotno, ALU.mult)
            V.drain()
            V.tensor_tensor(idxf, idxf, empty, ALU.add).then_inc(idxf_ready, 1)
            shared_out(1, 0)
            bank = FC.bank(("idxT",))
            dve.wait_ge(full[bank], FC.filled(("idxT",)))
            V.tensor_copy(idxU[:, 0:E], ps[:, bank, 0:E]).then_inc(empt[bank], 1)
            V.memset(idxU[:, E:E + UE], 0)
            V.drain()
            V.tensor_copy(idxg[:], idxU[:, 0:UE]).then_inc(idx_ready, 1)
            for j in range(1, 4):
                shared_out(1, j)
            def hidden_squared(s, i):
                bank = FE.bank(("h", s))
                dve.wait_ge(empt[bank], FE.drained(("h", s), i))
                V.tensor_tensor(hsq[:, s % 2, :, :], hrel[:, s % 2, :, :], hrel[:, s % 2, :, :], ALU.mult)\
                 .then_inc(hsq_ready, 1)

            def experts(i, more):
                for s in range(UE):
                    if s < UE - 1:
                        hidden_squared(s + 1, i)
                    elif more:
                        hidden_squared(0, i + 1)
                    dve.wait_ge(y_filled[s], i + 2)
                    dve.wait_ge(scatter_landed, i * (UE + 1) + (s + 2 if s >= 2 else s + 1))
                    dve.wait_ge(xg_loaded[s], i * 16 + 16)
                    V.tensor_copy(idxs[:, s % 2:s % 2 + 1], idxU[:, ds(i * UE + s, 1)])
                    V.tensor_copy(idxg[:, s:s + 1], idxU[:, ds(i * UE + (s + UE), 1)])
                    V.tensor_scalar(ysb[:, s % 2, :], ps[:, 4 + s % 2, :], xg[:, s, ds(i * UE + (D + s), 1)], None, ALU.mult)\
                     .then_inc(y_ready[s % 2], 1)
                    if s in (1, 3):
                        k = s // 2
                        dve.wait_ge(empt[6], FE.drained(("tile_up", k), i))
                        units = htile[:, 4 * k:4 * k + 4, :]
                        V.tensor_tensor(units, units, units, ALU.mult).then_inc(htile_ready, 1)
                dve.wait_ge(full[7], FE.filled(("tile_dn",), i))
                dve.wait_ge(scatter_landed, i * (UE + 1) + 3)
                V.tensor_copy(idxt[:], tile_rows[:, ds(i, 1)])
                V.tensor_copy(ytile, ps[:, 7, :]).then_inc(empt[7], 1)
                V.drain().then_inc(tile_ready, 1)

            hidden_squared(0, 0)
            with dve.Fori(0, E // UE - 1) as i:
                experts(i, True)
            experts(E // UE - 1, False)
        @block.tensor
        def _(pe):
            def fill(fills, name, i=0):
                bank = fills.bank(name)
                pe.wait_ge(empt[bank], fills.free(name, i))
                return bank

            def wait_drained(F, n, names, then):
                latest = {}
                for name in names:
                    bank, turn = F.at[name]
                    if bank not in latest or turn > F.at[latest[bank]][1]:
                        latest[bank] = name
                for bank, name in latest.items():
                    if bank != F.bank(then):
                        pe.wait_ge(empt[bank], F.drained(name, n))

            def product(out_ap, pairs):
                for n, (lhsT, rhs) in enumerate(pairs):
                    ins = TE.matmul(out_ap, lhsT, rhs, start=(n == 0), stop=(n == len(pairs) - 1))
                return ins

            def probs_T(F, n, b, c, i):
                for q in range(QB):
                    pe.wait_ge(prob_ready, i * 12 + ((2 * b + c) * QB + q + 1))
                    bank = fill(F, ("pT", b, c, q), n)
                    for g in range(4):
                        ins = TE.transpose(ps[:, bank, g * P:(g + 1) * P], prob[:, b, 4 * c + g, q, :], ident[:])
                    ins.then_inc(full[bank], 1)

            def scores(F, n, b, c):
                for q in range(QB):
                    bank = fill(F, ("s", b, c, q), n)
                    m, half = (0, b) if q == 0 else (1 + b, q - 1)
                    keys = (kbd[:, b, c, :, 64:192],
                            kbd[:, b, c, :, :].rearrange("p g (n t) -> p g n t", t=64)[:, :, 0:3:2, :],
                            kbd[:, b, c, :, 0:P])[q]
                    TE.matmul(ps[:, bank, :], qT[:, m, half, 2 * c:2 * c + 2, :], keys, start=True, stop=True)\
                        .then_inc(full[bank], 1)

            def attend(F, n, b):
                for c in range(2):
                    wait_drained(F, n, [("pT", b, c, q) for q in range(QB)], ("pv", b, c, 0))
                    for q in range(QB):
                        bank = fill(F, ("pv", b, c, q), n)
                        TE.matmul(ps[:, bank, :], vkey[:, b, q, c * P:(c + 1) * P], pT[:, 4 * c:4 * c + 4, q, :],
                                  start=True, stop=True).then_inc(full[bank], 1)

            def mean_rows(F, n, b):
                bank = fill(F, ("mean", b), n)
                for c in range(2):
                    ins = product(ps[:, bank, c * 64:(c + 1) * 64],
                                  [(vlo[:, b, c * P:(c + 1) * P], inv_s), (vkey[:, b, 0, c * P:(c + 1) * P], inv_s)])
                ins.then_inc(full[bank], 1)

            def project(F, n, b, h):
                if h == 0:
                    wait_drained(F, n, [("mean", b)] + [("pv", b, c, q) for c in range(2) for q in range(QB)], ("wo", b, 0))
                bank = fill(F, ("wo", b, h), n)
                product(ps[:, bank, :], [(oT[:, b, k, h * P:(h + 1) * P], wo[:, k, :]) for k in range(4)])\
                    .then_inc(full[bank], 1)

            pe.wait_ge(consts_ready, 1)

            tokens = (lambda c: xlnT[:, c, 0:2, :].rearrange("p u t -> p (u t)")[:, 64:64 + P],
                      lambda c: xlnT[:, c, 2, :], lambda c: xlnT[:, c, 3, :])

            def tokens_in(F, n, i):
                for u in range(4):
                    pe.wait_ge(xln_ready, i * 4 + u + 1)
                    bank = fill(F, ("xT", u), n)
                    for c in range(DC):
                        ins = TE.transpose(ps[:, bank, c * P:(c + 1) * P], xln[:, u, c * P:(c + 1) * P], ident[:])
                    ins.then_inc(full[bank], 1)

            def qk(F, n):
                wait_drained(F, n, [("xT", u) for u in range(4)], ("q", 0))
                for m in range(3):
                    for f, w, width in (("q", wq, D), ("k", wkv, D // 2)):
                        bank = fill(F, (f, m), n)
                        product(ps[:, bank, 0:width], [(tokens[m](c), w[:, c, 0:width]) for c in range(DC)])\
                            .then_inc(full[bank], 1)

            def values(F, n):
                for name, rows in (("vhi", tokens[1:]), ("vlo", [lambda c, b=b: xlnT[:, c, b, :] for b in range(2)])):
                    bank = fill(F, (name,), n)
                    for b in range(2):
                        ins = product(ps[:, bank, b * 256:(b + 1) * 256],
                                      [(rows[b](c), wkv[:, c, D // 2:D]) for c in range(DC)])
                    ins.then_inc(full[bank], 1)

            def qk_T(F, n, i):
                for m in range(3):
                    pe.wait_ge(rope_ready, i * 3 + m + 1)
                    bank = fill(F, ("kT", m), n)
                    for c in range(2):
                        ins = TE.transpose(ps[:, bank, c * P:(c + 1) * P], kr[:, m, c * P:(c + 1) * P], ident[:])
                    ins.then_inc(full[bank], 1)
                    bank = fill(F, ("qT", m), n)
                    for k in range(4):
                        ins = TE.transpose(ps[:, bank, k * P:(k + 1) * P], qr[:, m, k * P:(k + 1) * P], ident[:])
                    ins.then_inc(full[bank], 1)

            def qk_T_out(F, n):
                for m in range(3):
                    for f in ("kT", "qT"):
                        pe.wait_ge(empt[F.bank((f, m))], F.drained((f, m), n))

            def attention(F, n, i, more):
                scores(F, n, 0, 0)
                scores(F, n, 0, 1)
                values(F, n)
                probs_T(F, n, 0, 0, i)
                scores(F, n, 1, 0)
                if more:
                    tokens_in(F, n, i + 1)
                probs_T(F, n, 0, 1, i)
                scores(F, n, 1, 1)
                if more:
                    qk(F, n)
                attend(F, n, 0)
                probs_T(F, n, 1, 0, i)
                probs_T(F, n, 1, 1, i)
                mean_rows(F, n, 0)
                if more:
                    qk_T(F, n, i + 1)
                attend(F, n, 1)
                mean_rows(F, n, 1)
                project(F, n, 0, 0)
                project(F, n, 0, 1)
                project(F, n, 1, 0)
                project(F, n, 1, 1)
                if more:
                    qk_T_out(F, n)

            tokens_in(FA0, 0, 0)
            pe.wait_ge(w_loaded, 16 * 2)
            qk(FA0, 0)
            qk_T(FA0, 0, 0)
            qk_T_out(FA0, 0)
            pe.wait_ge(tables_loaded, 16 * 4)
            with pe.Fori(0, PAIRS - 1) as i:
                attention(FA, i, i, True)
            attention(FA1, 0, PAIRS - 1, False)
            def convolve(s, i):
                pe.wait_ge(head_loaded[s], i * 32 + 32)
                pe.wait_ge(kv_ready, i * NTR + s + 1)
                pe.wait_ge(conv_used[(s + 2) % NTR], i + (s // 2 + 1))
                for lt in range(DC):
                    ins = product(ps[:, 4 * (s % 2) + lt, 0:B * NPAIR],
                                  [(tring[:, s, (lt - mt) * P:(lt - mt + 1) * P],
                                    kvb[:, s, mt * B:(mt + 1) * B, :].rearrange("p b n -> p (b n)"))
                                   for mt in range(lt + 1)])
                ins.then_inc(conv_filled[s], 1)

            for k in range(4):
                pe.wait_ge(empt[k], FQ.all_drained(k))
            convolve(0, 0)
            for t in range(NT):
                pe.wait_ge(xl2_ready, t + 1)
                bank = fill(FQ, ("x2T", t))
                for c in range(DC):
                    ins = TE.transpose(ps[:, bank, c * P:(c + 1) * P], xl2[:, t % 4, c * P:(c + 1) * P], ident[:])
                ins.then_inc(full[bank], 1)
            for k in range(4, NBANK):
                pe.wait_ge(empt[k], FQ.all_drained(k))
            with pe.Fori(0, SH // NTR - 1) as i:
                for s in range(NTR):
                    convolve((s + 1) % NTR, i + (s + 1) // NTR)
            for s in range(1, NTR):
                convolve(s, SH // NTR - 1)
            pe.wait_ge(conv_done, SH // 2 + 2)
            pe.wait_ge(conv_used[NTR - 2], SH // NTR + 1)
            for k, t in enumerate(sorted(range(NT), key=lambda t: t % 2)):
                if k == NT // 2:
                    pe.wait_ge(conv_done, SH + 2)
                bank = fill(FC, ("o", t))
                at = (t % 2) * P
                for c in range(DC):
                    ins = TE.transpose(ps[:, bank, c * P:(c + 1) * P], O2[:, c, t // 2, at:at + P], ident[:])
                ins.then_inc(full[bank], 1)

            def logits(t):
                name = ("x3T", t)
                pe.wait_ge(empt[FC.bank(name)], FC.drained(name))
                bank = fill(FC, ("logit", t // 8))
                ins = product(ps[:, bank, (t % 8) * E:(t % 8 + 1) * E],
                              [(x3T[:, c, t * P:(t + 1) * P], gwT[:, c, :]) for c in range(DC)])
                if t in (NT // 2 - 2, NT - 2):
                    ins.then_inc(full[bank], 1)

            pe.wait_ge(ffnw_loaded, 16 * 5)
            for k, t in enumerate(TILES3):
                pe.wait_ge(x3_ready[k % NX], k // NX + 1)
                bank = fill(FC, ("x3T", t))
                for c in range(DC):
                    ins = TE.transpose(ps[:, bank, c * P:(c + 1) * P], x3[:, k % NX, c * P:(c + 1) * P], ident[:])
                ins.then_inc(full[bank], 1)
                if k:
                    logits(TILES3[k - 1])
            logits(TILES3[-1])

            def shared_up(c, js):
                for j in js:
                    bank = fill(FS, ("up", c, j))
                    product(ps[:, bank, :], [(suT[:, k, j * P:(j + 1) * P], x3T[:, k, c * 512:(c + 1) * 512])
                                             for k in range(DC)]).then_inc(full[bank], 1)

            def shared_down(c, js):
                pe.wait_ge(hid_ready, (c + 1) * (SHD // P))
                for j in js:
                    bank = fill(FS, ("dn", c, j))
                    product(ps[:, bank, :], [(hid[:, c % 2, k, j * P:(j + 1) * P], sdT[:, k, :])
                                             for k in range(SHD // P)]).then_inc(full[bank], 1)

            shared_up(0, range(SHD // P))
            shared_up(1, range(3))
            pe.wait_ge(sel_ready, 1)
            for q in range(2):
                bank = fill(FC, ("selT", q))
                for k in range(4):
                    ins = TE.transpose(ps[:, bank, k * P:(k + 1) * P],
                                       sel[:, 4 * q + k, :, :].rearrange("p h e -> p (h e)"), ident[:])
                ins.then_inc(full[bank], 1)
            shared_up(1, range(3, SHD // P))
            shared_down(0, range(4))
            shared_down(1, range(3))
            pe.wait_ge(idxf_ready, 1)
            bank = fill(FC, ("idxT",))
            TE.transpose(ps[:, bank, 0:E], idxf, ident[0:E, 0:E]).then_inc(full[bank], 1)
            shared_down(1, range(3, 4))

            def tokens_T(s, i):
                pe.wait_ge(xg_loaded[s], i * 16 + 16)
                bank = fill(FE, ("xgT", s), i)
                for c in range(DC):
                    ins = TE.transpose(ps[:, bank, c * P:(c + 1) * P], xg[:, s, c * P:(c + 1) * P], ident[:])
                ins.then_inc(full[bank], 1)

            def hidden(s, i):
                pe.wait_ge(empt[FE.bank(("xgT", s))], FE.drained(("xgT", s), i))
                pe.wait_ge(wexp_loaded[s % NW], i * (16 * UE // NW) + (16 * (s // NW) + 16))
                bank = fill(FE, ("h", s), i)
                for j in range(2):
                    ins = product(ps[:, bank, j * P:(j + 1) * P],
                                  [(wring[:, s % NW, c * I + j * P:c * I + (j + 1) * P], xgT[:, s % 2, c, :])
                                   for c in range(DC)])
                ins.then_inc(full[bank], 1)

            def outputs(s, i):
                pe.wait_ge(hsq_ready, i * UE + (s + 2))
                pe.wait_ge(y_ready[s % 2], i * (UE // 2) + (s // 2 + 1))
                product(ps[:, 4 + s % 2, :], [(hsq[:, s % 2, j, :], wring[:, s % NW, DC * I + j * D:DC * I + (j + 1) * D])
                                              for j in range(2)]).then_inc(y_filled[s], 1)

            def tile_part(s, i):
                if s in (0, 2):
                    k = s // 2
                    bank = fill(FE, ("tile_up", k), i)
                    for j in range(4):
                        ins = product(ps[:, bank, j * P:(j + 1) * P],
                                      [(suT[:, c, (4 * k + j) * P:(4 * k + j + 1) * P],
                                        x3T[:, c, ds(i * P + T // 2, P)]) for c in range(DC)])
                    ins.then_inc(full[bank], 1)
                if s in (5, 6):
                    if s == 5:
                        pe.wait_ge(htile_ready, i * 2 + 2)
                        fill(FE, ("tile_dn",), i)
                    for k in range(4 * (s - 5), 4 * (s - 5) + 4):
                        ins = TE.matmul(ps[:, 7, :], htile[:, k, :], sdT[:, k, :], start=(k == 0), stop=(k == 7))
                    if s == 6:
                        ins.then_inc(full[7], 1)

            for k in (4, 5):
                pe.wait_ge(empt[k], FS.all_drained(k))
            tokens_T(0, 0)
            tokens_T(1, 0)
            hidden(0, 0)
            last = E // UE - 1
            with pe.Fori(0, last) as i:
                for s in range(UE):
                    tokens_T((s + 2) % UE, i + (s + 2) // UE)
                    hidden((s + 1) % UE, i + (s + 1) // UE)
                    outputs(s, i)
                    tile_part(s, i)
            for s in range(UE):
                if s < UE - 2:
                    tokens_T(s + 2, last)
                if s < UE - 1:
                    hidden(s + 1, last)
                outputs(s, last)
                tile_part(s, last)



def constants():
    f = np.float32
    half = HD // 2
    freqs = f(1.0) / f(10000.0) ** (np.arange(half, dtype=f) / f(half))
    angle = np.outer(np.arange(S, dtype=f), freqs).astype(f)
    sin, cos = np.sin(angle), np.cos(angle)
    cos2 = np.concatenate([cos, cos], 1)
    sin2 = np.concatenate([-sin, sin], 1)
    pos = np.stack([64 + np.arange(P) % 64, 128 + np.arange(P)])
    rope = np.stack([cos2[pos], sin2[pos]], 1).transpose(2, 0, 1, 3).astype(f)
    slopes = np.power(f(2.0) ** f(-0.5), np.arange(1, H + 1, dtype=f)).astype(f)
    bias = np.zeros((P, KVH, QB, P), f)
    keys = [np.arange(128, 256), np.concatenate([np.arange(64, 128), np.arange(192, 256)]), np.arange(64, 192)]
    row = np.arange(P)
    for q in range(QB):
        dist = np.abs((64 * (q + 1) + row % 64)[:, None] - keys[q][None, :])
        for k in range(KVH):
            slope = slopes[2 * k + row // 64][:, None]
            bias[:, k, q] = np.where(dist > WIN // 2, -(slope * dist.astype(f)), f(NEG))
    tri = np.tile((np.arange(8)[None, :] < np.arange(8)[:, None]).astype(f).reshape(1, 64), (P, 1))
    return rope, bias, tri


def kernel(x, ctx_2048, L0_attn_Wq, L0_attn_Wkv, L0_attn_Wo, L0_attn_bo, L0_xattn_ssm_kernel, L0_xattn_D,
           L0_ffn_gate_w, L0_ffn_e_bias, L0_ffn_w1, L0_ffn_w2, L0_ffn_shared_up_w, L0_ffn_shared_down_w):
    import concourse.bacc as bacc
    from concourse.bass_utils import run_bass_kernel_spmd

    C = np.ascontiguousarray
    rope, bias, tri = constants()
    chunked = lambda w: C(np.asarray(w).reshape(w.shape[0] // P, P, w.shape[1]).transpose(1, 0, 2))
    wq = np.asarray(L0_attn_Wq).reshape(D, 2, 4, 2, HD).transpose(0, 1, 3, 2, 4).reshape(D, D)
    wo = np.asarray(L0_attn_Wo).reshape(2, 4, 2, HD, D).transpose(0, 2, 1, 3, 4).reshape(D, D)
    ctx = np.asarray(ctx_2048).reshape(B, SH, SD, DC, P)[..., ::-1]
    ctx = np.concatenate([ctx, ctx[:, :, :4]], 2).transpose(1, 4, 3, 0, 2)
    w1 = np.asarray(L0_ffn_w1).transpose(0, 2, 1).reshape(E, DC, P, I).transpose(0, 2, 1, 3).reshape(E, P, DC * I)
    w2 = np.asarray(L0_ffn_w2).transpose(0, 2, 1).reshape(E, 2, P, D).transpose(0, 2, 1, 3).reshape(E, P, 2 * D)
    arrays = {
        "x": C(np.asarray(x).reshape(T, D)),
        "wq": chunked(wq), "wkv": chunked(np.asarray(L0_attn_Wkv)), "wo": chunked(wo),
        "bo": C(np.broadcast_to(np.asarray(L0_attn_bo), (P, D))),
        "rope": C(rope), "bias": C(bias), "tri": C(tri),
        "kern": C(np.asarray(L0_xattn_ssm_kernel)), "skip": C(np.asarray(L0_xattn_D).reshape(SH, 1)),
        "ctxE": C(ctx.reshape(SH * P, DC * B * 12)),
        "suT": chunked(np.asarray(L0_ffn_shared_up_w).T), "sdT": chunked(np.asarray(L0_ffn_shared_down_w).T),
        "gwT": chunked(np.asarray(L0_ffn_gate_w).T),
        "ebias": C(np.broadcast_to(np.asarray(L0_ffn_e_bias), (P, E))),
        "wexp": C(np.concatenate([w1, w2], 2).reshape(E * P, 2048)),
    }
    nc = bacc.Bacc("TRN2", target_bir_lowering=False, num_devices=1)
    aps = {n: nc.dram_tensor(n, v.shape, mybir.dt.from_np(v.dtype), kind="ExternalInput").ap()
           for n, v in arrays.items()}
    out = nc.dram_tensor("out", (ROWS, D), mybir.dt.float32, kind="ExternalOutput").ap()
    program(nc, aps, out)
    r = run_bass_kernel_spmd(nc, [arrays], core_ids=[0])
    return r.results[0]["out"][:T].reshape(B, S, D)
```
